# Optimizing a Trainium2 kernel written in Bass

```python
import numpy as np
import jax
import jax.numpy as jnp

def _softmax(x, axis=-1):
    return jax.nn.softmax(x, axis=axis)

def _gelu(x):
    return jax.nn.gelu(x, approximate=True)

def _silu(x):
    return jax.nn.silu(x)

def _sigmoid(x):
    return jax.nn.sigmoid(x)

def _layernorm(x, axis=-1, eps=1e-05):
    m = jnp.mean(x, axis=axis, keepdims=True)
    v = jnp.var(x, axis=axis, keepdims=True)
    return (x - m) / jnp.sqrt(v + eps)

def _scatter_add(tgt, idx, src, axis=0):
    return tgt.at[idx].add(src)

def _segment_sum(src, seg, n):
    return jax.ops.segment_sum(src, seg, n)
kernel_name = 'mk_gnn_resnorm_d2_gnn_r8_15b642'

def setup_inputs(seed: int=0):
    np.random.seed(seed)
    _w = jnp.asarray

    def _rec_inputs():
        import jax
        import jax.numpy as jnp
        _gk = jax.random.key(seed)
        x = -0.0003713 + 1 * jax.random.normal(jax.random.fold_in(_gk, 1), (12500, 256), jnp.float32)
        src = jax.random.randint(jax.random.fold_in(_gk, 2), (200000,), 0, 12500, jnp.int32)
        dst = jax.random.randint(jax.random.fold_in(_gk, 3), (200000,), 0, 12500, jnp.int32)
        _o = jnp.argsort(dst, stable=True)
        src = src[_o]
        dst = dst[_o]
        edge_type_64 = jax.random.randint(jax.random.fold_in(_gk, 12), (200000,), 0, 64, jnp.int32)
        return (x, src, dst, edge_type_64)
    x, src, dst, edge_type_64 = _rec_inputs()

    def _L0_gnn_setup():
        import jax, jax.numpy as jnp
        import numpy as np
        N_NODES = 6250
        N_EDGES = 62500
        IN_DIM = 256
        HID = 64
        HEADS = 4
        N_REL = 64
        key = jax.random.key(seed)
        ks = jax.random.split(key, 16)
        s = 0.02
        return {'node_features': jax.random.normal(ks[0], (N_NODES, IN_DIM), jnp.float32), 'edge_index': jax.random.randint(ks[1], (2, N_EDGES), 0, N_NODES, jnp.int32), 'edge_relations': jax.random.randint(ks[2], (N_EDGES,), 0, N_REL, jnp.int32), 'query_emb': jax.random.normal(ks[3], (IN_DIM,), jnp.float32), 'Wq': jax.random.normal(ks[4], (IN_DIM, HID * HEADS), jnp.float32) * s, 'bq': jnp.zeros((HID * HEADS,), jnp.float32), 'Wk': jax.random.normal(ks[5], (IN_DIM, HID * HEADS), jnp.float32) * s, 'bk': jnp.zeros((HID * HEADS,), jnp.float32), 'Wv': jax.random.normal(ks[6], (IN_DIM, HID * HEADS), jnp.float32) * s, 'bv': jnp.zeros((HID * HEADS,), jnp.float32), 'rel_w': jax.random.normal(ks[7], (N_REL, HID), jnp.float32) * s, 'Wo': jax.random.normal(ks[8], (HID * HEADS, IN_DIM), jnp.float32) * s, 'bo': jnp.zeros((IN_DIM,), jnp.float32), 'gamma': jnp.ones((IN_DIM,), jnp.float32), 'beta': jnp.zeros((IN_DIM,), jnp.float32)}
    _L0_gnn_all = _L0_gnn_setup()
    _L0_gnn_in = {k: v for k, v in _L0_gnn_all.items() if k in ('query_emb', 'Wq', 'bq', 'Wk', 'bk', 'Wv', 'bv', 'rel_w', 'Wo', 'bo', 'gamma', 'beta')}
    del _L0_gnn_all

    def _L1_gnn_setup():
        import jax, jax.numpy as jnp
        import numpy as np
        N = 12500
        E = 200000
        IN = 256
        H = 4
        C = 64
        key = jax.random.key(seed)
        k1, k2, k3, k4, k5, k6 = jax.random.split(key, 6)
        x = jax.random.normal(k1, (N, IN), dtype=jnp.float32)
        edge_index = jax.random.randint(k2, (2, E), 0, N, dtype=jnp.int64)
        W = jax.random.normal(k3, (IN, H * C), dtype=jnp.float32) * (1.0 / np.sqrt(IN))
        att_src = jax.random.normal(k4, (H, C), dtype=jnp.float32) * 0.1
        att_dst = jax.random.normal(k5, (H, C), dtype=jnp.float32) * 0.1
        bias = jax.random.normal(k6, (H * C,), dtype=jnp.float32) * 0.01
        return {'x': x, 'edge_index': edge_index, 'W': W, 'att_src': att_src, 'att_dst': att_dst, 'bias': bias}
    _L1_gnn_all = _L1_gnn_setup()
    _L1_gnn_in = {k: v for k, v in _L1_gnn_all.items() if k in ('W', 'att_src', 'att_dst', 'bias')}
    del _L1_gnn_all
    return {'x': x, 'src': src, 'dst': dst, 'edge_type_64': edge_type_64, 'L0_gnn_query_emb': _L0_gnn_in['query_emb'], 'L0_gnn_Wq': _L0_gnn_in['Wq'], 'L0_gnn_bq': _L0_gnn_in['bq'], 'L0_gnn_Wk': _L0_gnn_in['Wk'], 'L0_gnn_bk': _L0_gnn_in['bk'], 'L0_gnn_Wv': _L0_gnn_in['Wv'], 'L0_gnn_bv': _L0_gnn_in['bv'], 'L0_gnn_rel_w': _L0_gnn_in['rel_w'], 'L0_gnn_Wo': _L0_gnn_in['Wo'], 'L0_gnn_bo': _L0_gnn_in['bo'], 'L0_gnn_gamma': _L0_gnn_in['gamma'], 'L0_gnn_beta': _L0_gnn_in['beta'], 'L1_gnn_W': _L1_gnn_in['W'], 'L1_gnn_att_src': _L1_gnn_in['att_src'], 'L1_gnn_att_dst': _L1_gnn_in['att_dst'], 'L1_gnn_bias': _L1_gnn_in['bias']}

def reference(x, src, dst, edge_type_64, L0_gnn_query_emb, L0_gnn_Wq, L0_gnn_bq, L0_gnn_Wk, L0_gnn_bk, L0_gnn_Wv, L0_gnn_bv, L0_gnn_rel_w, L0_gnn_Wo, L0_gnn_bo, L0_gnn_gamma, L0_gnn_beta, L1_gnn_W, L1_gnn_att_src, L1_gnn_att_dst, L1_gnn_bias):
    import jax
    import jax.numpy as jnp

    def _L0_gnn_ref(node_features, edge_index, edge_relations, query_emb, Wq, bq, Wk, bk, Wv, bv, rel_w, Wo, bo, gamma, beta):
        import jax, jax.numpy as jnp
        import numpy as np
        N_NODES = 6250
        N_EDGES = 62500
        IN_DIM = 256
        HID = 64
        HEADS = 4
        N_REL = 64
        N = node_features.shape[0]
        D = rel_w.shape[1]
        H = Wq.shape[1] // D
        enh = node_features + 0.1 * query_emb[None, :]
        Q = (enh @ Wq + bq).reshape(N, H, D)
        K = (enh @ Wk + bk).reshape(N, H, D)
        V = (enh @ Wv + bv).reshape(N, H, D)
        src, dst = (edge_index[0], edge_index[1])
        rel = rel_w[edge_relations]
        mod_k = K[src] + 0.2 * rel[:, None, :]
        scores = jnp.einsum('ehd,ehd->eh', Q[dst], mod_k) / D ** 0.5
        seg_max = jax.ops.segment_max(scores, dst, num_segments=N)
        ex = jnp.exp(scores - seg_max[dst])
        denom = jax.ops.segment_sum(ex, dst, num_segments=N)
        w = ex / denom[dst]
        agg = jax.ops.segment_sum(w[:, :, None] * V[src], dst, num_segments=N)
        deg = jax.ops.segment_sum(jnp.ones((src.shape[0],), jnp.float32), dst, num_segments=N)
        msgs = jnp.where(deg[:, None, None] > 0, agg, V)
        out = msgs.reshape(N, H * D) @ Wo + bo
        x = out + node_features
        mu = jnp.mean(x, axis=-1, keepdims=True)
        var = jnp.var(x, axis=-1, keepdims=True)
        return (x - mu) / jnp.sqrt(var + 1e-05) * gamma + beta

    def _L1_gnn_ref(x, edge_index, W, att_src, att_dst, bias):
        import jax, jax.numpy as jnp
        import numpy as np
        N = 12500
        E = 200000
        IN = 256
        H = 4
        C = 64
        n = x.shape[0]
        loops = jnp.arange(n, dtype=edge_index.dtype)
        src = jnp.concatenate([edge_index[0], loops])
        dst = jnp.concatenate([edge_index[1], loops])
        xp = (x @ W).reshape(n, H, C)
        a_src = jnp.einsum('nhc,hc->nh', xp, att_src)
        a_dst = jnp.einsum('nhc,hc->nh', xp, att_dst)
        alpha = jax.nn.leaky_relu(a_src[src] + a_dst[dst], negative_slope=0.2)
        amax = jax.ops.segment_max(alpha, dst, num_segments=n)
        amax = jnp.where(jnp.isfinite(amax), amax, 0.0)
        ex = jnp.exp(alpha - amax[dst])
        denom = jax.ops.segment_sum(ex, dst, num_segments=n)
        w = ex / denom[dst]
        msg = xp[src] * w[..., None]
        agg = jax.ops.segment_sum(msg, dst, num_segments=n)
        out = agg.reshape(n, H * C) + bias
        return jax.nn.elu(out)
    edge_index = jnp.stack([src, dst])
    x = _layernorm(x + _L0_gnn_ref(x, edge_index, edge_type_64, L0_gnn_query_emb, L0_gnn_Wq, L0_gnn_bq, L0_gnn_Wk, L0_gnn_bk, L0_gnn_Wv, L0_gnn_bv, L0_gnn_rel_w, L0_gnn_Wo, L0_gnn_bo, L0_gnn_gamma, L0_gnn_beta), axis=-1)
    x = _layernorm(x + _L1_gnn_ref(x, edge_index, L1_gnn_W, L1_gnn_att_src, L1_gnn_att_dst, L1_gnn_bias), axis=-1)
    return x

_drawn_inputs = setup_inputs


def setup_inputs(seed=0):
    import zlib

    import numpy as np

    out = dict(_drawn_inputs(seed))
    spreads = {'L0_gnn_bq': (0.0, 0.8),
     'L0_gnn_bk': (0.0, 2.0),
     'L0_gnn_bv': (0.0, 0.398),
     'L0_gnn_bo': (0.0, 0.1),
     'L0_gnn_gamma': (1.0, 0.2),
     'L0_gnn_beta': (0.0, 0.1)}
    factors = {'L0_gnn_query_emb': 8.0,
     'L0_gnn_Wq': 8.0,
     'L0_gnn_Wk': 8.0,
     'L0_gnn_Wv': 3.798,
     'L0_gnn_rel_w': 64.0,
     'L1_gnn_bias': 6.145}
    for name, (base, spread) in spreads.items():
        noise = np.random.default_rng([zlib.crc32(name.encode()), seed]).standard_normal(out[name].shape)
        drawn = base * np.exp(spread * noise) if base else spread * noise
        out[name] = jnp.asarray(drawn.astype(out[name].dtype))
    for name, factor in factors.items():
        out[name] = (out[name] * factor).astype(out[name].dtype)
    return out
```

```python
from contextlib import ExitStack

import numpy as np
import concourse.bass as bass
from concourse import mybir

F32 = mybir.dt.float32
BF16 = mybir.dt.bfloat16
I32 = mybir.dt.int32
ALU = mybir.AluOpType
ACT = mybir.ActivationFunctionType
AX = mybir.AxisListType.X

P = 128
N = 12500
E = 200000
D = 256
HEADS = 4
HC = 64
REL = 64
TN = 32
ROWS = -(-N // P)
NP = ROWS * P
TILES = NP // TN
TPB = P // TN
CH = 5
WIN = CH * P - TN
LAST = WIN - (CH - 1) * P
SW = WIN + TN
SAMPLE = 512
NS = -(-(E + WIN) // SAMPLE)
EP = NS * SAMPLE
GT = TILES // TPB
MAXPASS = -(-E // WIN)
BIG = float(2.0 ** 100)
NOEDGE = -float(2.0 ** 90)
C1 = D + 2 * HEADS
V1 = D + P
PAD_DST = 1 << 20

C_ID, C_DIAG, C_THR, C_CMP, C_NEG, C_TAU, C_PASS = 0, 128, 160, 164, 166, 294, 298
C_CMP1 = C_PASS + MAXPASS
C_NEG1 = C_CMP1 + 2
C_N = C_NEG1 + P


def constants():
    c = np.zeros((P, C_N), np.float32)
    p = np.arange(P)
    c[:, C_ID:C_ID + P] = np.eye(P)
    c[:, C_DIAG:C_DIAG + TN] = p[:, None] % TN == np.arange(TN)
    c[:GT, C_THR:C_THR + TPB] = TN * (GT * np.arange(TPB)[None, :] + np.arange(GT)[:, None])
    c[:REL, C_CMP] = np.arange(REL)
    c[REL:REL + TN, C_CMP] = np.arange(TN)
    c[REL:REL + TN, C_CMP + 1] = 1.0
    c[REL:REL + TN, C_NEG:C_NEG + P] = -BIG * (np.arange(TN)[:, None] == p[None, :] % TN)
    c[:, C_TAU:C_TAU + TPB] = p[:, None] // TN == np.arange(TPB)
    c[:, C_PASS:C_PASS + MAXPASS] = WIN * np.arange(MAXPASS)
    c[:TN, C_CMP1:C_CMP1 + 2] = c[REL:REL + TN, C_CMP:C_CMP + 2]
    c[:TN, C_NEG1:C_NEG1 + P] = c[REL:REL + TN, C_NEG:C_NEG + P]
    return c


class Step:

    def __init__(self, q, c, unroll):
        self.q, self.c, self.unroll = q, c, unroll

    @property
    def n(self):
        return self.q * self.unroll + self.c

    def known_below(self, k):
        return isinstance(self.q, int) and self.n < k

    def slot(self, depth):
        return self.c % depth

    def use(self, depth):
        return self.q * (self.unroll // depth) + self.c // depth

    def back(self, k=1):
        return Step(self.q, self.c - k, self.unroll)


def steps(eng, count, unroll, body):
    assert count % unroll == 0
    for c in range(unroll):
        body(Step(0, c, unroll))
    with eng.Fori(1, count // unroll) as q:
        for c in range(unroll):
            body(Step(q, c, unroll))
    return Step(0, count, unroll)


class Chain:

    def __init__(self, eng, sem, per_step=0):
        self.eng, self.sem, self.per_step = eng, sem, per_step
        self.base, self.count = 0, 0

    def begin(self, step):
        assert self.count in (0, self.per_step), (self.count, self.per_step)
        self.base, self.count = step.n * self.per_step, 0

    def __call__(self, instruction):
        self.count += 1
        instruction.then_inc(self.sem, 1)
        self.eng.wait_ge(self.sem, self.base + self.count)


class Stage:

    def __init__(self, nc, tag):
        self.nc, self.tag, self.held = nc, tag, []

    def __enter__(self):
        self.ctx = ExitStack().__enter__()
        return self

    def __exit__(self, *failure):
        self.ctx.__exit__(*failure)
        if failure[0] is None and self.held:
            self.nc.clear_and_free_semaphores(self.held)
            self.nc.all_engine_barrier()

    def sb(self, name, shape, dt=F32):
        return self.ctx.enter_context(self.nc.sbuf_tensor(f"{self.tag}_{name}", shape, dt))

    def ps(self, name, shape):
        return self.ctx.enter_context(self.nc.psum_tensor(f"{self.tag}_{name}", shape, F32))

    def sem(self, name):
        self.held.append(self.nc.alloc_semaphore(f"{self.tag}_{name}"))
        return self.held[-1]

    def sems(self, name, count):
        return [self.sem(f"{name}{k}") for k in range(count)]

    def block(self):
        return self.ctx.enter_context(self.nc.Block())


class Kernel:

    def __init__(self, nc, ctx, inputs, out):
        self.nc, self.i, self.out = nc, inputs, out
        g = ctx.enter_context(Stage(nc, "all"))
        self.cst = g.sb("cst", [P, C_N])
        self.idx = g.sb("idx", [P, TILES, CH], I32)
        self.qt = g.sb("qt", [P, 2, NP])
        self.logit = g.sb("logit", [P, TILES])
        self.low = g.sb("low", [P, TILES])
        self.total = g.sb("total", [P, TILES])
        self.adst = g.sb("adst", [P, TILES])
        self.start0 = g.sb("start0", [P, TPB])
        self.start = g.sb("start", [P, TPB])
        self.start_i = g.sb("start_i", [P, TPB], I32)
        self.npass = g.sb("npass", [1, 1], I32)
        dram = lambda name, shape, dt=F32: nc.dram_tensor(name, shape, dt).ap()
        self.starts = dram("starts", (TILES,), I32)
        self.windows = dram("windows", (TILES, 3, WIN), I32)
        self.match = dram("match", (TILES, 2, WIN), BF16)
        self.kv = dram("kv", (NP, 2 * D))
        self.xp = dram("xp", (NP, V1))
        self.agg = dram("agg", (TILES, HEADS, TN, HC))
        self.x1 = dram("x1", (NP, D))
        self.ident = self.cst[:, C_ID:C_ID + P]


def gat_kernel(nc, inputs, out):
    with ExitStack() as ctx:
        k = Kernel(nc, ctx, inputs, out)
        find_windows(k)
        load_windows(k, "lw")
        project_qkv(k)
        all_passes(k, 0)
        between_layers(k)
        all_passes(k, 1)
        finish(k)


def all_passes(k, layer):
    nc = k.nc
    attention(k, layer, f"att{layer}")
    many = nc.values_load(k.npass[0:1, 0:1], min_val=1, max_val=MAXPASS)
    with nc.If(many > 1):
        with nc.Fori(1, many):
            set_windows(k, f"next{layer}", layer, first=False)
            load_windows(k, f"lwn{layer}")
            attention(k, layer, f"attn{layer}")
        set_windows(k, f"first{layer}", layer, first=True)
        load_windows(k, f"lwf{layer}")


def find_windows(k):
    nc, cst = k.nc, k.cst
    with Stage(nc, "fw") as z:
        sample_i = z.sb("sample_i", [1, NS], I32)
        sample = z.sb("sample", [1, NS])
        ones = z.sb("ones", [1, P])
        less = z.sb("less", [P, SAMPLE])
        before = z.sb("before", [P, 2, TPB])
        row_f = z.sb("row_f", [P, TPB])
        row_i = z.sb("row_i", [P, TPB], I32)
        rows = z.sb("rows", [P, TPB, SAMPLE], I32)
        all_i = z.sb("all_i", [1, TILES], I32)
        all_f = z.sb("all_f", [1, TILES + 1])
        size = z.sb("size", [1, TILES])
        most = z.sb("most", [1, 1])
        over = z.sb("over", [1, MAXPASS])
        passes_f = z.sb("passes_f", [1, 1])
        spread = z.ps("spread", [P, 512])
        consts_in, sample_in, rows_in, starts_out, starts_in = (
            z.sem(x) for x in ("consts_in", "sample_in", "rows_in", "starts_out", "starts_in"))
        sample_ready, spread_ready, rows_known, starts_ready, order = (
            z.sem(x) for x in ("sample_ready", "spread_ready", "rows_known", "starts_ready", "order"))
        dst = k.i["edges"][1:2, :]
        block = z.block()

        @block.sync
        def _(sp):
            sp.dma_start(cst[:], k.i["consts"]).then_inc(consts_in, 16)
            with nc.allow_non_contiguous_dma(reason="one destination in SAMPLE, once"):
                sp.dma_start(sample_i[:], dst.rearrange("o (n s) -> o n s", s=SAMPLE)[:, :, 0]).then_inc(sample_in, 16)
            sp.wait_ge(starts_ready, 1)
            with nc.allow_non_contiguous_dma(reason="a few hundred numbers, once"):
                sp.dma_start(k.starts.rearrange("(g p) -> p g", p=GT), k.start_i[0:GT, :]).then_inc(starts_out, 16)
            sp.wait_ge(starts_out, 16)
            sp.dma_start(all_i[:], k.starts.rearrange("(o n) -> o n", o=1)).then_inc(starts_in, 16)

        @block.tensor
        def _(pe):
            pe.wait_ge(sample_ready, 1)
            pe.matmul(spread[0:GT, 0:NS], ones[0:1, 0:GT], sample[0:1, :], start=True, stop=True).then_inc(spread_ready, 1)

        @block.gpsimd
        def _(pool):
            pool.wait_ge(rows_known, 1)
            blocks = k.i["edges"].rearrange("a (n s) -> (a n) s", s=SAMPLE)
            for g in range(TPB):
                pool.indirect_dma_start(rows[0:GT, g, :], None, blocks, bass.IndirectOffsetOnAxis(
                    ap=row_i[0:GT, g:g + 1], axis=0)).then_inc(rows_in, 16)

        @block.vector
        def _(v):
            then = Chain(v, order)
            then(v.memset(ones[:], 1.0))
            v.wait_ge(sample_in, 16)
            then(v.tensor_copy(sample[:], sample_i[:]))
            v.sem_inc(sample_ready, 1)
            v.wait_ge(spread_ready, 1)
            v.wait_ge(consts_in, 16)

            def count(level, g, numbers):
                first_node = cst[0:GT, C_THR + g:C_THR + g + 1]
                small = less[0:GT, 0:numbers.shape[-1]]
                then(v.tensor_scalar(small, numbers, first_node, None, ALU.is_lt))
                then(v.tensor_reduce(before[0:GT, level, g:g + 1], small, AX, ALU.add))

            for g in range(TPB):
                count(0, g, spread[0:GT, 0:NS])
            then(v.tensor_scalar(row_f[0:GT, :], before[0:GT, 0, :], -1.0, 0.0, ALU.add, ALU.max))
            then(v.tensor_scalar(row_i[0:GT, :], row_f[0:GT, :], float(NS), None, ALU.add))
            v.sem_inc(rows_known, 1)
            v.wait_ge(rows_in, 16 * TPB)
            for g in range(TPB):
                count(1, g, rows[0:GT, g, :])
            then(v.tensor_scalar(row_f[0:GT, :], row_f[0:GT, :], float(SAMPLE), None, ALU.mult))
            then(v.tensor_tensor(k.start0[0:GT, :], row_f[0:GT, :], before[0:GT, 1, :], ALU.add))
            then(v.tensor_copy(k.start[0:GT, :], k.start0[0:GT, :]))
            then(v.tensor_copy(k.start_i[0:GT, :], k.start0[0:GT, :]))
            v.sem_inc(starts_ready, 1)
            then(v.memset(all_f[:], float(E)))
            v.wait_ge(starts_in, 16)
            then(v.tensor_copy(all_f[:, 0:TILES], all_i[:]))
            then(v.tensor_tensor(size[:], all_f[:, 1:TILES + 1], all_f[:, 0:TILES], ALU.subtract))
            then(v.tensor_reduce(most[:], size[:], AX, ALU.max))
            then(v.tensor_scalar(over[:], cst[0:1, C_PASS:C_PASS + MAXPASS], most[:, 0:1], None, ALU.is_lt))
            then(v.tensor_reduce(passes_f[:], over[:], AX, ALU.add))
            then(v.tensor_scalar(passes_f[:], passes_f[:], 1.0, None, ALU.max))
            then(v.tensor_copy(k.npass[:], passes_f[:]))


def set_windows(k, tag, layer, first):
    nc = k.nc
    with Stage(nc, tag) as z:
        starts_ready, starts_out, log_ready, order = (z.sem(x) for x in ("starts_ready", "starts_out", "log_ready", "order"))
        log = z.sb("log", [P, TILES])
        block = z.block()

        @block.vector
        def _(v):
            then = Chain(v, order)
            if first:
                then(v.tensor_copy(k.start[0:GT, :], k.start0[0:GT, :]))
            else:
                then(v.tensor_scalar(k.start[0:GT, :], k.start[0:GT, :], float(WIN), float(E), ALU.add, ALU.min))
            then(v.tensor_copy(k.start_i[0:GT, :], k.start[0:GT, :]))
            v.sem_inc(starts_ready, 1)
            if not first:
                v.wait_ge(log_ready, 1)
                then(v.tensor_tensor(k.logit[:], log[:], k.low[:], ALU.subtract))

        @block.scalar
        def _(act):
            if not first:
                act.activation(log[:], k.total[:], ACT.Ln).then_inc(log_ready, 1)

        @block.sync
        def _(sp):
            sp.wait_ge(starts_ready, 1)
            with nc.allow_non_contiguous_dma(reason="a few hundred numbers, once"):
                sp.dma_start(k.starts.rearrange("(g p) -> p g", p=GT), k.start_i[0:GT, :]).then_inc(starts_out, 16)
            sp.wait_ge(starts_out, 16)


def load_windows(k, tag):
    nc, cst = k.nc, k.cst
    with Stage(nc, tag) as z:
        halves = 2
        copied = z.sems("copied", halves)
        block = z.block()

        def copy(eng, half):
            with eng.Fori(0, TILES // halves) as t:
                tile = t + half * (TILES // halves)
                first = eng.value_load(k.starts.rearrange("(o n) -> o n", o=1)[:, bass.ds(tile, 1)], min_val=0, max_val=E)
                eng.dma_start(k.windows[bass.ds(tile, 1)].rearrange("t a w -> (t a) w"),
                              k.i["edges"][:, bass.ds(first, WIN)]).then_inc(copied[half], 16)
            eng.wait_ge(copied[half], 16 * (TILES // halves))

        @block.sync
        def _(sp):
            copy(sp, 0)

        @block.scalar
        def _(act):
            copy(act, 1)

    with Stage(nc, tag + "b") as z:
        win = z.sb("win", [P, 2, 3, WIN], I32)
        src = z.sb("src", [P, 2, WIN])
        node = z.sb("node", [P, 2, WIN])
        row = z.sb("row", [P, 2, 2, WIN], BF16)
        turned = z.ps("turned", [P, 2, 1024])
        win_in, row_out = z.sems("win_in", 2), z.sems("row_out", 2)
        src_ready, row_ready, turned_ready, idx_ready, order, zero = (
            z.sem(x) for x in ("src_ready", "row_ready", "turned_ready", "idx_ready", "order", "zero"))
        block = z.block()

        @block.sync
        def _(sp):
            for g in range(TPB):
                if g >= 2:
                    sp.wait_ge(row_ready, g - 1)
                sp.dma_start(win[0:GT, g % 2], k.windows[GT * g:GT * g + GT]).then_inc(win_in[g % 2], 16)
            for g in range(TPB):
                sp.wait_ge(row_ready, g + 1)
                sp.dma_start(k.match[GT * g:GT * g + GT], row[0:GT, g % 2]).then_inc(row_out[g % 2], 16)
            for half in range(2):
                sp.wait_ge(row_out[half], 16 * (TPB // 2))

        @block.tensor
        def _(pe):
            for g in range(TPB):
                pe.wait_ge(src_ready, g + 1)
                if g >= 2:
                    pe.wait_ge(idx_ready, g - 1)
                for j in range(CH):
                    w = P if j < CH - 1 else LAST
                    last = pe.transpose(turned[0:w, g % 2, j * P:j * P + GT], src[0:GT, g % 2, j * P:j * P + w],
                                        k.ident[0:GT, 0:GT])
                last.then_inc(turned_ready, 1)

        @block.vector
        def _(v):
            then = Chain(v, order)
            v.memset(k.idx[:], 0).then_inc(zero, 1)
            v.wait_ge(zero, 1)
            for g in range(TPB):
                v.wait_ge(win_in[g % 2], 16 * (g // 2 + 1))
                if g >= 2:
                    v.wait_ge(turned_ready, g - 1)
                    v.wait_ge(row_out[g % 2], 16 * (g // 2))
                v.tensor_copy(src[0:GT, g % 2], win[0:GT, g % 2, 0]).then_inc(src_ready, 1)
                first_node = cst[0:GT, C_THR + g:C_THR + g + 1]
                then(v.tensor_scalar(node[0:GT, g % 2], win[0:GT, g % 2, 1], first_node, float(TN), ALU.subtract, ALU.min))
                then(v.tensor_scalar(row[0:GT, g % 2, 1], node[0:GT, g % 2], -1.0, None, ALU.max))
                then(v.tensor_copy(row[0:GT, g % 2, 0], win[0:GT, g % 2, 2]))
                v.sem_inc(row_ready, 1)
                v.wait_ge(turned_ready, g + 1)
                for j in range(CH):
                    w = P if j < CH - 1 else LAST
                    last = v.tensor_copy(k.idx[0:w, g * GT:g * GT + GT, j], turned[0:w, g % 2, j * P:j * P + GT])
                last.then_inc(idx_ready, 1)


def project_qkv(k):
    nc, cst = k.nc, k.cst
    scale = float(HC) ** -0.5
    with Stage(nc, "qkv") as z:
        wq = z.sb("wq", [P, 2, D])
        wkv = z.sb("wkv", [P, 2, 2 * D])
        bq = z.sb("bq", [P, 2])
        bkv = z.sb("bkv", [P, 2 * D])
        query = z.sb("query", [P, D])
        x = z.sb("x", [P, 2, D])
        enh = z.sb("enh", [P, 2, D])
        enh_t = z.sb("enh_t", [P, 2, D])
        kv = z.sb("kv", [P, 2, 2 * D])
        p_t = z.ps("p_t", [P, 2, 512])
        p_q = z.ps("p_q", [P, 2, 512])
        p_kv = z.ps("p_kv", [P, 2, 512])
        weights_in, x_in, kv_out = z.sem("weights_in"), z.sems("x_in", 2), z.sems("kv_out", 2)
        small_ready, enh_ready, turned, enh_t_ready, q_done, kv_done, q_copied, kv_ready, zeroed = (
            z.sem(n) for n in ("small_ready", "enh_ready", "turned", "enh_t_ready", "q_done", "kv_done",
                               "q_copied", "kv_ready", "zeroed"))
        block = z.block()

        @block.sync
        def _(sp):
            for w, dst in (("Wq", wq[:]), ("Wk", wkv[:, :, 0:D]), ("Wv", wkv[:, :, D:2 * D])):
                sp.dma_start(dst, k.i["L0_gnn_" + w].rearrange("(a p) n -> p a n", p=P)).then_inc(weights_in, 16)
            row = lambda name: k.i[name].rearrange("(o n) -> o n", o=1).broadcast_to((P, D))
            sp.dma_start(bkv[:, 0:D], row("L0_gnn_bk")).then_inc(weights_in, 16)
            sp.dma_start(bkv[:, D:2 * D], row("L0_gnn_bv")).then_inc(weights_in, 16)
            sp.dma_start(query[:], row("L0_gnn_query_emb")).then_inc(weights_in, 16)
            with nc.allow_non_contiguous_dma(reason="one bias, once"):
                sp.dma_start(bq[:], k.i["L0_gnn_bq"].rearrange("(a p) -> p a", p=P)).then_inc(weights_in, 16)

            def store(t):
                b = t.slot(2)
                sp.wait_ge(kv_ready, t.n + 1)
                sp.dma_start(k.kv[bass.ds(t.n * P, P), :], kv[:, b]).then_inc(kv_out[b], 16)
                for j in range(TPB):
                    sp.dma_start(k.agg[bass.ds(t.n * TPB + j, 1)].rearrange("t h d c -> (t d) h c"),
                                 kv[TN * j:TN * j + TN, b, D:2 * D].rearrange("d (h c) -> d h c", h=HEADS)).then_inc(kv_out[b], 16)

            def step(t):
                if not t.known_below(2):
                    sp.wait_ge(enh_ready, t.n - 1)
                sp.dma_start(x[:, t.slot(2)], k.i["x"][bass.ds(t.n * P, P), :]).then_inc(x_in[t.slot(2)], 16)
                if not t.known_below(1):
                    store(t.back())

            store(steps(sp, ROWS, 2, step).back())
            for b in range(2):
                sp.wait_ge(kv_out[b], 16 * (1 + TPB) * (ROWS // 2))

        @block.tensor
        def _(pe):
            def turn(t):
                pe.wait_ge(enh_ready, t.n + 1)
                if not t.known_below(2):
                    pe.wait_ge(enh_t_ready, t.n - 1)
                for a in range(2):
                    last = pe.transpose(p_t[:, t.slot(2), a * P:a * P + P], enh[:, t.slot(2), a * P:a * P + P], k.ident)
                last.then_inc(turned, 1)

            def project(t):
                b = t.slot(2)
                pe.wait_ge(enh_t_ready, t.n + 1)
                if not t.known_below(2):
                    pe.wait_ge(q_copied, t.n - 1)
                    pe.wait_ge(kv_ready, t.n - 1)
                for pair in range(2):
                    for a in range(2):
                        last = pe.matmul(p_q[:, b, pair * P:pair * P + P], wq[:, a, pair * P:pair * P + P],
                                         enh_t[:, b, a * P:a * P + P], start=a == 0, stop=a == 1)
                last.then_inc(q_done, 1)
                for a in range(2):
                    last = pe.matmul(p_kv[:, b], enh_t[:, b, a * P:a * P + P], wkv[:, a], start=a == 0, stop=a == 1)
                last.then_inc(kv_done, 1)

            def step(t):
                turn(t)
                if not t.known_below(1):
                    project(t.back())

            pe.wait_ge(weights_in, 16 * 7)
            project(steps(pe, ROWS, 2, step).back())

        @block.vector
        def _(v):
            def bias(t):
                b = t.slot(2)
                v.wait_ge(kv_done, t.n + 1)
                if not t.known_below(2):
                    v.wait_ge(kv_out[b], 16 * (1 + TPB) * t.use(2))
                v.tensor_tensor(kv[:, b], p_kv[:, b], bkv[:], ALU.add).then_inc(kv_ready, 1)

            def step(t):
                b = t.slot(2)
                v.wait_ge(x_in[b], 16 * (t.use(2) + 1))
                if not t.known_below(2):
                    v.wait_ge(turned, t.n - 1)
                v.scalar_tensor_tensor(enh[:, b], query[:], 0.1, x[:, b], ALU.mult, ALU.add).then_inc(enh_ready, 1)
                if not t.known_below(1):
                    bias(t.back())

            v.memset(k.logit[:], NOEDGE).then_inc(zeroed, 1)
            v.wait_ge(weights_in, 16 * 7)
            bias(steps(v, ROWS, 2, step).back())

        @block.scalar
        def _(act):
            def q_out(t):
                act.wait_ge(q_done, t.n + 1)
                for pair in range(2):
                    last = act.activation(k.qt[:, pair, bass.ds(t.n * P, P)], p_q[:, t.slot(2), pair * P:pair * P + P],
                                          ACT.Identity, bias=bq[:, pair:pair + 1], scale=scale)
                last.then_inc(q_copied, 1)

            def step(t):
                act.wait_ge(turned, t.n + 1)
                if not t.known_below(2):
                    act.wait_ge(kv_done, t.n - 1)
                act.copy(enh_t[:, t.slot(2)], p_t[:, t.slot(2), 0:D]).then_inc(enh_t_ready, 1)
                if not t.known_below(1):
                    q_out(t.back())

            act.wait_ge(weights_in, 16 * 7)
            act.mul(bq[:], bq[:], scale).then_inc(small_ready, 1)
            act.wait_ge(small_ready, 1)
            q_out(steps(act, ROWS, 2, step).back())


def attention(k, layer, tag):
    nc, cst, ident = k.nc, k.cst, k.ident
    table = k.xp if layer else k.kv
    width = V1 if layer else 2 * D
    val = 0 if layer else D
    krows = TN if layer else REL + TN
    cmp = C_CMP1 if layer else C_CMP
    with Stage(nc, tag) as z:
        rows = z.sb("rows", [P, 4, CH, width])
        index = z.sb("index", [P, 2, 4 * CH], I32)
        match = z.sb("match", [REL + TN, 2, WIN], BF16)
        hit = z.sb("hit", [REL + TN, 2, WIN], BF16 if layer else F32)
        lower = z.sb("lower", [REL + TN, 2, P], BF16 if layer else F32)
        weight = z.sb("weight", [P, 2, SW])
        weight_t = z.sb("weight_t", [P, CH * P])
        col = z.sb("col", [P, 2, 6])
        result = z.sb("result", [P, 2, HC])
        MAXED, SUM, SELF, WHOLE, INV, RAW = range(6)
        if layer:
            alpha = z.sb("alpha", [P, 2, WIN])
        else:
            kt = z.sb("kt", [P, 2, WIN])
            q = z.sb("q", [P, 2, 2, P])
            rel = z.sb("rel", [P, REL])
            rel2 = z.sb("rel2", [REL, P])
            p_kt = z.ps("p_kt", [P, 3, 512])
        p_s = z.ps("p_s", [P, 1024])
        p_w = z.ps("p_w", [P, 1024])
        p_o = z.ps("p_o", [P, 512])
        rows_in, self_in, match_in, result_out = z.sems("rows_in", 4), z.sems("self_in", 4), z.sems("match_in", 2), z.sems("result_out", 2)
        (consts_ready, index_ready, settled, hit_ready, scores_ready, low_ready, exp_done, weight_ready, turned,
         weight_t_ready, agg_done, result_ready, order, zeroed, setup) = (z.sem(n) for n in (
            "consts_ready", "index_ready", "settled", "hit_ready", "scores_ready", "low_ready", "exp_done",
            "weight_ready", "turned", "weight_t_ready", "agg_done", "result_ready", "order", "zeroed", "setup"))
        if layer:
            alpha_ready = z.sem("alpha_ready")
        else:
            rel_in, kt_turned, kt0_ready, kt1_ready, q_ready, qr_done, qr_ready = (z.sem(n) for n in (
                "rel_in", "kt_turned", "kt0_ready", "kt1_ready", "q_ready", "qr_done", "qr_ready"))
        block = z.block()

        def chunks():
            return [(j, P if j < CH - 1 else LAST) for j in range(CH)]

        @block.gpsimd
        def _(pool):
            def gather(t):
                b = t.slot(4)
                if not t.known_below(4):
                    pool.wait_ge(agg_done, t.n - 3)
                if t.slot(4) == 0:
                    half = t.slot(8) // 4
                    pool.tensor_copy(index[:, half], k.idx[:, bass.ds(t.n, 4), :].rearrange("p t j -> p (t j)")).then_inc(index_ready, 1)
                    pool.wait_ge(index_ready, t.q * 2 + t.c // 4 + 1)
                pool.sem_inc(settled, 1)
                for j, w in chunks():
                    at = t.slot(4) * CH + j
                    pool.indirect_dma_start(rows[0:w, b, j, :], None, table, bass.IndirectOffsetOnAxis(
                        ap=index[0:w, t.slot(8) // 4, at:at + 1], axis=0)).then_inc(rows_in[b], 16)

            steps(pool, TILES, 8, gather)

        @block.sync
        def _(sp):
            if not layer:
                for half in range(2):
                    sp.dma_start(rel2[:, half * HC:half * HC + HC], k.i["L0_gnn_rel_w"]).then_inc(rel_in, 16)

            def step(t):
                b, c = t.slot(4), t.slot(2)
                if not t.known_below(4):
                    sp.wait_ge(agg_done, t.n - 3)
                sp.dma_start(rows[LAST:P, b, CH - 1, val:val + D].rearrange("d (h c) -> d h c", h=HEADS),
                             k.agg[bass.ds(t.n, 1)].rearrange("t h d c -> (t d) h c")).then_inc(self_in[b], 16)
                if not t.known_below(2):
                    sp.wait_ge(hit_ready, t.n - 1)
                if not layer:
                    sp.dma_start(match[0:REL, c], k.match[bass.ds(t.n, 1), 0].broadcast_to((REL, WIN))).then_inc(match_in[c], 16)
                sp.dma_start(match[krows - TN:krows, c], k.match[bass.ds(t.n, 1), 1].broadcast_to((TN, WIN))).then_inc(match_in[c], 16)

            steps(sp, TILES, 4, step)

        @block.tensor
        def _(pe):
            def turn_keys(t):
                b = t.slot(4)
                pe.wait_ge(rows_in[b], 16 * CH * (t.use(4) + 1))
                if layer:
                    return
                if not t.known_below(1):
                    pe.wait_ge(kt0_ready, t.n)
                    pe.wait_ge(kt1_ready, t.n)
                for pair in range(2):
                    for j, w in chunks():
                        to = p_kt[:, pair, j * P:j * P + P] if j < CH - 1 else p_kt[:, 2, pair * LAST:pair * LAST + LAST]
                        last = pe.transpose(to, rows[0:w, b, j, pair * P:pair * P + P], ident[0:w, 0:w])
                last.then_inc(kt_turned, 1)
                pe.wait_ge(q_ready, t.n + 1)
                for pair in range(2):
                    last = pe.matmul(p_o[0:REL, D:D + P], rel[:, :], q[:, t.slot(2), pair], start=pair == 0, stop=pair == 1)
                last.then_inc(qr_done, 1)

            def turn_weights(t):
                pe.wait_ge(weight_ready, t.n + 1)
                if not t.known_below(1):
                    pe.wait_ge(weight_t_ready, t.n)
                for j in range(CH):
                    last = pe.transpose(p_w[:, j * P:j * P + P], weight[:, t.slot(2), j * P:j * P + P], ident)
                last.then_inc(turned, 1)

            def score(t):
                b, c = t.slot(4), t.slot(2)
                pe.wait_ge(hit_ready, t.n + 1)
                if layer:
                    for lo, hi in ((0, 512), (512, WIN)):
                        pe.matmul(p_s[:, lo:hi], lower[0:TN, 0], hit[0:TN, c, lo:hi], start=True, stop=False,
                                  skip_group_check=True)
                    for j, w in chunks():
                        last = pe.matmul(p_s[:, j * P:j * P + w], rows[0:w, b, j, D:V1], ident[0:w, 0:w], start=False,
                                         stop=j >= CH - 2, skip_group_check=True)
                else:
                    pe.wait_ge(kt0_ready, t.n + 1)
                    pe.wait_ge(kt1_ready, t.n + 1)
                    pe.wait_ge(qr_ready, t.n + 1)
                    for lo, hi in ((0, 512), (512, WIN)):
                        pe.matmul(p_s[:, lo:hi], lower[:, c], hit[:, c, lo:hi], start=True, stop=False)
                        for pair in range(2):
                            last = pe.matmul(p_s[:, lo:hi], q[:, c, pair], kt[:, pair, lo:hi], start=False, stop=pair == 1)
                last.then_inc(scores_ready, 1)

            def aggregate(t):
                b = t.slot(4)
                pe.wait_ge(weight_t_ready, t.n + 1)
                pe.wait_ge(self_in[b], 16 * (t.use(4) + 1))
                if not t.known_below(1):
                    pe.wait_ge(result_ready, t.n)
                for j in range(CH):
                    last = pe.matmul(p_o[:, 0:D], weight_t[:, j * P:j * P + P], rows[:, b, j, val:val + D],
                                     start=j == 0, stop=j == CH - 1)
                last.then_inc(agg_done, 1)

            def step(t):
                turn_keys(t)
                if not t.known_below(1):
                    turn_weights(t.back())
                score(t)
                if not t.known_below(1):
                    aggregate(t.back())

            if not layer:
                pe.wait_ge(rel_in, 32)
                pe.transpose(p_w[:, 0:REL], rel2[:, :], ident[0:REL, 0:REL]).then_inc(setup, 1)
            pe.wait_ge(consts_ready, 1)
            end = steps(pe, TILES, 4, step).back()
            turn_weights(end)
            aggregate(end)

        @block.vector
        def _(v):
            then = Chain(v, order, 2)

            def finish_weights(t):
                c = t.slot(2)
                then.begin(t)
                v.wait_ge(exp_done, t.n + 1)
                v.tensor_scalar(weight[:, c, WIN:SW], cst[:, C_DIAG:C_DIAG + TN], col[:, c, SELF:SELF + 1], None, ALU.mult).then_inc(weight_ready, 1)
                add = lambda to: v.tensor_tensor(to, col[:, c, SUM:SUM + 1], col[:, c, SELF:SELF + 1], ALU.add)
                add(k.total[:, bass.ds(t.n, 1)])
                then(add(col[:, c, WHOLE:WHOLE + 1]))
                then(v.reciprocal(col[:, c, INV:INV + 1], col[:, c, WHOLE:WHOLE + 1]))

            def step(t):
                b, c = t.slot(4), t.slot(2)
                if not t.known_below(1):
                    finish_weights(t.back())
                v.wait_ge(match_in[c], (1 if layer else 2) * 16 * (t.use(2) + 1))
                if not t.known_below(2):
                    v.wait_ge(scores_ready, t.n - 1)
                v.tensor_scalar(hit[0:krows, c], match[0:krows, c], cst[0:krows, cmp:cmp + 1],
                                cst[0:krows, cmp + 1:cmp + 2], ALU.is_equal, ALU.not_equal).then_inc(hit_ready, 1)
                if not layer:
                    for half in range(2):
                        lo = half * HC
                        to = q[lo:lo + HC, c].rearrange("p a m -> p (a m)")
                        for pair in range(2):
                            at = pair * P + (2 * pair + half) * TN
                            last = v.tensor_copy(to[:, at:at + TN], k.qt[lo:lo + HC, pair, bass.ds(t.n * TN, TN)])
                    last.then_inc(q_ready, 1)
                    v.wait_ge(kt_turned, t.n + 1)
                    v.tensor_copy(kt[:, 1, 0:512], p_kt[:, 1, :]) 
                    v.tensor_copy(kt[:, :, 512:WIN], p_kt[:, 2, 0:2 * LAST].rearrange("p (a w) -> p a w", a=2)).then_inc(kt1_ready, 1)
                    v.wait_ge(qr_done, t.n + 1)
                    v.tensor_copy(lower[0:REL, c], p_o[0:REL, D:D + P]).then_inc(qr_ready, 1)
                if not t.known_below(1):
                    v.wait_ge(turned, t.n)
                    if not t.known_below(2):
                        v.wait_ge(agg_done, t.n - 1)
                    v.tensor_copy(weight_t[:], p_w[:, 0:CH * P]).then_inc(weight_t_ready, 1)
                if layer:
                    v.wait_ge(scores_ready, t.n + 1)
                    v.tensor_scalar(alpha[:, c], p_s[:, 0:WIN], k.adst[:, bass.ds(t.n, 1)], -3.0e38, ALU.add, ALU.max,
                                    accum_out=col[:, c, RAW:RAW + 1]).then_inc(alpha_ready, 1)
                    v.wait_ge(alpha_ready, 2 * t.n + 1)
                    raw = col[:, c, RAW:RAW + 1]
                    v.scalar_tensor_tensor(col[:, c, MAXED:MAXED + 1], raw, 0.2, raw, ALU.mult, ALU.max).then_inc(setup, 1)
                    v.scalar_tensor_tensor(alpha[:, c], alpha[:, c], 0.2, alpha[:, c], ALU.mult, ALU.max).then_inc(alpha_ready, 1)
                else:
                    v.wait_ge(scores_ready, t.n + 1)
                    v.tensor_reduce(col[:, c, MAXED:MAXED + 1], p_s[:, 0:WIN], AX, ALU.max).then_inc(setup, 1)
                v.wait_ge(setup, t.n + 2)
                v.tensor_scalar(k.low[:, bass.ds(t.n, 1)], col[:, c, MAXED:MAXED + 1], k.logit[:, bass.ds(t.n, 1)], -1.0,
                                ALU.max, ALU.mult).then_inc(low_ready, 1)
                if not t.known_below(1):
                    put_result(t.back())

            def put_result(t):
                c = t.slot(2)
                v.wait_ge(agg_done, t.n + 1)
                if not t.known_below(2):
                    v.wait_ge(result_out[c], 16 * t.use(2))
                for h in range(HEADS):
                    at = slice(TN * h, TN * h + TN)
                    last = v.tensor_scalar(result[at, c], p_o[at, HC * h:HC * h + HC], col[at, c, INV:INV + 1], None, ALU.mult)
                last.then_inc(result_ready, 1)

            if layer:
                v.tensor_copy(lower[0:TN, 0], cst[0:TN, C_NEG1:C_NEG1 + P]).then_inc(setup, 1)
                v.wait_ge(setup, 1)
            else:
                v.memset(q[:], 0.0).then_inc(zeroed, 1)
                for c in range(2):
                    v.tensor_copy(lower[REL:REL + TN, c], cst[REL:REL + TN, C_NEG:C_NEG + P]).then_inc(zeroed, 1)
                v.wait_ge(setup, 1)
                v.tensor_scalar(rel[:, :], p_w[:, 0:REL], 0.2, None, ALU.mult).then_inc(zeroed, 1)
                v.wait_ge(zeroed, 4)
            v.sem_inc(consts_ready, 1)
            end = steps(v, TILES, 4, step).back()
            finish_weights(end)
            v.wait_ge(turned, TILES)
            v.wait_ge(agg_done, TILES - 1)
            v.tensor_copy(weight_t[:], p_w[:, 0:CH * P]).then_inc(weight_t_ready, 1)
            put_result(end)

        @block.scalar
        def _(act):
            def step(t):
                c = t.slot(2)
                if not layer:
                    act.wait_ge(kt_turned, t.n + 1)
                    act.copy(kt[:, 0, 0:512], p_kt[:, 0, :]).then_inc(kt0_ready, 1)
                if not t.known_below(2):
                    act.wait_ge(turned, t.n - 1)
                act.wait_ge(low_ready, t.n + 1)
                low = k.low[:, bass.ds(t.n, 1)]
                act.activation(col[:, c, SELF:SELF + 1], k.logit[:, bass.ds(t.n, 1)], ACT.Exp, bias=low)
                act.activation(weight[:, c, 0:WIN], alpha[:, c] if layer else p_s[:, 0:WIN], ACT.Exp, bias=low,
                               accum_out=col[:, c, SUM:SUM + 1]).then_inc(exp_done, 1)
                if not t.known_below(1):
                    put(t.back())

            def put(t):
                c = t.slot(2)
                act.wait_ge(result_ready, t.n + 1)
                act.dma_start(k.agg[bass.ds(t.n, 1)].rearrange("t h d c -> (t h d) c"), result[:, c]).then_inc(result_out[c], 16)

            put(steps(act, TILES, 4, step).back())
            for c in range(2):
                act.wait_ge(result_out[c], 16 * (TILES // 2))


def row(k, name, lo=0, count=D):
    return k.i[name].rearrange("(o n) -> o n", o=1).broadcast_to((P, count))


def between_layers(k):
    nc, cst, ident = k.nc, k.cst, k.ident
    with Stage(nc, "mid") as z:
        wo = z.sb("wo", [P, 2, D])
        w1 = z.sb("w1", [P, 2, C1])
        att = z.sb("att", [P, 2, D])
        prod = z.sb("prod", [P, 2, 2, D])
        bo, gamma, beta = (z.sb(n, [P, D]) for n in ("bo", "gamma", "beta"))
        eps = z.sb("eps", [P, 1])
        x = z.sb("x", [P, 2, D])
        agg = z.sb("agg", [P, 2, D])
        agg_t = z.sb("agg_t", [P, 2, D])
        y = z.sb("y", [P, 2, D])
        stats = z.sb("stats", [P, 6])
        moments = z.sb("moments", [P, 2, 2])
        std = z.sb("std", [P, 2])
        x1 = z.sb("x1", [P, 2, D])
        x1_t = z.sb("x1_t", [P, 2, D])
        row1 = z.sb("row1", [P, 2, V1])
        both_a = z.sb("both_a", [P, 2, 2 * HEADS])
        spread = z.sb("spread", [P, 2, 2 * HEADS, TN])
        sum_a = z.sb("sum_a", [P, TILES])
        leak = z.sb("leak", [P, TILES])
        p_t = z.ps("p_t", [P, 2, 512])
        p_o = z.ps("p_o", [P, 512])
        p_t1 = z.ps("p_t1", [P, 512])
        p_1 = z.ps("p_1", [P, 512])
        p_a = z.ps("p_a", [P, 512])
        weights_in, consts_ready = z.sem("weights_in"), z.sem("consts_ready")
        x_in, agg_in, x1_out, row1_out = (z.sems(n, 2) for n in ("x_in", "agg_in", "x1_out", "row1_out"))
        (agg_turned, agg_t_ready, out_done, summed, moments_ready, std_ready, x1_ready, x1_turned, x1_t_ready,
         projected, row1_ready, spread_ready, a_done, a_copied, order, setup, settled) = (z.sem(n) for n in (
            "agg_turned", "agg_t_ready", "out_done", "summed", "moments_ready", "std_ready", "x1_ready", "x1_turned",
            "x1_t_ready", "projected", "row1_ready", "spread_ready", "a_done", "a_copied", "order", "setup", "settled"))
        block = z.block()
        WEIGHTS = 7

        @block.sync
        def _(sp):
            sp.dma_start(wo[:], k.i["L0_gnn_Wo"].rearrange("(a p) n -> p a n", p=P)).then_inc(weights_in, 16)
            sp.dma_start(w1[:, :, 0:D], k.i["L1_gnn_W"].rearrange("(a p) n -> p a n", p=P)).then_inc(weights_in, 16)
            for to, name in ((bo, "L0_gnn_bo"), (gamma, "L0_gnn_gamma"), (beta, "L0_gnn_beta")):
                sp.dma_start(to[:], row(k, name)).then_inc(weights_in, 16)
            for a, name in enumerate(("L1_gnn_att_src", "L1_gnn_att_dst")):
                sp.dma_start(att[:, a], k.i[name].rearrange("(o h) c -> o (h c)", o=1).broadcast_to((P, D))).then_inc(weights_in, 16)

            def store(t):
                b = t.slot(2)
                sp.wait_ge(x1_ready, t.n + 1)
                sp.dma_start(k.x1[bass.ds(t.n * P, P), :], x1[:, b]).then_inc(x1_out[b], 16)
                sp.wait_ge(row1_ready, t.n + 1)
                sp.dma_start(k.xp[bass.ds(t.n * P, P), :], row1[:, b]).then_inc(row1_out[b], 16)
                for j in range(TPB):
                    sp.dma_start(k.agg[bass.ds(t.n * TPB + j, 1)].rearrange("t h d c -> (t d) h c"),
                                 row1[TN * j:TN * j + TN, b, 0:D].rearrange("d (h c) -> d h c", h=HEADS)).then_inc(row1_out[b], 16)

            def step(t):
                b = t.slot(2)
                if not t.known_below(2):
                    sp.wait_ge(x1_ready, t.n - 1)
                sp.dma_start(x[:, b], k.i["x"][bass.ds(t.n * P, P), :]).then_inc(x_in[b], 16)
                for j in range(TPB):
                    sp.dma_start(agg[TN * j:TN * j + TN, b].rearrange("d (h c) -> d h c", h=HEADS),
                                 k.agg[bass.ds(t.n * TPB + j, 1)].rearrange("t h d c -> (t d) h c")).then_inc(agg_in[b], 16)
                if not t.known_below(1):
                    store(t.back())

            store(steps(sp, ROWS, 2, step).back())
            for b in range(2):
                sp.wait_ge(x1_out[b], 16 * (ROWS // 2))
                sp.wait_ge(row1_out[b], 16 * (1 + TPB) * (ROWS // 2))

        @block.tensor
        def _(pe):
            def layer0(t):
                b = t.slot(2)
                pe.wait_ge(agg_in[b], 16 * TPB * (t.use(2) + 1))
                if not t.known_below(2):
                    pe.wait_ge(agg_t_ready, t.n - 1)
                for a in range(2):
                    last = pe.transpose(p_t[:, b, a * P:a * P + P], agg[:, b, a * P:a * P + P], ident)
                last.then_inc(agg_turned, 1)
                pe.wait_ge(agg_t_ready, t.n + 1)
                if not t.known_below(1):
                    pe.wait_ge(summed, t.n)
                for a in range(2):
                    last = pe.matmul(p_o[:, 0:D], agg_t[:, b, a * P:a * P + P], wo[:, a], start=a == 0, stop=a == 1)
                last.then_inc(out_done, 1)

            def layer1(t):
                b = t.slot(2)
                pe.wait_ge(x1_ready, t.n + 1)
                if not t.known_below(1):
                    pe.wait_ge(x1_t_ready, t.n)
                for a in range(2):
                    last = pe.transpose(p_t1[:, a * P:a * P + P], x1[:, b, a * P:a * P + P], ident)
                last.then_inc(x1_turned, 1)
                pe.wait_ge(x1_t_ready, t.n + 1)
                if not t.known_below(1):
                    pe.wait_ge(row1_ready, t.n)
                for a in range(2):
                    last = pe.matmul(p_1[:, 0:C1], x1_t[:, b, a * P:a * P + P], w1[:, a], start=a == 0, stop=a == 1)
                last.then_inc(projected, 1)
                pe.wait_ge(spread_ready, t.n + 1)
                if not t.known_below(1):
                    pe.wait_ge(a_copied, t.n)
                for a in range(2):
                    last = pe.matmul(p_a[:, a * TPB:a * TPB + TPB], spread[:, b, a * HEADS:a * HEADS + HEADS].rearrange("p h d -> p (h d)"),
                                     cst[:, C_TAU:C_TAU + TPB], start=True, stop=True)
                last.then_inc(a_done, 1)

            def step(t):
                layer0(t)
                if not t.known_below(1):
                    layer1(t.back())

            pe.wait_ge(weights_in, 16 * WEIGHTS)
            pe.wait_ge(consts_ready, 1)
            layer1(steps(pe, ROWS, 2, step).back())

        @block.gpsimd
        def _(pool):
            def spread_a(t):
                b = t.slot(2)
                pool.wait_ge(row1_ready, t.n + 1)
                if not t.known_below(2):
                    pool.wait_ge(a_done, t.n - 1)
                pool.tensor_tensor(spread[:, b], both_a[:, b].unsqueeze(2).broadcast_to((P, 2 * HEADS, TN)),
                                   cst[:, C_DIAG:C_DIAG + TN].unsqueeze(1).broadcast_to((P, 2 * HEADS, TN)),
                                   ALU.mult).then_inc(spread_ready, 1)

            steps(pool, ROWS, 2, spread_a)

        @block.vector
        def _(v):
            then = Chain(v, order, 9)

            def norm(t, y, which, to):
                m = moments[:, which]
                then(v.bn_stats(stats[:], y))
                v.sem_inc(settled, 1)
                v.bn_aggr(m, stats[:]).then_inc(moments_ready, 1)
                v.wait_ge(std_ready, 2 * t.n + which + 1)
                then(v.reciprocal(std[:, which:which + 1], std[:, which:which + 1]))
                return v.tensor_scalar(to, y, m[:, 0:1], std[:, which:which + 1], ALU.subtract, ALU.mult)

            def copy_a(t):
                v.wait_ge(a_done, t.n + 1)
                v.tensor_copy(k.logit[:, bass.ds(t.n * TPB, TPB)], p_a[:, 0:TPB])
                v.tensor_copy(k.adst[:, bass.ds(t.n * TPB, TPB)], p_a[:, TPB:2 * TPB]).then_inc(a_copied, 1)

            def step(t):
                b = t.slot(2)
                then.begin(t)
                v.wait_ge(x_in[b], 16 * (t.use(2) + 1))
                v.wait_ge(out_done, t.n + 1)
                v.tensor_tensor(y[:, b], p_o[:, 0:D], x[:, b], ALU.add).then_inc(summed, 1)
                v.wait_ge(summed, t.n + 1)
                then(v.tensor_tensor(y[:, b], y[:, b], bo[:], ALU.add))
                then(norm(t, y[:, b], 0, y[:, b]))
                then(v.tensor_tensor(y[:, b], y[:, b], gamma[:], ALU.mult))
                then(v.tensor_tensor(y[:, b], y[:, b], beta[:], ALU.add))
                then(v.tensor_tensor(y[:, b], y[:, b], x[:, b], ALU.add))
                if not t.known_below(2):
                    v.wait_ge(x1_turned, t.n - 1)
                    v.wait_ge(x1_out[b], 16 * t.use(2))
                norm(t, y[:, b], 1, x1[:, b]).then_inc(x1_ready, 1)
                if not t.known_below(1):
                    copy_a(t.back())

            v.memset(eps[:], 1e-5).then_inc(setup, 1)
            v.wait_ge(weights_in, 16 * WEIGHTS)
            for side in range(2):
                for a in range(2):
                    v.tensor_tensor(prod[:, side, a], w1[:, a, 0:D], att[:, side], ALU.mult).then_inc(setup, 1)
            v.wait_ge(setup, 5)
            for side in range(2):
                at = D + side * HEADS
                v.tensor_reduce(w1[:, :, at:at + HEADS], prod[:, side].rearrange("p a (h c) -> p a h c", h=HEADS), AX, ALU.add).then_inc(setup, 1)
            v.wait_ge(setup, 7)
            v.sem_inc(consts_ready, 1)
            copy_a(steps(v, ROWS, 2, step).back())
            v.wait_ge(a_copied, ROWS)
            v.tensor_tensor(sum_a[:], k.logit[:], k.adst[:], ALU.add).then_inc(setup, 1)
            v.wait_ge(setup, 8)
            v.tensor_scalar(leak[:], sum_a[:], 0.2, None, ALU.mult).then_inc(setup, 1)
            v.wait_ge(setup, 9)
            v.tensor_tensor(k.logit[:], leak[:], sum_a[:], ALU.max).then_inc(setup, 1)

        @block.scalar
        def _(act):
            def layer1(t):
                b = t.slot(2)
                act.wait_ge(x1_turned, t.n + 1)
                if not t.known_below(2):
                    act.wait_ge(projected, t.n - 1)
                act.copy(x1_t[:, b], p_t1[:, 0:D]).then_inc(x1_t_ready, 1)
                act.wait_ge(projected, t.n + 1)
                if not t.known_below(2):
                    act.wait_ge(row1_out[b], 16 * (1 + TPB) * t.use(2))
                    act.wait_ge(spread_ready, t.n - 1)
                act.copy(both_a[:, b], p_1[:, D:C1])
                act.copy(row1[:, b, D:V1].rearrange("p (h d) -> p h d", h=HEADS),
                         p_1[:, D:D + HEADS].unsqueeze(2).broadcast_to((P, HEADS, TN)))
                act.copy(row1[:, b, 0:D], p_1[:, 0:D]).then_inc(row1_ready, 1)

            def step(t):
                b = t.slot(2)
                act.wait_ge(agg_turned, t.n + 1)
                if not t.known_below(2):
                    act.wait_ge(out_done, t.n - 1)
                act.copy(agg_t[:, b], p_t[:, b, 0:D]).then_inc(agg_t_ready, 1)
                if not t.known_below(1):
                    layer1(t.back())
                for which in range(2):
                    act.wait_ge(moments_ready, 2 * t.n + which + 1)
                    act.activation(std[:, which:which + 1], moments[:, which, 1:2], ACT.Sqrt, bias=eps[:, 0:1]).then_inc(std_ready, 1)

            act.wait_ge(consts_ready, 1)
            layer1(steps(act, ROWS, 2, step).back())


def finish(k):
    nc = k.nc
    with Stage(nc, "fin") as z:
        bias = z.sb("bias", [P, D])
        eps = z.sb("eps", [P, 1])
        agg = z.sb("agg", [P, 2, D])
        x1 = z.sb("x1", [P, 2, D])
        low = z.sb("low", [P, 2, D])
        grown = z.sb("grown", [P, 2, D])
        y = z.sb("y", [P, 2, D])
        stats = z.sb("stats", [P, 6])
        moments = z.sb("moments", [P, 2, 2])
        std = z.sb("std", [P, 2])
        rstd = z.sb("rstd", [P, 2])
        res = z.sb("res", [P, 2, D])
        bias_in, setup = z.sem("bias_in"), z.sem("setup")
        in_, out_ = z.sems("in", 2), z.sems("out", 2)
        low_ready, grown_ready, var_ready, std_ready, used, res_ready, order, settled = (
            z.sem(n) for n in ("low_ready", "grown_ready", "var_ready", "std_ready", "used", "res_ready", "order", "settled"))
        block = z.block()

        @block.sync
        def _(sp):
            sp.dma_start(bias[:], row(k, "L1_gnn_bias")).then_inc(bias_in, 16)

            def store(t):
                b = t.slot(2)
                sp.wait_ge(res_ready, t.n + 1)
                sp.dma_start(k.out[bass.ds(t.n * P, P), :], res[:, b]).then_inc(out_[b], 16)

            def step(t):
                b = t.slot(2)
                if not t.known_below(2):
                    sp.wait_ge(used, t.n - 1)
                sp.dma_start(x1[:, b], k.x1[bass.ds(t.n * P, P), :]).then_inc(in_[b], 16)
                for j in range(TPB):
                    sp.dma_start(agg[TN * j:TN * j + TN, b].rearrange("d (h c) -> d h c", h=HEADS),
                                 k.agg[bass.ds(t.n * TPB + j, 1)].rearrange("t h d c -> (t d) h c")).then_inc(in_[b], 16)
                if not t.known_below(1):
                    store(t.back())

            store(steps(sp, ROWS, 2, step).back())
            for b in range(2):
                sp.wait_ge(out_[b], 16 * (ROWS // 2))

        @block.vector
        def _(v):
            then = Chain(v, order, 5)

            def first(t):
                b = t.slot(2)
                v.wait_ge(in_[b], 16 * (1 + TPB) * (t.use(2) + 1))
                then(v.tensor_tensor(agg[:, b], agg[:, b], bias[:], ALU.add))
                v.tensor_scalar(low[:, b], agg[:, b], 0.0, None, ALU.min).then_inc(low_ready, 1)
                then(v.tensor_scalar(agg[:, b], agg[:, b], 0.0, -1.0, ALU.max, ALU.add))
                v.tensor_tensor(y[:, b], agg[:, b], x1[:, b], ALU.add).then_inc(used, 1)

            def second(t):
                b = t.slot(2)
                v.wait_ge(used, t.n + 1)
                v.wait_ge(grown_ready, t.n + 1)
                then(v.tensor_tensor(y[:, b], y[:, b], grown[:, b], ALU.add))
                then(v.bn_stats(stats[:], y[:, b]))
                v.sem_inc(settled, 1)
                v.bn_aggr(moments[:, b], stats[:]).then_inc(var_ready, 1)
                v.wait_ge(std_ready, t.n + 1)
                then(v.reciprocal(rstd[:, b:b + 1], std[:, b:b + 1]))
                if not t.known_below(2):
                    v.wait_ge(out_[b], 16 * t.use(2))
                v.tensor_scalar(res[:, b], y[:, b], moments[:, b, 0:1], rstd[:, b:b + 1], ALU.subtract, ALU.mult).then_inc(res_ready, 1)

            def step(t):
                then.begin(t)
                first(t)
                second(t)

            v.memset(eps[:], 1e-5).then_inc(setup, 1)
            v.wait_ge(bias_in, 16)
            steps(v, ROWS, 2, step)

        @block.scalar
        def _(act):
            def step(t):
                b = t.slot(2)
                act.wait_ge(low_ready, t.n + 1)
                act.activation(grown[:, b], low[:, b], ACT.Exp).then_inc(grown_ready, 1)
                act.wait_ge(var_ready, t.n + 1)
                act.activation(std[:, b:b + 1], moments[:, b, 1:2], ACT.Sqrt, bias=eps[:, 0:1]).then_inc(std_ready, 1)

            act.wait_ge(setup, 1)
            steps(act, ROWS, 2, step)


def kernel(**inputs):
    import numpy as _np
    import concourse.bacc as _bacc
    from concourse import mybir as _mybir
    from concourse.bass_utils import run_bass_kernel_spmd as _run

    nc = _bacc.Bacc("TRN2", target_bir_lowering=False, num_devices=1)
    given = {name: _np.ascontiguousarray(a) for name, a in inputs.items()}
    x = given.pop("x")
    src, dst, rel = (given.pop(name) for name in ("src", "dst", "edge_type_64"))
    given["x"] = _np.concatenate([x, _np.zeros((NP - N, D), x.dtype)])
    pad = lambda a, value: _np.concatenate([a, _np.full((EP - E,), value, a.dtype)])
    given["edges"] = _np.stack([pad(src, 0), pad(dst, PAD_DST), pad(rel, 0)])
    given["consts"] = constants()
    aps = {name: nc.dram_tensor(f"in_{name}", a.shape, _mybir.dt.from_np(a.dtype), kind="ExternalInput").ap()
           for name, a in given.items()}
    out = nc.dram_tensor("out_dram", (NP, D), _mybir.dt.float32, kind="ExternalOutput").ap()
    gat_kernel(nc, aps, out)
    r = _run(nc, [{f"in_{name}": a for name, a in given.items()}], core_ids=[0])
    return r.results[0]["out_dram"][0:N]
```

```python
from contextlib import ExitStack

import numpy as np
import concourse.bass as bass
from concourse import mybir

F32 = mybir.dt.float32
BF16 = mybir.dt.bfloat16
I32 = mybir.dt.int32
ALU = mybir.AluOpType
ACT = mybir.ActivationFunctionType
AX = mybir.AxisListType.X

P = 128
N = 12500
E = 200000
D = 256
HEADS = 4
HC = 64
REL = 64
TN = 32
ROWS = -(-N // P)
NP = ROWS * P
TILES = NP // TN
TPB = P // TN
PAIRS = TILES // 2
CH = 4
MAIN = CH * P
LEFT = P
SLOTS = MAIN + LEFT
SAMPLE = 512
NS = -(-(E + SLOTS) // SAMPLE)
EP = NS * SAMPLE
GT = TILES // TPB
MAXPASS = -(-E // MAIN)
UNROLL = 8
BIG = float(2.0 ** 100)
NOEDGE = -float(2.0 ** 90)
C1 = D + 2 * HEADS
V1 = D + P
PAD_DST = 1 << 20

C_ID, C_DIAG, C_THR, C_CMP, C_NEG, C_TAU, C_GRP, C_SLOT = 0, 128, 160, 164, 166, 294, 298, 302
C_PASS = C_SLOT + LEFT
C_CMP1 = C_PASS + MAXPASS
C_NEG1 = C_CMP1 + 2
C_N = C_NEG1 + P


def constants():
    c = np.zeros((P, C_N), np.float32)
    p = np.arange(P)
    c[:, C_ID:C_ID + P] = np.eye(P)
    c[:, C_DIAG:C_DIAG + TN] = p[:, None] % TN == np.arange(TN)
    c[:GT, C_THR:C_THR + TPB] = TN * (GT * np.arange(TPB)[None, :] + np.arange(GT)[:, None])
    c[:REL, C_CMP] = np.arange(REL)
    c[REL:REL + TN, C_CMP] = np.arange(TN)
    c[REL:REL + TN, C_CMP + 1] = 1.0
    c[REL:REL + TN, C_NEG:C_NEG + P] = -BIG * (np.arange(TN)[:, None] == p[None, :] % TN)
    c[:, C_TAU:C_TAU + TPB] = p[:, None] // TN == np.arange(TPB)
    c[:, C_GRP:C_GRP + TPB] = P * p[:, None] + TN * np.arange(TPB)
    c[:, C_SLOT:C_SLOT + LEFT] = np.arange(LEFT)
    c[:, C_PASS:C_PASS + MAXPASS] = MAIN * np.arange(MAXPASS)
    c[:TN, C_CMP1:C_CMP1 + 2] = c[REL:REL + TN, C_CMP:C_CMP + 2]
    c[:TN, C_NEG1:C_NEG1 + P] = c[REL:REL + TN, C_NEG:C_NEG + P]
    return c


class Step:

    def __init__(self, q, c, unroll):
        self.q, self.c, self.unroll = q, c, unroll

    @property
    def n(self):
        return self.q * self.unroll + self.c

    def known_below(self, k):
        return isinstance(self.q, int) and self.n < k

    def slot(self, depth):
        return self.c % depth

    def use(self, depth):
        return self.q * (self.unroll // depth) + self.c // depth

    def back(self, k=1):
        return Step(self.q, self.c - k, self.unroll)


def steps(eng, count, unroll, body, peel=None):
    peel = peel or unroll
    assert count % unroll == 0 and peel % unroll == 0
    for c in range(peel):
        body(Step(0, c, unroll))
    with eng.Fori(peel // unroll, count // unroll) as q:
        for c in range(unroll):
            body(Step(q, c, unroll))
    return Step(0, count, unroll)


class Chain:

    def __init__(self, eng, sem, per_step=0):
        self.eng, self.sem, self.per_step = eng, sem, per_step
        self.base, self.count = 0, 0

    def begin(self, step):
        assert self.count in (0, self.per_step), (self.count, self.per_step)
        self.base, self.count = step.n * self.per_step, 0

    def __call__(self, instruction):
        self.count += 1
        instruction.then_inc(self.sem, 1)
        self.eng.wait_ge(self.sem, self.base + self.count)


class Stage:

    def __init__(self, nc, tag):
        self.nc, self.tag, self.held = nc, tag, []

    def __enter__(self):
        self.ctx = ExitStack().__enter__()
        return self

    def __exit__(self, *failure):
        self.ctx.__exit__(*failure)
        if failure[0] is None and self.held:
            self.nc.clear_and_free_semaphores(self.held)
            self.nc.all_engine_barrier()

    def sb(self, name, shape, dt=F32):
        return self.ctx.enter_context(self.nc.sbuf_tensor(f"{self.tag}_{name}", shape, dt))

    def ps(self, name, shape):
        return self.ctx.enter_context(self.nc.psum_tensor(f"{self.tag}_{name}", shape, F32))

    def sem(self, name):
        self.held.append(self.nc.alloc_semaphore(f"{self.tag}_{name}"))
        return self.held[-1]

    def sems(self, name, count):
        return [self.sem(f"{name}{k}") for k in range(count)]

    def block(self):
        return self.ctx.enter_context(self.nc.Block())


class Kernel:

    def __init__(self, nc, ctx, inputs, out):
        self.nc, self.i, self.out = nc, inputs, out
        g = ctx.enter_context(Stage(nc, "all"))
        self.cst = g.sb("cst", [P, C_N])
        self.idx = g.sb("idx", [P, TILES, CH], I32)
        self.left_idx = g.sb("left_idx", [P, PAIRS], I32)
        self.left = g.sb("left", [P, PAIRS, 3], I32)
        self.left_at = g.sb("left_at", [P, PAIRS], I32)
        self.starts_row = g.sb("starts_row", [1, TILES], I32)
        self.qt = g.sb("qt", [P, 2, NP])
        self.logit = g.sb("logit", [P, TILES])
        self.low = g.sb("low", [P, TILES])
        self.total = g.sb("total", [P, TILES])
        self.adst = g.sb("adst", [P, TILES])
        self.start0 = g.sb("start0", [P, TPB])
        self.start = g.sb("start", [P, TPB])
        self.start_i = g.sb("start_i", [P, TPB], I32)
        self.npass = g.sb("npass", [P, 1], I32)
        dram = lambda name, shape, dt=F32: nc.dram_tensor(name, shape, dt).ap()
        self.starts = dram("starts", (TILES + TPB,), I32)
        self.windows = dram("windows", (TILES, 3, MAIN), I32)
        self.match = dram("match", (TILES, 2, SLOTS), BF16)
        self.relq = dram("relq", (ROWS, REL, TPB, 3, P), BF16)
        self.kv = dram("kv", (NP, 2 * D))
        self.xp = dram("xp", (NP, V1))
        self.agg = dram("agg", (TILES, HEADS, TN, HC))
        self.x1 = dram("x1", (NP, D))
        self.ident = self.cst[:, C_ID:C_ID + P]


def gat_kernel(nc, inputs, out):
    with ExitStack() as ctx:
        k = Kernel(nc, ctx, inputs, out)
        find_windows(k)
        project_qkv(k)
        prepare_windows(k, "pw", shared=True)
        all_passes(k, 0)
        between_layers(k)
        all_passes(k, 1)
        finish(k)


def all_passes(k, layer):
    nc = k.nc
    attention(k, layer, f"att{layer}")
    many = nc.values_load(k.npass[0:1, 0:1], min_val=1, max_val=MAXPASS)
    with nc.If(many > 1):
        with nc.Fori(1, many):
            set_windows(k, f"next{layer}", first=False)
            prepare_windows(k, f"pwn{layer}")
            attention(k, layer, f"attn{layer}")
        set_windows(k, f"first{layer}", first=True)
        prepare_windows(k, f"pwf{layer}")


def find_windows(k):
    nc, cst = k.nc, k.cst
    with Stage(nc, "fw") as z:
        sample_i = z.sb("sample_i", [1, NS], I32)
        sample = z.sb("sample", [1, NS])
        ones = z.sb("ones", [1, P])
        less = z.sb("less", [P, SAMPLE])
        before = z.sb("before", [P, 2, TPB])
        row_f = z.sb("row_f", [P, TPB])
        row_i = z.sb("row_i", [P, TPB], I32)
        rows = z.sb("rows", [P, TPB, SAMPLE], I32)
        ends = z.sb("ends", [1, TPB], I32)
        first_i = z.sb("first_i", [P, TPB + 1], I32)
        first = z.sb("first", [P, TPB + 1])
        size = z.sb("size", [P, TPB])
        rest = z.sb("rest", [P, TPB])
        offset = z.sb("offset", [P, TPB])
        base = z.sb("base", [P, TPB])
        extreme = z.sb("extreme", [P, 2])
        most = z.sb("most", [P, 2])
        full = z.sb("full", [P, 1])
        more = z.sb("more", [P, MAXPASS - 1])
        passes_f = z.sb("passes_f", [P, 1])
        both = z.sb("both", [P, 2])
        at = z.sb("at", [P, 2, LEFT])
        behind = z.sb("behind", [P, LEFT])
        step = z.sb("step", [P, 1])
        spread = z.ps("spread", [P, 512])
        consts_in, sample_in, rows_in, starts_out, starts_in = (
            z.sem(x) for x in ("consts_in", "sample_in", "rows_in", "starts_out", "starts_in"))
        sample_ready, spread_ready, rows_known, starts_ready, order, extreme_ready, most_ready, at_ready, at_turned = (
            z.sem(x) for x in ("sample_ready", "spread_ready", "rows_known", "starts_ready", "order",
                               "extreme_ready", "most_ready", "at_ready", "at_turned"))
        dst = k.i["edges"][1:2, :]
        block = z.block()

        @block.sync
        def _(sp):
            sp.dma_start(cst[:], k.i["consts"]).then_inc(consts_in, 16)
            with nc.allow_non_contiguous_dma(reason="one destination in SAMPLE, once"):
                sp.dma_start(sample_i[:], dst.rearrange("o (n s) -> o n s", s=SAMPLE)[:, :, 0]).then_inc(sample_in, 16)
            sp.wait_ge(starts_ready, 1)
            with nc.allow_non_contiguous_dma(reason="a few hundred numbers, once"):
                sp.dma_start(k.starts[0:TILES].rearrange("(g p) -> p g", p=GT), k.start_i[0:GT, :]).then_inc(starts_out, 16)
                sp.dma_start(k.starts[TILES:].rearrange("(o n) -> o n", o=1), ends[:]).then_inc(starts_out, 16)
            sp.wait_ge(starts_out, 32)
            sp.dma_start(k.starts_row[:], k.starts[0:TILES].rearrange("(o n) -> o n", o=1)).then_inc(starts_in, 16)
            with nc.allow_non_contiguous_dma(reason="a few hundred numbers, once"):
                sp.dma_start(first_i[0:ROWS, 0:TPB], k.starts[0:TILES].rearrange("(g j) -> g j", j=TPB)).then_inc(starts_in, 16)
                sp.dma_start(first_i[0:ROWS, TPB:TPB + 1], k.starts[TPB:].rearrange("(g j) -> g j", j=TPB)[:, 0:1]).then_inc(starts_in, 16)

        @block.tensor
        def _(pe):
            pe.wait_ge(sample_ready, 1)
            pe.matmul(spread[0:GT, 0:NS], ones[0:1, 0:GT], sample[0:1, :], start=True, stop=True).then_inc(spread_ready, 1)
            pe.wait_ge(at_ready, 1)
            for u in range(2):
                last = pe.transpose(spread[:, u * P:u * P + ROWS], at[0:ROWS, u], k.ident[0:ROWS, 0:ROWS])
            last.then_inc(at_turned, 1)

        @block.gpsimd
        def _(pool):
            pool.wait_ge(rows_known, 1)
            blocks = k.i["edges"].rearrange("a (n s) -> (a n) s", s=SAMPLE)
            for g in range(TPB):
                pool.indirect_dma_start(rows[0:GT, g, :], None, blocks, bass.IndirectOffsetOnAxis(
                    ap=row_i[0:GT, g:g + 1], axis=0)).then_inc(rows_in, 16)
            pool.wait_ge(extreme_ready, 1)
            pool.partition_all_reduce(most[:], extreme[:], P, bass.bass_isa.ReduceOp.max).then_inc(most_ready, 1)

        @block.vector
        def _(v):
            then = Chain(v, order)
            then(v.memset(ones[:], 1.0))
            v.wait_ge(sample_in, 16)
            then(v.tensor_copy(sample[:], sample_i[:]))
            v.sem_inc(sample_ready, 1)
            v.wait_ge(spread_ready, 1)
            v.wait_ge(consts_in, 16)

            def count(level, g, numbers):
                first_node = cst[0:GT, C_THR + g:C_THR + g + 1]
                small = less[0:GT, 0:numbers.shape[-1]]
                then(v.tensor_scalar(small, numbers, first_node, None, ALU.is_lt))
                then(v.tensor_reduce(before[0:GT, level, g:g + 1], small, AX, ALU.add))

            for g in range(TPB):
                count(0, g, spread[0:GT, 0:NS])
            then(v.tensor_scalar(row_f[0:GT, :], before[0:GT, 0, :], -1.0, 0.0, ALU.add, ALU.max))
            then(v.tensor_scalar(row_i[0:GT, :], row_f[0:GT, :], float(NS), None, ALU.add))
            v.sem_inc(rows_known, 1)
            v.wait_ge(rows_in, 16 * TPB)
            for g in range(TPB):
                count(1, g, rows[0:GT, g, :])
            then(v.tensor_scalar(row_f[0:GT, :], row_f[0:GT, :], float(SAMPLE), None, ALU.mult))
            then(v.tensor_tensor(k.start0[0:GT, :], row_f[0:GT, :], before[0:GT, 1, :], ALU.add))
            then(v.tensor_copy(k.start[0:GT, :], k.start0[0:GT, :]))
            then(v.tensor_copy(k.start_i[0:GT, :], k.start0[0:GT, :]))
            then(v.memset(ends[:], E))
            v.sem_inc(starts_ready, 1)
            v.wait_ge(starts_in, 16 * 3)
            g = slice(0, ROWS)
            then(v.memset(extreme[:], 0.0))
            then(v.tensor_copy(first[g], first_i[g]))
            then(v.tensor_tensor(size[g], first[g, 1:TPB + 1], first[g, 0:TPB], ALU.subtract))
            then(v.tensor_scalar(rest[g], size[g], -float(MAIN), 0.0, ALU.add, ALU.max))
            then(v.memset(offset[:], 0.0))
            for j in (1, 3):
                then(v.tensor_copy(offset[g, j:j + 1], rest[g, j - 1:j]))
            then(v.tensor_reduce(both[g], rest[g].rearrange("p (u j) -> p u j", j=2), AX, ALU.add))
            then(v.tensor_reduce(extreme[g, 0:1], both[g], AX, ALU.max))
            then(v.tensor_reduce(extreme[g, 1:2], size[g], AX, ALU.max))
            v.sem_inc(extreme_ready, 1)
            v.wait_ge(most_ready, 1)
            then(v.tensor_scalar(full[:], most[:, 0:1], float(LEFT), None, ALU.is_gt))
            then(v.tensor_scalar(more[:], cst[:, C_PASS + 1:C_PASS + MAXPASS], most[:, 1:2], full[:, 0:1], ALU.is_lt, ALU.mult))
            then(v.tensor_reduce(passes_f[:], more[:], AX, ALU.add))
            then(v.tensor_scalar(k.npass[:], passes_f[:], 1.0, None, ALU.add))
            then(v.tensor_scalar(full[:], full[:], float(EP), None, ALU.mult))
            then(v.tensor_tensor(base[g], first[g, 0:TPB], offset[g], ALU.subtract))
            for u in range(2):
                j = 2 * u + 1
                slots = cst[g, C_SLOT:C_SLOT + LEFT]
                then(v.tensor_tensor(step[g], base[g, j:j + 1], base[g, j - 1:j], ALU.subtract))
                then(v.tensor_scalar(behind[g], slots, offset[g, j:j + 1], step[g, 0:1], ALU.is_ge, ALU.mult))
                then(v.tensor_scalar(at[g, u], slots, base[g, j - 1:j], float(MAIN), ALU.add, ALU.add))
                then(v.tensor_tensor(at[g, u], at[g, u], behind[g], ALU.add))
                then(v.tensor_scalar(at[g, u], at[g, u], full[g, 0:1], float(EP - 1), ALU.add, ALU.min))
            v.sem_inc(at_ready, 1)
            v.wait_ge(at_turned, 1)
            then(v.tensor_copy(k.left_at[:].rearrange("p (g u) -> p u g", u=2),
                               spread[:, 0:2 * P].rearrange("p (u g) -> p u g", u=2)[:, :, 0:ROWS]))


def set_windows(k, tag, first):
    nc = k.nc
    with Stage(nc, tag) as z:
        starts_ready, starts_out, log_ready, order = (z.sem(x) for x in ("starts_ready", "starts_out", "log_ready", "order"))
        log = z.sb("log", [P, TILES])
        block = z.block()

        @block.vector
        def _(v):
            then = Chain(v, order)
            if first:
                then(v.tensor_copy(k.start[0:GT, :], k.start0[0:GT, :]))
            else:
                then(v.tensor_scalar(k.start[0:GT, :], k.start[0:GT, :], float(MAIN), float(E), ALU.add, ALU.min))
            then(v.tensor_copy(k.start_i[0:GT, :], k.start[0:GT, :]))
            v.sem_inc(starts_ready, 1)
            if not first:
                v.wait_ge(log_ready, 1)
                then(v.tensor_tensor(k.logit[:], log[:], k.low[:], ALU.subtract))

        @block.scalar
        def _(act):
            if not first:
                act.activation(log[:], k.total[:], ACT.Ln).then_inc(log_ready, 1)

        @block.sync
        def _(sp):
            sp.wait_ge(starts_ready, 1)
            with nc.allow_non_contiguous_dma(reason="a few hundred numbers, once"):
                sp.dma_start(k.starts[0:TILES].rearrange("(g p) -> p g", p=GT), k.start_i[0:GT, :]).then_inc(starts_out, 16)
            sp.wait_ge(starts_out, 16)
            sp.dma_start(k.starts_row[:], k.starts[0:TILES].rearrange("(o n) -> o n", o=1)).then_inc(starts_out, 16)
            sp.wait_ge(starts_out, 32)

    with Stage(nc, tag + "c") as z:
        copied = z.sem("copied")
        block = z.block()

        @block.sync
        def _(sp):
            places = [sp.alloc_register(f"{tag}_place{j}") for j in range(TPB)]
            with sp.Fori(0, ROWS) as q:
                copy_windows_of(k, sp, q * TPB, places, copied)
            sp.wait_ge(copied, 16 * TILES)


def copy_windows_of(k, eng, tile, places, copied):
    eng.load(places, k.starts_row[:, bass.ds(tile, len(places))])
    for j, place in enumerate(places):
        first = eng.snap(place, min_val=0, max_val=E)
        eng.dma_start(k.windows[bass.ds(tile + j, 1)].rearrange("t a w -> (t a) w"),
                      k.i["edges"][:, bass.ds(first, MAIN)]).then_inc(copied, 16)


def prepare_windows(k, tag, shared=False):
    nc, cst = k.nc, k.cst
    with Stage(nc, tag) as z:
        win = z.sb("win", [P, 2, 3, MAIN], I32)
        src = z.sb("src", [P, 2, MAIN])
        node = z.sb("node", [P, 2, MAIN])
        row = z.sb("row", [P, 2, 2, MAIN], BF16)
        turned = z.ps("turned", [P, 2, 512])
        win_in, row_out = z.sems("win_in", 2), z.sems("row_out", 2)
        src_ready, row_ready, turned_ready, idx_ready, order = (
            z.sem(x) for x in ("src_ready", "row_ready", "turned_ready", "idx_ready", "order"))
        if shared:
            left_f = z.sb("left_f", [P, 2, 2, ROWS])
            left_rel = z.sb("left_rel", [P, 2, LEFT], BF16)
            left_row = z.sb("left_row", [P, TPB, LEFT], BF16)
            left_node = z.sb("left_node", [P, TPB, LEFT])
            left_t = z.ps("left_t", [P, 2, 2, LEFT])
            left_ready, left_turned, left_row_ready, left_out = (
                z.sem(x) for x in ("left_ready", "left_turned", "left_row_ready", "left_out"))
        block = z.block()

        @block.sync
        def _(sp):
            if shared:
                sp.wait_ge(left_row_ready, 1)
                to = k.match.rearrange("(g j) a w -> g j a w", j=TPB)
                for j in range(TPB):
                    sp.dma_start(to[:, j, 0, MAIN:SLOTS], left_rel[0:ROWS, j // 2]).then_inc(left_out, 16)
                    sp.dma_start(to[:, j, 1, MAIN:SLOTS], left_row[0:ROWS, j]).then_inc(left_out, 16)
            for g in range(TPB):
                if g >= 2:
                    sp.wait_ge(row_ready, g - 1)
                    sp.wait_ge(src_ready, g - 1)
                sp.dma_start(win[0:GT, g % 2], k.windows[GT * g:GT * g + GT]).then_inc(win_in[g % 2], 16)
            for g in range(TPB):
                sp.wait_ge(row_ready, g + 1)
                sp.dma_start(k.match[GT * g:GT * g + GT, :, 0:MAIN], row[0:GT, g % 2]).then_inc(row_out[g % 2], 16)
            for half in range(2):
                sp.wait_ge(row_out[half], 16 * (TPB // 2))
            if shared:
                sp.wait_ge(left_out, 16 * 2 * TPB)

        @block.tensor
        def _(pe):
            if shared:
                pe.wait_ge(left_ready, 1)
                for a in range(2):
                    for u in range(2):
                        last = pe.transpose(left_t[0:ROWS, a, u], left_f[:, a, u], k.ident)
                last.then_inc(left_turned, 1)
            for g in range(TPB):
                pe.wait_ge(src_ready, g + 1)
                if g >= 2:
                    pe.wait_ge(idx_ready, g - 1)
                for j in range(CH):
                    last = pe.transpose(turned[:, g % 2, j * P:j * P + GT], src[0:GT, g % 2, j * P:j * P + P],
                                        k.ident[0:GT, 0:GT])
                last.then_inc(turned_ready, 1)

        @block.vector
        def _(v):
            then = Chain(v, order)
            if shared:
                g = slice(0, ROWS)
                for a in range(2):
                    then(v.tensor_copy(left_f[:, a], k.left[:, :, 1 + a].rearrange("p (g u) -> p u g", u=2)))
                v.sem_inc(left_ready, 1)
                then(v.tensor_copy(k.left_idx[:], k.left[:, :, 0]))
                v.wait_ge(left_turned, 1)
                then(v.tensor_copy(left_rel[g], left_t[g, 1]))
                for j in range(TPB):
                    then(v.tensor_scalar(left_node[g, j], left_t[g, 0, j // 2], cst[g, C_GRP + j:C_GRP + j + 1], float(TN), ALU.subtract, ALU.min))
                    then(v.tensor_scalar(left_row[g, j], left_node[g, j], -1.0, None, ALU.max))
                v.sem_inc(left_row_ready, 1)
            for g in range(TPB):
                v.wait_ge(win_in[g % 2], 16 * (g // 2 + 1))
                if g >= 2:
                    v.wait_ge(turned_ready, g - 1)
                    v.wait_ge(row_out[g % 2], 16 * (g // 2))
                v.tensor_copy(src[0:GT, g % 2], win[0:GT, g % 2, 0]).then_inc(src_ready, 1)
                first_node = cst[0:GT, C_THR + g:C_THR + g + 1]
                then(v.tensor_scalar(node[0:GT, g % 2], win[0:GT, g % 2, 1], first_node, float(TN), ALU.subtract, ALU.min))
                then(v.tensor_scalar(row[0:GT, g % 2, 1], node[0:GT, g % 2], -1.0, None, ALU.max))
                then(v.tensor_copy(row[0:GT, g % 2, 0], win[0:GT, g % 2, 2]))
                v.sem_inc(row_ready, 1)
                v.wait_ge(turned_ready, g + 1)
                v.tensor_copy(k.idx[:, g * GT:g * GT + GT, :].rearrange("p t j -> p j t"),
                              turned[:, g % 2].rearrange("p (j t) -> p j t", j=CH)[:, :, 0:GT]).then_inc(idx_ready, 1)


def project_qkv(k):
    nc, cst = k.nc, k.cst
    scale = float(HC) ** -0.5
    LN = 14
    with Stage(nc, "qkv") as z:
        wq = z.sb("wq", [P, 2, D])
        wkv = z.sb("wkv", [P, 2, 2 * D])
        bq = z.sb("bq", [P, 2])
        bkv = z.sb("bkv", [P, 2 * D])
        query = z.sb("query", [P, D])
        x = z.sb("x", [P, 2, D])
        enh = z.sb("enh", [P, 2, D])
        enh_t = z.sb("enh_t", [P, 2, D])
        kv = z.sb("kv", [P, 2, 2 * D])
        q_now = z.sb("q_now", [P, 2, 2, P])
        p_t = z.ps("p_t", [P, 2, 512])
        p_q = z.ps("p_q", [P, 2, 512])
        p_kv = z.ps("p_kv", [P, 2, 512])
        p_rq = z.ps("p_rq", [P, 512])
        p_rel = z.ps("p_rel", [P, 512])
        rel2 = z.sb("rel2", [REL, P])
        rel = z.sb("rel", [P, 2, REL])
        rq = z.sb("rq", [REL, 2, TPB, 3, HEADS, TN], BF16)
        rest = z.sb("rest", [REL, 2, TPB, HEADS, TN])
        left_now = z.sb("left_now", [P, LN], I32)
        left_got = z.sb("left_got", [P, LN, 3], I32)
        rq_out = z.sems("rq_out", 2)
        rel_turned, rel_ready, rq_done, rq_hi, rq_rest, rq_mid, rq_ready, copied, copied2, left_now_ready, left_in, left_ready, settled = (
            z.sem(n) for n in ("rel_turned", "rel_ready", "rq_done", "rq_hi", "rq_rest", "rq_mid", "rq_ready", "copied", "copied2",
                               "left_now_ready", "left_in", "left_ready", "settled"))
        weights_in, x_in, kv_out = z.sem("weights_in"), z.sems("x_in", 2), z.sems("kv_out", 2)
        small_ready, enh_ready, turned, enh_t_ready, q_done, kv_done, q_copied, kv_ready, zeroed = (
            z.sem(n) for n in ("small_ready", "enh_ready", "turned", "enh_t_ready", "q_done", "kv_done",
                               "q_copied", "kv_ready", "zeroed"))
        block = z.block()

        @block.sync
        def _(sp):
            for w, dst in (("Wq", wq[:]), ("Wk", wkv[:, :, 0:D]), ("Wv", wkv[:, :, D:2 * D])):
                sp.dma_start(dst, k.i["L0_gnn_" + w].rearrange("(a p) n -> p a n", p=P)).then_inc(weights_in, 16)
            row = lambda name: k.i[name].rearrange("(o n) -> o n", o=1).broadcast_to((P, D))
            sp.dma_start(bkv[:, 0:D], row("L0_gnn_bk")).then_inc(weights_in, 16)
            sp.dma_start(bkv[:, D:2 * D], row("L0_gnn_bv")).then_inc(weights_in, 16)
            sp.dma_start(query[:], row("L0_gnn_query_emb")).then_inc(weights_in, 16)
            with nc.allow_non_contiguous_dma(reason="one bias, once"):
                sp.dma_start(bq[:], k.i["L0_gnn_bq"].rearrange("(a p) -> p a", p=P)).then_inc(weights_in, 16)
            for half in range(2):
                sp.dma_start(rel2[:, half * HC:half * HC + HC], k.i["L0_gnn_rel_w"]).then_inc(weights_in, 16)

            def store(t):
                b = t.slot(2)
                sp.wait_ge(kv_ready, t.n + 1)
                sp.dma_start(k.kv[bass.ds(t.n * P, P), :], kv[:, b]).then_inc(kv_out[b], 16)
                for j in range(TPB):
                    sp.dma_start(k.agg[bass.ds(t.n * TPB + j, 1)].rearrange("t h d c -> (t d) h c"),
                                 kv[TN * j:TN * j + TN, b, D:2 * D].rearrange("d (h c) -> d h c", h=HEADS)).then_inc(kv_out[b], 16)

            def store_relations(t):
                b = t.slot(2)
                sp.wait_ge(rq_ready, t.n + 1)
                sp.dma_start(k.relq[bass.ds(t.n, 1)].rearrange("o r j s m -> (o r) (j s m)"),
                             rq[:, b].rearrange("r j s h d -> r (j s h d)")).then_inc(rq_out[b], 16)

            def step(t):
                if not t.known_below(2):
                    sp.wait_ge(enh_ready, t.n - 1)
                sp.dma_start(x[:, t.slot(2)], k.i["x"][bass.ds(t.n * P, P), :]).then_inc(x_in[t.slot(2)], 16)
                if not t.known_below(2):
                    store(t.back(2))
                if not t.known_below(3):
                    store_relations(t.back(3))
                copy_windows_of(k, sp, t.n * 2, places, copied)

            places = [sp.alloc_register(f"place{j}") for j in range(2)]
            end = steps(sp, ROWS, 2, step, peel=4)
            for back in (2, 1):
                store(end.back(back))
            for back in (3, 2, 1):
                store_relations(end.back(back))
            sp.wait_ge(copied, 16 * (TILES // 2))
            for b in range(2):
                sp.wait_ge(kv_out[b], 16 * (1 + TPB) * (ROWS // 2))
                sp.wait_ge(rq_out[b], 16 * (ROWS // 2))

        @block.gpsimd
        def _(pool):
            places = [pool.alloc_register(f"pool_place{j}") for j in range(TPB)]
            with pool.Fori(TILES // 2 // TPB, TILES // TPB) as q:
                copy_windows_of(k, pool, q * TPB, places, copied2)
            pool.wait_ge(copied2, 16 * (TILES // 2))
            with pool.Fori(0, PAIRS // LN) as q:
                pool.tensor_copy(left_now[:], k.left_at[:, bass.ds(q * LN, LN)]).then_inc(left_now_ready, 1)
                pool.wait_ge(left_now_ready, q + 1)
                pool.sem_inc(settled, 1)
                for u in range(LN):
                    pool.indirect_dma_start(left_got[:, u, :], None, k.i["edge_rows"], bass.IndirectOffsetOnAxis(
                        ap=left_now[:, u:u + 1], axis=0)).then_inc(left_in, 16)
                pool.wait_ge(left_in, q * (16 * LN) + 16 * LN)
                pool.sem_inc(settled, 1)
                pool.tensor_copy(k.left[:, bass.ds(q * LN, LN), :], left_got[:]).then_inc(left_ready, 1)
                pool.wait_ge(left_ready, q + 1)
                pool.sem_inc(settled, 1)

        @block.tensor
        def _(pe):
            def turn(t):
                pe.wait_ge(enh_ready, t.n + 1)
                if not t.known_below(2):
                    pe.wait_ge(enh_t_ready, t.n - 1)
                for a in range(2):
                    last = pe.transpose(p_t[:, t.slot(2), a * P:a * P + P], enh[:, t.slot(2), a * P:a * P + P], k.ident)
                last.then_inc(turned, 1)

            def project(t):
                b = t.slot(2)
                pe.wait_ge(enh_t_ready, t.n + 1)
                if not t.known_below(2):
                    pe.wait_ge(q_copied, t.n - 1)
                    pe.wait_ge(kv_ready, t.n - 1)
                for pair in range(2):
                    for a in range(2):
                        last = pe.matmul(p_q[:, b, pair * P:pair * P + P], wq[:, a, pair * P:pair * P + P],
                                         enh_t[:, b, a * P:a * P + P], start=a == 0, stop=a == 1)
                last.then_inc(q_done, 1)
                for a in range(2):
                    last = pe.matmul(p_kv[:, b], enh_t[:, b, a * P:a * P + P], wkv[:, a], start=a == 0, stop=a == 1)
                last.then_inc(kv_done, 1)

            def relations(t):
                pe.wait_ge(q_copied, t.n + 1)
                if not t.known_below(1):
                    pe.wait_ge(rq_rest, t.n)
                for h in range(HEADS):
                    last = pe.matmul(p_rq[0:REL, h * P:h * P + P], rel[:, h % 2], q_now[:, t.slot(2), h // 2], start=True, stop=True)
                last.then_inc(rq_done, 1)

            def step(t):
                turn(t)
                if not t.known_below(1):
                    project(t.back())
                if not t.known_below(2):
                    relations(t.back(2))

            pe.wait_ge(weights_in, 16 * 9)
            pe.transpose(p_rel[:, 0:REL], rel2[:, :], k.ident[0:REL, 0:REL]).then_inc(rel_turned, 1)
            pe.wait_ge(rel_ready, 3)
            end = steps(pe, ROWS, 2, step)
            project(end.back())
            relations(end.back(2))
            relations(end.back())

        @block.vector
        def _(v):
            def split(t):
                b = t.slot(2)
                v.wait_ge(rq_hi, t.n + 1)
                psum = p_rq[0:REL].rearrange("r (h j d) -> r j h d", h=HEADS, j=TPB)
                for j in range(TPB):
                    last = v.tensor_tensor(rest[:, b, j], psum[:, j], rq[:, b, j, 0], ALU.subtract)
                last.then_inc(rq_rest, 1)
                v.wait_ge(rq_mid, t.n + 1)
                for j in range(TPB):
                    last = v.tensor_tensor(rq[:, b, j, 2], rest[:, b, j], rq[:, b, j, 1], ALU.subtract)
                last.then_inc(rq_ready, 1)

            def bias(t):
                b = t.slot(2)
                v.wait_ge(kv_done, t.n + 1)
                if not t.known_below(2):
                    v.wait_ge(kv_out[b], 16 * (1 + TPB) * t.use(2))
                v.tensor_tensor(kv[:, b], p_kv[:, b], bkv[:], ALU.add).then_inc(kv_ready, 1)

            def step(t):
                b = t.slot(2)
                v.wait_ge(x_in[b], 16 * (t.use(2) + 1))
                if not t.known_below(2):
                    v.wait_ge(turned, t.n - 1)
                v.scalar_tensor_tensor(enh[:, b], query[:], 0.1, x[:, b], ALU.mult, ALU.add).then_inc(enh_ready, 1)
                if not t.known_below(1):
                    bias(t.back())
                if not t.known_below(2):
                    split(t.back(2))

            v.memset(k.logit[:], NOEDGE).then_inc(zeroed, 1)
            v.memset(rel[:], 0.0).then_inc(rel_ready, 1)
            v.wait_ge(rel_ready, 1)
            v.wait_ge(rel_turned, 1)
            for half in range(2):
                at = slice(half * HC, half * HC + HC)
                v.tensor_scalar(rel[at, half], p_rel[at, 0:REL], 0.2, None, ALU.mult).then_inc(rel_ready, 1)
            v.wait_ge(weights_in, 16 * 9)
            end = steps(v, ROWS, 2, step)
            bias(end.back())
            for back in (2, 1):
                split(end.back(back))

        @block.scalar
        def _(act):
            def q_out(t):
                act.wait_ge(q_done, t.n + 1)
                if not t.known_below(2):
                    act.wait_ge(rq_done, t.n - 1)
                for pair in range(2):
                    act.activation(k.qt[:, pair, bass.ds(t.n * P, P)], p_q[:, t.slot(2), pair * P:pair * P + P],
                                   ACT.Identity, bias=bq[:, pair:pair + 1], scale=scale)
                    last = act.activation(q_now[:, t.slot(2), pair], p_q[:, t.slot(2), pair * P:pair * P + P],
                                          ACT.Identity, bias=bq[:, pair:pair + 1], scale=scale)
                last.then_inc(q_copied, 1)

            def split(t):
                b = t.slot(2)
                act.wait_ge(rq_done, t.n + 1)
                if not t.known_below(2):
                    act.wait_ge(rq_out[b], 16 * t.use(2))
                psum = p_rq[0:REL].rearrange("r (h j d) -> r j h d", h=HEADS, j=TPB)
                for j in range(TPB):
                    last = act.copy(rq[:, b, j, 0], psum[:, j])
                last.then_inc(rq_hi, 1)
                act.wait_ge(rq_rest, t.n + 1)
                for j in range(TPB):
                    last = act.copy(rq[:, b, j, 1], rest[:, b, j])
                last.then_inc(rq_mid, 1)

            def step(t):
                act.wait_ge(turned, t.n + 1)
                if not t.known_below(2):
                    act.wait_ge(kv_done, t.n - 1)
                act.copy(enh_t[:, t.slot(2)], p_t[:, t.slot(2), 0:D]).then_inc(enh_t_ready, 1)
                if not t.known_below(1):
                    q_out(t.back())
                if not t.known_below(2):
                    split(t.back(2))

            act.wait_ge(weights_in, 16 * 9)
            act.mul(bq[:], bq[:], scale).then_inc(small_ready, 1)
            act.wait_ge(small_ready, 1)
            end = steps(act, ROWS, 2, step)
            q_out(end.back())
            for back in (2, 1):
                split(end.back(back))


def attention(k, layer, tag):
    nc, cst, ident = k.nc, k.cst, k.ident
    table = k.xp if layer else k.kv
    width = V1 if layer else 2 * D
    val = 0 if layer else D
    parts = 1 if layer else 3
    krows = TN if layer else REL + TN
    cmp = C_CMP1 if layer else C_CMP
    neg = C_NEG1 if layer else C_NEG
    R = 8 if layer else 4
    B = 2 if layer else 1
    LAG = B
    with Stage(nc, tag) as z:
        rows = z.sb("rows", [P, R, CH, width])
        left = z.sb("left", [P, 4, width])
        index = z.sb("index", [P, 2, 4 * CH], I32)
        left_index = z.sb("left_index", [P, 4], I32)
        match = z.sb("match", [REL + TN, 2, SLOTS], BF16)
        hit = z.sb("hit", [REL + TN, 2, SLOTS], BF16)
        lower = z.sb("lower", [REL + TN, 2, parts, P], BF16)
        value = z.sb("value", [P, 4, HC])
        weight = z.sb("weight", [P, 2, SLOTS])
        weight_t = z.sb("weight_t", [P, SLOTS])
        col = z.sb("col", [P, 4, 6])
        MAXED, SUM, SELF, WHOLE, INV, RAW = range(6)
        joined = z.sb("joined", [P, HC])
        result = z.sb("result", [P, 2, HC])
        if layer:
            alpha = z.sb("alpha", [P, 2, SLOTS])
        else:
            kt = z.sb("kt", [P, 2, MAIN])
            left_kt = z.sb("left_kt", [P, 2, 2, LEFT])
            q = z.sb("q", [P, 2, 2, P])
            p_kt = z.ps("p_kt", [P, 2, 512])
            p_left = z.ps("p_left", [P, 512])
        p_s = z.ps("p_s", [P, B, 1024])
        p_w = z.ps("p_w", [P, 1024])
        p_o = z.ps("p_o", [P, 512])
        rows_in, left_in, value_in = z.sems("rows_in", R), z.sems("left_in", 4), z.sems("value_in", 4)
        match_in, result_out = z.sems("match_in", 2), z.sems("result_out", 2)
        (consts_ready, index_ready, settled, hit_ready, scores_ready, low_ready, exp_done, turned,
         weight_t_ready, agg_done, result_ready, max_ready, order, joined_ready, setup) = (z.sem(n) for n in (
            "consts_ready", "index_ready", "settled", "hit_ready", "scores_ready", "low_ready", "exp_done",
            "turned", "weight_t_ready", "agg_done", "result_ready", "max_ready", "order", "joined_ready", "setup"))
        if layer:
            alpha_ready = z.sem("alpha_ready")
        else:
            kt_turned, left_turned, kt0_ready, kt1_ready, left_kt_ready, q_ready = (z.sem(n) for n in (
                "kt_turned", "left_turned", "kt0_ready", "kt1_ready", "left_kt_ready", "q_ready"))
        block = z.block()
        MATCHED = 32 if layer else 64

        def pair_of(t):
            return t.slot(UNROLL) // 2, t.q * (UNROLL // 2) + t.c // 2, t.q + t.c // UNROLL

        @block.gpsimd
        def _(pool):
            def gather(t):
                b, r = t.slot(4), t.slot(R)
                ls, pair, _ = pair_of(t)
                half = t.slot(UNROLL) // 4
                if not t.known_below(R):
                    pool.wait_ge(agg_done, t.n - R + (1 if R < 8 or b % 2 else 2))
                if b == 0:
                    if not t.known_below(8):
                        pool.wait_ge(scores_ready, t.n - 4)
                    pool.tensor_copy(index[:, half], k.idx[:, bass.ds(t.n, TPB), :].rearrange("p t j -> p (t j)")).then_inc(index_ready, 1)
                    pool.tensor_copy(left_index[:, 2 * half:2 * half + 2], k.left_idx[:, bass.ds(pair, 2)]).then_inc(index_ready, 1)
                    pool.wait_ge(index_ready, t.q * 4 + (t.c // 4) * 2 + 2)
                pool.sem_inc(settled, 1)
                if b % 2 == 0:
                    pool.indirect_dma_start(left[:, ls, :], None, table, bass.IndirectOffsetOnAxis(
                        ap=left_index[:, ls:ls + 1], axis=0)).then_inc(left_in[ls], 16)
                for j in range(CH):
                    at = b * CH + j
                    pool.indirect_dma_start(rows[:, r, j, :], None, table, bass.IndirectOffsetOnAxis(
                        ap=index[:, half, at:at + 1], axis=0)).then_inc(rows_in[r], 16)

            steps(pool, TILES, UNROLL, gather)

        @block.sync
        def _(sp):
            def step(t):
                b, c = t.slot(4), t.slot(2)
                if not t.known_below(4):
                    sp.wait_ge(result_ready, t.n - 3)
                sp.dma_start(value[:, b], k.agg[bass.ds(t.n, 1)].rearrange("t h d c -> (t h d) c")).then_inc(value_in[b], 16)
                if not t.known_below(2):
                    sp.wait_ge(scores_ready, t.n - 1)
                if not layer:
                    sp.dma_start(match[0:REL, c], k.match[bass.ds(t.n, 1), 0].broadcast_to((REL, SLOTS))).then_inc(match_in[c], 16)
                    sp.dma_start(lower[0:REL, c], k.relq[bass.ds(t.q * 2 + t.c // TPB, 1), :, b].rearrange("o r s m -> (o r) s m")).then_inc(match_in[c], 32)
                sp.dma_start(match[krows - TN:krows, c], k.match[bass.ds(t.n, 1), 1].broadcast_to((TN, SLOTS))).then_inc(match_in[c], 16 if not layer else 32)

            steps(sp, TILES, UNROLL, step)

        @block.tensor
        def _(pe):
            def turn_keys(t):
                b = t.slot(4)
                ls, pair, used = pair_of(t)
                pe.wait_ge(rows_in[t.slot(R)], t.use(R) * (16 * CH) + 16 * CH)
                if b % 2 == 0:
                    pe.wait_ge(left_in[ls], used * 16 + 16)
                if layer:
                    return
                if b % 2 == 0:
                    for pair in range(2):
                        last = pe.transpose(p_left[:, pair * P:pair * P + P], left[:, ls, pair * P:pair * P + P], ident)
                    last.then_inc(left_turned, 1)
                if not t.known_below(1):
                    pe.wait_ge(kt0_ready, t.n)
                    pe.wait_ge(kt1_ready, t.n)
                for pair in range(2):
                    for j in range(CH):
                        last = pe.transpose(p_kt[:, pair, j * P:j * P + P], rows[:, b, j, pair * P:pair * P + P], ident)
                last.then_inc(kt_turned, 1)

            def turn_weights(t):
                pe.wait_ge(exp_done, t.n + 1)
                if not t.known_below(1):
                    pe.wait_ge(weight_t_ready, t.n)
                for j in range(CH + 1):
                    last = pe.transpose(p_w[:, j * P:j * P + P], weight[:, t.slot(2), j * P:j * P + P], ident)
                last.then_inc(turned, 1)

            def score(t):
                b, c = t.slot(4), t.slot(2)
                ls, pair_number, _ = pair_of(t)
                ps = p_s[:, t.slot(B)]
                pe.wait_ge(hit_ready, t.n + 1)
                for lo, hi in ((0, MAIN), (MAIN, SLOTS)):
                    for part in range(parts):
                        pe.matmul(ps[:, lo:hi], lower[0:krows, 0 if layer else c, part], hit[0:krows, c, lo:hi],
                                  start=part == 0, stop=False, skip_group_check=True)
                if layer:
                    for j in range(CH + 1):
                        a_src = rows[:, t.slot(R), j, D:V1] if j < CH else left[:, ls, D:V1]
                        last = pe.matmul(ps[:, j * P:j * P + P], a_src, ident, start=False, stop=j >= CH - 1, skip_group_check=True)
                else:
                    pe.wait_ge(kt0_ready, t.n + 1)
                    pe.wait_ge(kt1_ready, t.n + 1)
                    pe.wait_ge(left_kt_ready, pair_number + 1)
                    pe.wait_ge(q_ready, t.n + 1)
                    for pair in range(2):
                        pe.matmul(ps[:, 0:MAIN], q[:, c, pair], kt[:, pair], start=False, stop=pair == 1, skip_group_check=True)
                        last = pe.matmul(ps[:, MAIN:SLOTS], q[:, c, pair], left_kt[:, b // 2, pair], start=False, stop=pair == 1,
                                         skip_group_check=True)
                last.then_inc(scores_ready, 1)

            def aggregate(t):
                ls, _, _ = pair_of(t)
                pe.wait_ge(weight_t_ready, t.n + 1)
                if not t.known_below(1):
                    pe.wait_ge(joined_ready, t.n)
                for j in range(CH + 1):
                    v = rows[:, t.slot(R), j, val:val + D] if j < CH else left[:, ls, val:val + D]
                    for h in range(HEADS):
                        at = TN * h
                        last = pe.matmul(p_o[at:at + TN, 0:HC], weight_t[:, j * P + at:j * P + at + TN], v[:, HC * h:HC * h + HC],
                                         start=j == 0, stop=j == CH, tile_position=(0, at), skip_group_check=True)
                last.then_inc(agg_done, 1)

            def step(t):
                turn_keys(t)
                if not t.known_below(LAG):
                    turn_weights(t.back(LAG))
                score(t)
                if not t.known_below(LAG):
                    aggregate(t.back(LAG))

            pe.wait_ge(consts_ready, 1)
            end = steps(pe, TILES, UNROLL, step)
            for back in range(LAG, 0, -1):
                turn_weights(end.back(back))
                aggregate(end.back(back))

        @block.vector
        def _(v):
            then = Chain(v, order, 2)

            def sums(t):
                c = t.slot(4)
                then.begin(t)
                v.wait_ge(exp_done, t.n + 1)
                add = lambda to: v.tensor_tensor(to, col[:, c, SUM:SUM + 1], col[:, c, SELF:SELF + 1], ALU.add)
                add(k.total[:, bass.ds(t.n, 1)])
                then(add(col[:, c, WHOLE:WHOLE + 1]))
                then(v.reciprocal(col[:, c, INV:INV + 1], col[:, c, WHOLE:WHOLE + 1]))

            def copy_weights(t):
                v.wait_ge(turned, t.n + 1)
                if not t.known_below(1):
                    v.wait_ge(agg_done, t.n)
                v.tensor_copy(weight_t[:], p_w[:, 0:SLOTS]).then_inc(weight_t_ready, 1)

            def put_result(t):
                b, c, o = t.slot(4), t.slot(4), t.slot(2)
                v.wait_ge(agg_done, t.n + 1)
                v.wait_ge(value_in[b], t.use(4) * 16 + 16)
                v.scalar_tensor_tensor(joined[:], value[:, b], col[:, c, SELF:SELF + 1], p_o[:, 0:HC], ALU.mult, ALU.add).then_inc(joined_ready, 1)
                if not t.known_below(2):
                    v.wait_ge(result_out[o], t.use(2) * 16)
                v.wait_ge(joined_ready, t.n + 1)
                v.tensor_scalar(result[:, o], joined[:], col[:, c, INV:INV + 1], None, ALU.mult).then_inc(result_ready, 1)

            def step(t):
                b, c = t.slot(4), t.slot(2)
                _, pair, _ = pair_of(t)
                v.wait_ge(match_in[c], t.use(2) * MATCHED + MATCHED)
                if not t.known_below(2):
                    v.wait_ge(scores_ready, t.n - 1)
                v.tensor_scalar(hit[0:krows, c], match[0:krows, c], cst[0:krows, cmp:cmp + 1],
                                cst[0:krows, cmp + 1:cmp + 2], ALU.is_equal, ALU.not_equal).then_inc(hit_ready, 1)
                if not layer:
                    for h in range(HEADS):
                        lo = (h % 2) * HC
                        last = v.tensor_copy(q[lo:lo + HC, c, h // 2, h * TN:h * TN + TN], k.qt[lo:lo + HC, h // 2, bass.ds(t.n * TN, TN)])
                    last.then_inc(q_ready, 1)
                    if b % 2 == 0:
                        v.wait_ge(left_turned, pair + 1)
                        v.tensor_copy(left_kt[:, b // 2], p_left[:, 0:2 * LEFT].rearrange("p (a w) -> p a w", a=2)).then_inc(left_kt_ready, 1)
                    v.wait_ge(kt_turned, t.n + 1)
                    v.tensor_copy(kt[:, 1], p_kt[:, 1]).then_inc(kt1_ready, 1)
                if not t.known_below(LAG):
                    copy_weights(t.back(LAG))
                    sums(t.back(LAG))
                v.wait_ge(scores_ready, t.n + 1)
                m = t.slot(4)
                ps = p_s[:, t.slot(B), 0:SLOTS]
                if layer:
                    raw = col[:, m, RAW:RAW + 1]
                    v.tensor_scalar(alpha[:, c], ps, k.adst[:, bass.ds(t.n, 1)], -3.0e38, ALU.add, ALU.max,
                                    accum_out=raw).then_inc(alpha_ready, 1)
                    v.wait_ge(alpha_ready, 2 * t.n + 1)
                    v.scalar_tensor_tensor(col[:, m, MAXED:MAXED + 1], raw, 0.2, raw, ALU.mult, ALU.max).then_inc(max_ready, 1)
                    v.scalar_tensor_tensor(alpha[:, c], alpha[:, c], 0.2, alpha[:, c], ALU.mult, ALU.max).then_inc(alpha_ready, 1)
                else:
                    v.tensor_reduce(col[:, m, MAXED:MAXED + 1], ps, AX, ALU.max).then_inc(max_ready, 1)
                v.wait_ge(max_ready, t.n + 1)
                v.tensor_scalar(k.low[:, bass.ds(t.n, 1)], col[:, m, MAXED:MAXED + 1], k.logit[:, bass.ds(t.n, 1)], -1.0,
                                ALU.max, ALU.mult).then_inc(low_ready, 1)
                if not t.known_below(LAG):
                    put_result(t.back(LAG))

            if layer:
                v.tensor_copy(lower[0:TN, 0, 0], cst[0:TN, neg:neg + P]).then_inc(setup, 1)
                v.wait_ge(setup, 1)
            else:
                v.memset(q[:], 0.0).then_inc(setup, 1)
                v.memset(lower[REL:REL + TN], 0.0).then_inc(setup, 1)
                v.wait_ge(setup, 2)
                for c in range(2):
                    v.tensor_copy(lower[REL:REL + TN, c, 0], cst[REL:REL + TN, neg:neg + P]).then_inc(setup, 1)
                v.wait_ge(setup, 4)
            v.sem_inc(consts_ready, 1)
            end = steps(v, TILES, UNROLL, step)
            for back in range(LAG, 0, -1):
                copy_weights(end.back(back))
                sums(end.back(back))
                put_result(end.back(back))

        @block.scalar
        def _(act):
            def step(t):
                c, m = t.slot(2), t.slot(4)
                if not layer:
                    act.wait_ge(kt_turned, t.n + 1)
                    act.copy(kt[:, 0], p_kt[:, 0]).then_inc(kt0_ready, 1)
                if not t.known_below(2):
                    act.wait_ge(turned, t.n - 1)
                act.wait_ge(low_ready, t.n + 1)
                if layer:
                    act.wait_ge(alpha_ready, 2 * t.n + 2)
                low = k.low[:, bass.ds(t.n, 1)]
                act.activation(col[:, m, SELF:SELF + 1], k.logit[:, bass.ds(t.n, 1)], ACT.Exp, bias=low)
                act.activation(weight[:, c], alpha[:, c] if layer else p_s[:, 0, 0:SLOTS], ACT.Exp, bias=low,
                               accum_out=col[:, m, SUM:SUM + 1]).then_inc(exp_done, 1)
                if not t.known_below(LAG):
                    put(t.back(LAG))

            def put(t):
                c = t.slot(2)
                act.wait_ge(result_ready, t.n + 1)
                act.dma_start(k.agg[bass.ds(t.n, 1)].rearrange("t h d c -> (t h d) c"), result[:, c]).then_inc(result_out[c], 16)

            end = steps(act, TILES, UNROLL, step)
            for back in range(LAG, 0, -1):
                put(end.back(back))
            for c in range(2):
                act.wait_ge(result_out[c], 16 * (TILES // 2))


def row(k, name, lo=0, count=D):
    return k.i[name].rearrange("(o n) -> o n", o=1).broadcast_to((P, count))


def between_layers(k):
    nc, cst, ident = k.nc, k.cst, k.ident
    with Stage(nc, "mid") as z:
        wo = z.sb("wo", [P, 2, D])
        w1 = z.sb("w1", [P, 2, C1])
        att = z.sb("att", [P, 2, D])
        prod = z.sb("prod", [P, 2, 2, D])
        bo, gamma, beta = (z.sb(n, [P, D]) for n in ("bo", "gamma", "beta"))
        eps = z.sb("eps", [P, 1])
        x = z.sb("x", [P, 2, D])
        agg = z.sb("agg", [P, 2, D])
        agg_t = z.sb("agg_t", [P, 2, D])
        y = z.sb("y", [P, 2, D])
        x_bo = z.sb("x_bo", [P, 2, D])
        x_beta = z.sb("x_beta", [P, 2, D])
        stats = z.sb("stats", [P, 2, 6])
        moments = z.sb("moments", [P, 2, 2, 2])
        std = z.sb("std", [P, 2, 2])
        rstd = z.sb("rstd", [P, 2, 2])
        x1 = z.sb("x1", [P, 2, D])
        x1_t = z.sb("x1_t", [P, 2, D])
        row1 = z.sb("row1", [P, 2, V1])
        both_a = z.sb("both_a", [P, 2, 2 * HEADS])
        spread = z.sb("spread", [P, 2, 2 * HEADS, TN])
        sum_a = z.sb("sum_a", [P, TILES])
        leak = z.sb("leak", [P, TILES])
        p_t = z.ps("p_t", [P, 2, 512])
        p_o = z.ps("p_o", [P, 512])
        p_t1 = z.ps("p_t1", [P, 512])
        p_1 = z.ps("p_1", [P, 512])
        p_a = z.ps("p_a", [P, 2, 512])
        weights_in, consts_ready = z.sem("weights_in"), z.sem("consts_ready")
        x_in, agg_in, x1_out, row1_out = (z.sems(n, 2) for n in ("x_in", "agg_in", "x1_out", "row1_out"))
        (residual_ready, moments1, moments2, std1, std2, normed, order1, order2, order3) = (z.sem(n) for n in (
            "residual_ready", "moments1", "moments2", "std1", "std2", "normed", "order1", "order2", "order3"))
        (agg_turned, agg_t_ready, out_done, summed, x1_ready, x1_turned, x1_t_ready,
         projected, row1_ready, spread_ready, a_done, a_copied, setup, settled) = (z.sem(n) for n in (
            "agg_turned", "agg_t_ready", "out_done", "summed", "x1_ready", "x1_turned",
            "x1_t_ready", "projected", "row1_ready", "spread_ready", "a_done", "a_copied", "setup", "settled"))
        block = z.block()
        WEIGHTS = 7

        @block.sync
        def _(sp):
            sp.dma_start(wo[:], k.i["L0_gnn_Wo"].rearrange("(a p) n -> p a n", p=P)).then_inc(weights_in, 16)
            sp.dma_start(w1[:, :, 0:D], k.i["L1_gnn_W"].rearrange("(a p) n -> p a n", p=P)).then_inc(weights_in, 16)
            for to, name in ((bo, "L0_gnn_bo"), (gamma, "L0_gnn_gamma"), (beta, "L0_gnn_beta")):
                sp.dma_start(to[:], row(k, name)).then_inc(weights_in, 16)
            for a, name in enumerate(("L1_gnn_att_src", "L1_gnn_att_dst")):
                sp.dma_start(att[:, a], k.i[name].rearrange("(o h) c -> o (h c)", o=1).broadcast_to((P, D))).then_inc(weights_in, 16)

            def store(t):
                b = t.slot(2)
                sp.wait_ge(x1_ready, t.n + 1)
                sp.dma_start(k.x1[bass.ds(t.n * P, P), :], x1[:, b]).then_inc(x1_out[b], 16)
                sp.wait_ge(row1_ready, t.n + 1)
                sp.dma_start(k.xp[bass.ds(t.n * P, P), :], row1[:, b]).then_inc(row1_out[b], 16)
                for j in range(TPB):
                    sp.dma_start(k.agg[bass.ds(t.n * TPB + j, 1)].rearrange("t h d c -> (t d) h c"),
                                 row1[TN * j:TN * j + TN, b, 0:D].rearrange("d (h c) -> d h c", h=HEADS)).then_inc(row1_out[b], 16)

            def step(t):
                b = t.slot(2)
                if not t.known_below(2):
                    sp.wait_ge(residual_ready, t.n - 1)
                    sp.wait_ge(agg_turned, t.n - 1)
                sp.dma_start(x[:, b], k.i["x"][bass.ds(t.n * P, P), :]).then_inc(x_in[b], 16)
                for j in range(TPB):
                    sp.dma_start(agg[TN * j:TN * j + TN, b].rearrange("d (h c) -> d h c", h=HEADS),
                                 k.agg[bass.ds(t.n * TPB + j, 1)].rearrange("t h d c -> (t d) h c")).then_inc(agg_in[b], 16)
                if not t.known_below(3):
                    store(t.back(3))

            end = steps(sp, ROWS, 2, step, peel=4)
            for back in (3, 2, 1):
                store(end.back(back))
            for b in range(2):
                sp.wait_ge(x1_out[b], 16 * (ROWS // 2))
                sp.wait_ge(row1_out[b], 16 * (1 + TPB) * (ROWS // 2))

        @block.tensor
        def _(pe):
            def layer0(t):
                b = t.slot(2)
                pe.wait_ge(agg_in[b], 16 * TPB * (t.use(2) + 1))
                if not t.known_below(2):
                    pe.wait_ge(agg_t_ready, t.n - 1)
                for a in range(2):
                    last = pe.transpose(p_t[:, b, a * P:a * P + P], agg[:, b, a * P:a * P + P], ident)
                last.then_inc(agg_turned, 1)
                pe.wait_ge(agg_t_ready, t.n + 1)
                if not t.known_below(1):
                    pe.wait_ge(summed, t.n)
                for a in range(2):
                    last = pe.matmul(p_o[:, 0:D], agg_t[:, b, a * P:a * P + P], wo[:, a], start=a == 0, stop=a == 1)
                last.then_inc(out_done, 1)

            def layer1(t):
                b = t.slot(2)
                pe.wait_ge(x1_ready, t.n + 1)
                if not t.known_below(1):
                    pe.wait_ge(x1_t_ready, t.n)
                for a in range(2):
                    last = pe.transpose(p_t1[:, a * P:a * P + P], x1[:, b, a * P:a * P + P], ident)
                last.then_inc(x1_turned, 1)
                pe.wait_ge(x1_t_ready, t.n + 1)
                if not t.known_below(1):
                    pe.wait_ge(row1_ready, t.n)
                for a in range(2):
                    last = pe.matmul(p_1[:, 0:C1], x1_t[:, b, a * P:a * P + P], w1[:, a], start=a == 0, stop=a == 1)
                last.then_inc(projected, 1)
                pe.wait_ge(spread_ready, t.n + 1)
                if not t.known_below(2):
                    pe.wait_ge(a_copied, t.n - 1)
                for a in range(2):
                    last = pe.matmul(p_a[:, b, a * TPB:a * TPB + TPB], spread[:, b, a * HEADS:a * HEADS + HEADS].rearrange("p h d -> p (h d)"),
                                     cst[:, C_TAU:C_TAU + TPB], start=True, stop=True)
                last.then_inc(a_done, 1)

            def step(t):
                layer0(t)
                if not t.known_below(2):
                    layer1(t.back(2))

            pe.wait_ge(weights_in, 16 * WEIGHTS)
            pe.wait_ge(consts_ready, 1)
            end = steps(pe, ROWS, 2, step, peel=4)
            layer1(end.back(2))
            layer1(end.back())

        @block.gpsimd
        def _(pool):
            def residual(t):
                b = t.slot(2)
                pool.wait_ge(x_in[b], 16 * (t.use(2) + 1))
                if not t.known_below(2):
                    pool.wait_ge(summed, t.n - 1)
                    pool.wait_ge(normed, t.n - 1)
                pool.tensor_tensor(x_bo[:, b], x[:, b], bo[:], ALU.add)
                pool.tensor_tensor(x_beta[:, b], x[:, b], beta[:], ALU.add).then_inc(residual_ready, 1)

            def spread_a(t):
                b = t.slot(2)
                pool.wait_ge(row1_ready, t.n + 1)
                if not t.known_below(2):
                    pool.wait_ge(a_done, t.n - 1)
                pool.tensor_tensor(spread[:, b], both_a[:, b].unsqueeze(2).broadcast_to((P, 2 * HEADS, TN)),
                                   cst[:, C_DIAG:C_DIAG + TN].unsqueeze(1).broadcast_to((P, 2 * HEADS, TN)),
                                   ALU.mult).then_inc(spread_ready, 1)

            def step(t):
                residual(t)
                if not t.known_below(3):
                    spread_a(t.back(3))

            pool.wait_ge(weights_in, 16 * WEIGHTS)
            end = steps(pool, ROWS, 2, step, peel=4)
            for back in (3, 2, 1):
                spread_a(end.back(back))

        @block.vector
        def _(v):
            one, two, three = Chain(v, order1, 1), Chain(v, order2, 4), Chain(v, order3, 1)

            def summing(t):
                b = t.slot(2)
                one.begin(t)
                if not t.known_below(2):
                    v.wait_ge(x1_ready, t.n - 1)
                v.wait_ge(residual_ready, t.n + 1)
                v.wait_ge(out_done, t.n + 1)
                v.tensor_tensor(y[:, b], p_o[:, 0:D], x_bo[:, b], ALU.add).then_inc(summed, 1)
                v.wait_ge(summed, t.n + 1)
                one(v.bn_stats(stats[:, 0], y[:, b]))
                v.sem_inc(settled, 1)
                v.bn_aggr(moments[:, b, 0], stats[:, 0]).then_inc(moments1, 1)

            def norming(t):
                b = t.slot(2)
                two.begin(t)
                v.wait_ge(moments1, t.n + 1)
                two(v.scalar_tensor_tensor(y[:, b], y[:, b], moments[:, b, 0, 0:1], gamma[:], ALU.subtract, ALU.mult))
                v.wait_ge(std1, t.n + 1)
                two(v.reciprocal(rstd[:, b, 0:1], std[:, b, 0:1]))
                two(v.scalar_tensor_tensor(y[:, b], y[:, b], rstd[:, b, 0:1], x_beta[:, b], ALU.mult, ALU.add))
                two(v.bn_stats(stats[:, 1], y[:, b]))
                v.sem_inc(settled, 1)
                v.bn_aggr(moments[:, b, 1], stats[:, 1]).then_inc(moments2, 1)
                v.sem_inc(normed, 1)

            def ending(t):
                b = t.slot(2)
                three.begin(t)
                v.wait_ge(moments2, t.n + 1)
                v.wait_ge(std2, t.n + 1)
                three(v.reciprocal(rstd[:, b, 1:2], std[:, b, 1:2]))
                if not t.known_below(2):
                    v.wait_ge(x1_turned, t.n - 1)
                    v.wait_ge(x1_out[b], 16 * t.use(2))
                v.tensor_scalar(x1[:, b], y[:, b], moments[:, b, 1, 0:1], rstd[:, b, 1:2], ALU.subtract, ALU.mult).then_inc(x1_ready, 1)

            def copy_a(t):
                v.wait_ge(a_done, t.n + 1)
                v.tensor_copy(k.logit[:, bass.ds(t.n * TPB, TPB)], p_a[:, t.slot(2), 0:TPB])
                v.tensor_copy(k.adst[:, bass.ds(t.n * TPB, TPB)], p_a[:, t.slot(2), TPB:2 * TPB]).then_inc(a_copied, 1)

            def step(t):
                if not t.known_below(2):
                    ending(t.back(2))
                summing(t)
                if not t.known_below(1):
                    norming(t.back())
                if not t.known_below(4):
                    copy_a(t.back(4))

            v.memset(eps[:], 1e-5).then_inc(setup, 1)
            v.wait_ge(weights_in, 16 * WEIGHTS)
            for side in range(2):
                for a in range(2):
                    v.tensor_tensor(prod[:, side, a], w1[:, a, 0:D], att[:, side], ALU.mult).then_inc(setup, 1)
            v.wait_ge(setup, 5)
            for side in range(2):
                at = D + side * HEADS
                v.tensor_reduce(w1[:, :, at:at + HEADS], prod[:, side].rearrange("p a (h c) -> p a h c", h=HEADS), AX, ALU.add).then_inc(setup, 1)
            v.wait_ge(setup, 7)
            v.sem_inc(consts_ready, 1)
            end = steps(v, ROWS, 2, step, peel=4)
            ending(end.back(2))
            norming(end.back())
            ending(end.back())
            for back in (4, 3, 2, 1):
                copy_a(end.back(back))
            v.wait_ge(a_copied, ROWS)
            v.tensor_tensor(sum_a[:], k.logit[:], k.adst[:], ALU.add).then_inc(setup, 1)
            v.wait_ge(setup, 8)
            v.tensor_scalar(leak[:], sum_a[:], 0.2, None, ALU.mult).then_inc(setup, 1)
            v.wait_ge(setup, 9)
            v.tensor_tensor(k.logit[:], leak[:], sum_a[:], ALU.max).then_inc(setup, 1)

        @block.scalar
        def _(act):
            def layer1(t):
                b = t.slot(2)
                act.wait_ge(x1_turned, t.n + 1)
                if not t.known_below(2):
                    act.wait_ge(projected, t.n - 1)
                act.copy(x1_t[:, b], p_t1[:, 0:D]).then_inc(x1_t_ready, 1)
                act.wait_ge(projected, t.n + 1)
                if not t.known_below(2):
                    act.wait_ge(row1_out[b], 16 * (1 + TPB) * t.use(2))
                    act.wait_ge(spread_ready, t.n - 1)
                act.copy(both_a[:, b], p_1[:, D:C1])
                act.copy(row1[:, b, D:V1].rearrange("p (h d) -> p h d", h=HEADS),
                         p_1[:, D:D + HEADS].unsqueeze(2).broadcast_to((P, HEADS, TN)))
                act.copy(row1[:, b, 0:D], p_1[:, 0:D]).then_inc(row1_ready, 1)

            def step(t):
                b = t.slot(2)
                act.wait_ge(agg_turned, t.n + 1)
                if not t.known_below(2):
                    act.wait_ge(out_done, t.n - 1)
                act.copy(agg_t[:, b], p_t[:, b, 0:D]).then_inc(agg_t_ready, 1)
                if not t.known_below(1):
                    root(t.back(), 0)
                if not t.known_below(2):
                    root(t.back(2), 1)
                    layer1(t.back(2))

            def root(t, which):
                b = t.slot(2)
                act.wait_ge((moments1, moments2)[which], t.n + 1)
                act.activation(std[:, b, which:which + 1], moments[:, b, which, 1:2], ACT.Sqrt, bias=eps[:, 0:1]).then_inc((std1, std2)[which], 1)

            act.wait_ge(consts_ready, 1)
            end = steps(act, ROWS, 2, step, peel=4)
            root(end.back(), 0)
            root(end.back(2), 1)
            layer1(end.back(2))
            root(end.back(), 1)
            layer1(end.back())


def finish(k):
    nc = k.nc
    with Stage(nc, "fin") as z:
        bias = z.sb("bias", [P, D])
        eps = z.sb("eps", [P, 1])
        power = z.sb("power", [P, 1])
        agg = z.sb("agg", [P, 2, D])
        x1 = z.sb("x1", [P, 2, D])
        h = z.sb("h", [P, 2, D])
        low = z.sb("low", [P, 2, D])
        grown = z.sb("grown", [P, 2, D])
        kept = z.sb("kept", [P, 2, D])
        y = z.sb("y", [P, 2, D])
        stats = z.sb("stats", [P, 6])
        moments = z.sb("moments", [P, 2, 2])
        var = z.sb("var", [P, 2])
        rstd = z.sb("rstd", [P, 2])
        res = z.sb("res", [P, 2, D])
        bias_in, setup = z.sem("bias_in"), z.sem("setup")
        in_, out_ = z.sems("in", 2), z.sems("out", 2)
        h_ready, low_ready, grown_ready, kept_ready, y_ready, moments_ready, var_ready, rstd_ready, res_ready, order, settled, settled2 = (
            z.sem(n) for n in ("h_ready", "low_ready", "grown_ready", "kept_ready", "y_ready", "moments_ready",
                               "var_ready", "rstd_ready", "res_ready", "order", "settled", "settled2"))
        block = z.block()
        U = 2

        @block.sync
        def _(sp):
            sp.dma_start(bias[:], row(k, "L1_gnn_bias")).then_inc(bias_in, 16)

            def store(t):
                b = t.slot(2)
                sp.wait_ge(res_ready, t.n + 1)
                sp.dma_start(k.out[bass.ds(t.n * P, P), :], res[:, b]).then_inc(out_[b], 16)

            def step(t):
                b = t.slot(2)
                if not t.known_below(2):
                    sp.wait_ge(h_ready, t.n - 1)
                    sp.wait_ge(kept_ready, t.n - 1)
                sp.dma_start(x1[:, b], k.x1[bass.ds(t.n * P, P), :]).then_inc(in_[b], 16)
                for j in range(TPB):
                    sp.dma_start(agg[TN * j:TN * j + TN, b].rearrange("d (h c) -> d h c", h=HEADS),
                                 k.agg[bass.ds(t.n * TPB + j, 1)].rearrange("t h d c -> (t d) h c")).then_inc(in_[b], 16)
                if not t.known_below(3):
                    store(t.back(3))

            end = steps(sp, ROWS, U, step, peel=4)
            for back in (3, 2, 1):
                store(end.back(back))
            for b in range(2):
                sp.wait_ge(out_[b], 16 * (ROWS // 2))

        @block.gpsimd
        def _(pool):
            def biased(t):
                b = t.slot(2)
                pool.wait_ge(in_[b], 16 * (1 + TPB) * (t.use(2) + 1))
                if not t.known_below(2):
                    pool.wait_ge(kept_ready, t.n - 1)
                    pool.wait_ge(grown_ready, t.n - 1)
                    pool.sem_inc(settled, 1)
                pool.tensor_tensor(h[:, b], agg[:, b], bias[:], ALU.add).then_inc(h_ready, 1)
                pool.wait_ge(h_ready, t.n + 1)
                pool.sem_inc(settled, 1)
                pool.tensor_scalar(low[:, b], h[:, b], 0.0, None, ALU.min).then_inc(low_ready, 1)

            def root(t):
                b = t.slot(2)
                pool.wait_ge(moments_ready, t.n + 1)
                pool.sem_inc(settled, 1)
                pool.tensor_tensor(var[:, b:b + 1], moments[:, b, 1:2], eps[:, 0:1], ALU.add).then_inc(var_ready, 1)
                pool.wait_ge(var_ready, t.n + 1)
                pool.sem_inc(settled, 1)
                pool.tensor_tensor(rstd[:, b:b + 1], var[:, b:b + 1], power[:, 0:1], ALU.pow).then_inc(rstd_ready, 1)

            def step(t):
                biased(t)
                if not t.known_below(2):
                    root(t.back(2))

            pool.wait_ge(setup, 2)
            pool.wait_ge(bias_in, 16)
            end = steps(pool, ROWS, U, step, peel=4)
            root(end.back(2))
            root(end.back())

        @block.vector
        def _(v):
            then = Chain(v, order, 1)

            def keep(t):
                b = t.slot(2)
                v.wait_ge(h_ready, t.n + 1)
                if not t.known_below(2):
                    v.wait_ge(y_ready, t.n - 1)
                v.scalar_tensor_tensor(kept[:, b], h[:, b], 0.0, x1[:, b], ALU.max, ALU.add).then_inc(kept_ready, 1)

            def join(t):
                b = t.slot(2)
                then.begin(t)
                v.wait_ge(kept_ready, t.n + 1)
                v.wait_ge(grown_ready, t.n + 1)
                if not t.known_below(2):
                    v.wait_ge(res_ready, t.n - 1)
                v.scalar_tensor_tensor(y[:, b], grown[:, b], -1.0, kept[:, b], ALU.add, ALU.add).then_inc(y_ready, 1)
                v.wait_ge(y_ready, t.n + 1)
                then(v.bn_stats(stats[:], y[:, b]))
                v.sem_inc(settled2, 1)
                v.bn_aggr(moments[:, b], stats[:]).then_inc(moments_ready, 1)

            def end_norm(t):
                b = t.slot(2)
                v.wait_ge(rstd_ready, t.n + 1)
                if not t.known_below(2):
                    v.wait_ge(out_[b], 16 * t.use(2))
                v.tensor_scalar(res[:, b], y[:, b], moments[:, b, 0:1], rstd[:, b:b + 1], ALU.subtract, ALU.mult).then_inc(res_ready, 1)

            def step(t):
                keep(t)
                if not t.known_below(3):
                    end_norm(t.back(3))
                if not t.known_below(1):
                    join(t.back())

            v.memset(eps[:], 1e-5).then_inc(setup, 1)
            v.memset(power[:], -0.5).then_inc(setup, 1)
            end = steps(v, ROWS, U, step, peel=4)
            end_norm(end.back(3))
            join(end.back())
            end_norm(end.back(2))
            end_norm(end.back())

        @block.scalar
        def _(act):
            def step(t):
                b = t.slot(2)
                act.wait_ge(low_ready, t.n + 1)
                if not t.known_below(2):
                    act.wait_ge(y_ready, t.n - 1)
                act.activation(grown[:, b], low[:, b], ACT.Exp).then_inc(grown_ready, 1)

            steps(act, ROWS, U, step)


def kernel(**inputs):
    import numpy as _np
    import concourse.bacc as _bacc
    from concourse import mybir as _mybir
    from concourse.bass_utils import run_bass_kernel_spmd as _run

    nc = _bacc.Bacc("TRN2", target_bir_lowering=False, num_devices=1)
    given = {name: _np.ascontiguousarray(a) for name, a in inputs.items()}
    x = given.pop("x")
    src, dst, rel = (given.pop(name) for name in ("src", "dst", "edge_type_64"))
    given["x"] = _np.concatenate([x, _np.zeros((NP - N, D), x.dtype)])
    pad = lambda a, value: _np.concatenate([a, _np.full((EP - E,), value, a.dtype)])
    given["edges"] = _np.stack([pad(src, 0), pad(dst, PAD_DST), pad(rel, 0)])
    given["edge_rows"] = _np.ascontiguousarray(given["edges"].T)
    given["consts"] = constants()
    aps = {name: nc.dram_tensor(f"in_{name}", a.shape, _mybir.dt.from_np(a.dtype), kind="ExternalInput").ap()
           for name, a in given.items()}
    out = nc.dram_tensor("out_dram", (NP, D), _mybir.dt.float32, kind="ExternalOutput").ap()
    gat_kernel(nc, aps, out)
    r = _run(nc, [{f"in_{name}": a for name, a in given.items()}], core_ids=[0])
    return r.results[0]["out_dram"][0:N]
```

```python
from contextlib import ExitStack

import numpy as np
import concourse.bass as bass
from concourse import mybir

F32 = mybir.dt.float32
BF16 = mybir.dt.bfloat16
I32 = mybir.dt.int32
ALU = mybir.AluOpType
ACT = mybir.ActivationFunctionType
AX = mybir.AxisListType.X

P = 128
N = 12500
E = 200000
D = 256
HEADS = 4
HC = 64
REL = 64
TN = 32
ROWS = -(-N // P)
NP = ROWS * P
TILES = NP // TN
TPB = P // TN
PAIRS = TILES // 2
CH = 4
MAIN = CH * P
LEFT = P
SLOTS = MAIN + LEFT
SAMPLE = 512
NS = -(-(E + SLOTS) // SAMPLE)
EP = NS * SAMPLE
GT = TILES // TPB
MAXPASS = -(-E // MAIN)
UNROLL = 8
BLOCKS = 4
AHEAD = 4
BIG = float(2.0 ** 100)
NOEDGE = -float(2.0 ** 90)
C1 = D + 2 * HEADS
V1 = D + P
PAD_DST = 1 << 20

C_ID, C_DIAG, C_THR, C_CMP, C_NEG, C_TAU, C_GRP, C_SLOT = 0, 128, 160, 164, 166, 294, 298, 302
C_PASS = C_SLOT + LEFT
C_CMP1 = C_PASS + MAXPASS
C_NEG1 = C_CMP1 + 2
C_N = C_NEG1 + P


def constants():
    c = np.zeros((P, C_N), np.float32)
    p = np.arange(P)
    c[:, C_ID:C_ID + P] = np.eye(P)
    c[:, C_DIAG:C_DIAG + TN] = p[:, None] % TN == np.arange(TN)
    c[:GT, C_THR:C_THR + TPB] = TN * (GT * np.arange(TPB)[None, :] + np.arange(GT)[:, None])
    c[:REL, C_CMP] = np.arange(REL)
    c[REL:REL + TN, C_CMP] = np.arange(TN)
    c[REL:REL + TN, C_CMP + 1] = 1.0
    c[REL:REL + TN, C_NEG:C_NEG + P] = -BIG * (np.arange(TN)[:, None] == p[None, :] % TN)
    c[:, C_TAU:C_TAU + TPB] = p[:, None] // TN == np.arange(TPB)
    c[:, C_GRP:C_GRP + TPB] = P * p[:, None] + TN * np.arange(TPB)
    c[:, C_SLOT:C_SLOT + LEFT] = np.arange(LEFT)
    c[:, C_PASS:C_PASS + MAXPASS] = MAIN * np.arange(MAXPASS)
    c[:TN, C_CMP1:C_CMP1 + 2] = c[REL:REL + TN, C_CMP:C_CMP + 2]
    c[:TN, C_NEG1:C_NEG1 + P] = c[REL:REL + TN, C_NEG:C_NEG + P]
    return c


class Step:

    def __init__(self, q, c, unroll):
        self.q, self.c, self.unroll = q, c, unroll

    @property
    def n(self):
        return self.q * self.unroll + self.c

    def known_below(self, k):
        return isinstance(self.q, int) and self.n < k

    def slot(self, depth):
        return self.c % depth

    def use(self, depth):
        return self.q * (self.unroll // depth) + self.c // depth

    def back(self, k=1):
        return Step(self.q, self.c - k, self.unroll)


def steps(eng, count, unroll, body, peel=None):
    peel, odd = peel or unroll, count % unroll
    assert peel % unroll == 0
    for c in range(odd + peel):
        body(Step(0, c, unroll))
    with eng.Fori(peel // unroll, count // unroll) as q:
        for c in range(odd, odd + unroll):
            body(Step(q, c, unroll))
    return Step(0, count, unroll)


def blocks_of(slot):
    return -(-(ROWS - slot) // AHEAD)


def in_turn(eng, *parts, count=ROWS, unroll=BLOCKS):
    deepest = max(lag for lag, _ in parts)
    ahead = deepest + AHEAD - count % unroll

    def step(t):
        for lag, part in parts:
            if not t.known_below(lag):
                part(t.back(lag))

    end = steps(eng, count, unroll, step, peel=-(-ahead // unroll) * unroll)
    for past in range(deepest):
        for lag, part in parts:
            if past < lag:
                part(end.back(lag - past))


class Chain:

    def __init__(self, eng, sem, per_step=0):
        self.eng, self.sem, self.per_step = eng, sem, per_step
        self.base, self.count = 0, 0

    def begin(self, step):
        assert self.count in (0, self.per_step), (self.count, self.per_step)
        self.base, self.count = step.n * self.per_step, 0

    def __call__(self, instruction):
        self.count += 1
        instruction.then_inc(self.sem, 1)
        self.eng.wait_ge(self.sem, self.base + self.count)


class Stage:

    def __init__(self, nc, tag):
        self.nc, self.tag, self.held = nc, tag, []

    def __enter__(self):
        self.ctx = ExitStack().__enter__()
        return self

    def __exit__(self, *failure):
        self.ctx.__exit__(*failure)
        if failure[0] is None and self.held:
            self.nc.clear_and_free_semaphores(self.held)
            self.nc.all_engine_barrier()

    def sb(self, name, shape, dt=F32):
        return self.ctx.enter_context(self.nc.sbuf_tensor(f"{self.tag}_{name}", shape, dt))

    def ps(self, name, shape):
        return self.ctx.enter_context(self.nc.psum_tensor(f"{self.tag}_{name}", shape, F32))

    def sem(self, name):
        self.held.append(self.nc.alloc_semaphore(f"{self.tag}_{name}"))
        return self.held[-1]

    def sems(self, name, count):
        return [self.sem(f"{name}{k}") for k in range(count)]

    def block(self):
        return self.ctx.enter_context(self.nc.Block())


class Kernel:

    def __init__(self, nc, ctx, inputs, out):
        self.nc, self.i, self.out = nc, inputs, out
        g = ctx.enter_context(Stage(nc, "all"))
        self.cst = g.sb("cst", [P, C_N])
        self.idx = g.sb("idx", [P, TILES, CH], I32)
        self.left_idx = g.sb("left_idx", [P, PAIRS], I32)
        self.left = g.sb("left", [P, PAIRS, 3], I32)
        self.left_at = g.sb("left_at", [P, PAIRS], I32)
        self.starts_row = g.sb("starts_row", [1, TILES], I32)
        self.logit = g.sb("logit", [P, TILES])
        self.low = g.sb("low", [P, TILES])
        self.total = g.sb("total", [P, TILES])
        self.adst = g.sb("adst", [P, TILES])
        self.start0 = g.sb("start0", [P, TPB])
        self.start = g.sb("start", [P, TPB])
        self.start_i = g.sb("start_i", [P, TPB], I32)
        self.npass = g.sb("npass", [P, 1], I32)
        dram = lambda name, shape, dt=F32: nc.dram_tensor(name, shape, dt).ap()
        self.starts = dram("starts", (TILES + TPB,), I32)
        self.windows = dram("windows", (TILES, 3, MAIN), I32)
        self.match = dram("match", (TILES, 2, SLOTS), BF16)
        self.relq = dram("relq", (ROWS, REL, TPB, 3, P), BF16)
        self.qt = dram("qt", (ROWS, P, 2, P))
        self.kv = dram("kv", (NP, 2 * D))
        self.xp = dram("xp", (NP, V1))
        self.agg = dram("agg", (NP, D))
        self.x1 = dram("x1", (NP, D))
        self.ident = self.cst[:, C_ID:C_ID + P]


def gat_kernel(nc, inputs, out):
    with ExitStack() as ctx:
        k = Kernel(nc, ctx, inputs, out)
        find_windows(k)
        project_qkv(k)
        prepare_windows(k, "pw", shared=True)
        all_passes(k, 0)
        between_layers(k)
        all_passes(k, 1)
        finish(k)


def all_passes(k, layer):
    nc = k.nc
    attention(k, layer, f"att{layer}")
    many = nc.values_load(k.npass[0:1, 0:1], min_val=1, max_val=MAXPASS)
    with nc.If(many > 1):
        with nc.Fori(1, many):
            set_windows(k, f"next{layer}", first=False)
            prepare_windows(k, f"pwn{layer}")
            attention(k, layer, f"attn{layer}")
        set_windows(k, f"first{layer}", first=True)
        prepare_windows(k, f"pwf{layer}")


def find_windows(k):
    nc, cst = k.nc, k.cst
    with Stage(nc, "fw") as z:
        sample_i = z.sb("sample_i", [1, NS], I32)
        sample = z.sb("sample", [1, NS])
        ones = z.sb("ones", [1, P])
        less = z.sb("less", [P, SAMPLE])
        before = z.sb("before", [P, 2, TPB])
        row_f = z.sb("row_f", [P, TPB])
        row_i = z.sb("row_i", [P, TPB], I32)
        rows = z.sb("rows", [P, TPB, SAMPLE], I32)
        ends = z.sb("ends", [1, TPB], I32)
        first_i = z.sb("first_i", [P, TPB + 1], I32)
        first = z.sb("first", [P, TPB + 1])
        size = z.sb("size", [P, TPB])
        rest = z.sb("rest", [P, TPB])
        offset = z.sb("offset", [P, TPB])
        base = z.sb("base", [P, TPB])
        extreme = z.sb("extreme", [P, 2])
        most = z.sb("most", [P, 2])
        full = z.sb("full", [P, 1])
        more = z.sb("more", [P, MAXPASS - 1])
        passes_f = z.sb("passes_f", [P, 1])
        both = z.sb("both", [P, 2])
        at = z.sb("at", [P, 2, LEFT])
        behind = z.sb("behind", [P, LEFT])
        step = z.sb("step", [P, 1])
        spread = z.ps("spread", [P, 512])
        consts_in, sample_in, rows_in, starts_out, starts_in = (
            z.sem(x) for x in ("consts_in", "sample_in", "rows_in", "starts_out", "starts_in"))
        sample_ready, spread_ready, rows_known, starts_ready, order, extreme_ready, most_ready, at_ready, at_turned = (
            z.sem(x) for x in ("sample_ready", "spread_ready", "rows_known", "starts_ready", "order",
                               "extreme_ready", "most_ready", "at_ready", "at_turned"))
        dst = k.i["edges"][1:2, :]
        block = z.block()

        @block.sync
        def _(sp):
            sp.dma_start(cst[:], k.i["consts"]).then_inc(consts_in, 16)
            with nc.allow_non_contiguous_dma(reason="one destination in SAMPLE, once"):
                sp.dma_start(sample_i[:], dst.rearrange("o (n s) -> o n s", s=SAMPLE)[:, :, 0]).then_inc(sample_in, 16)
            sp.wait_ge(starts_ready, 1)
            with nc.allow_non_contiguous_dma(reason="a few hundred numbers, once"):
                sp.dma_start(k.starts[0:TILES].rearrange("(g p) -> p g", p=GT), k.start_i[0:GT, :]).then_inc(starts_out, 16)
                sp.dma_start(k.starts[TILES:].rearrange("(o n) -> o n", o=1), ends[:]).then_inc(starts_out, 16)
            sp.wait_ge(starts_out, 32)
            sp.dma_start(k.starts_row[:], k.starts[0:TILES].rearrange("(o n) -> o n", o=1)).then_inc(starts_in, 16)
            with nc.allow_non_contiguous_dma(reason="a few hundred numbers, once"):
                sp.dma_start(first_i[0:ROWS, 0:TPB], k.starts[0:TILES].rearrange("(g j) -> g j", j=TPB)).then_inc(starts_in, 16)
                sp.dma_start(first_i[0:ROWS, TPB:TPB + 1], k.starts[TPB:].rearrange("(g j) -> g j", j=TPB)[:, 0:1]).then_inc(starts_in, 16)

        @block.tensor
        def _(pe):
            pe.wait_ge(sample_ready, 1)
            pe.matmul(spread[0:GT, 0:NS], ones[0:1, 0:GT], sample[0:1, :], start=True, stop=True).then_inc(spread_ready, 1)
            pe.wait_ge(at_ready, 1)
            for u in range(2):
                last = pe.transpose(spread[:, u * P:u * P + ROWS], at[0:ROWS, u], k.ident[0:ROWS, 0:ROWS])
            last.then_inc(at_turned, 1)

        @block.gpsimd
        def _(pool):
            pool.wait_ge(rows_known, 1)
            blocks = k.i["edges"].rearrange("a (n s) -> (a n) s", s=SAMPLE)
            for g in range(TPB):
                pool.indirect_dma_start(rows[0:GT, g, :], None, blocks, bass.IndirectOffsetOnAxis(
                    ap=row_i[0:GT, g:g + 1], axis=0)).then_inc(rows_in, 16)
            pool.wait_ge(extreme_ready, 1)
            pool.partition_all_reduce(most[:], extreme[:], P, bass.bass_isa.ReduceOp.max).then_inc(most_ready, 1)

        @block.vector
        def _(v):
            then = Chain(v, order)
            then(v.memset(ones[:], 1.0))
            v.wait_ge(sample_in, 16)
            then(v.tensor_copy(sample[:], sample_i[:]))
            v.sem_inc(sample_ready, 1)
            v.wait_ge(spread_ready, 1)
            v.wait_ge(consts_in, 16)

            def count(level, g, numbers):
                first_node = cst[0:GT, C_THR + g:C_THR + g + 1]
                small = less[0:GT, 0:numbers.shape[-1]]
                then(v.tensor_scalar(small, numbers, first_node, None, ALU.is_lt))
                then(v.tensor_reduce(before[0:GT, level, g:g + 1], small, AX, ALU.add))

            for g in range(TPB):
                count(0, g, spread[0:GT, 0:NS])
            then(v.tensor_scalar(row_f[0:GT, :], before[0:GT, 0, :], -1.0, 0.0, ALU.add, ALU.max))
            then(v.tensor_scalar(row_i[0:GT, :], row_f[0:GT, :], float(NS), None, ALU.add))
            v.sem_inc(rows_known, 1)
            v.wait_ge(rows_in, 16 * TPB)
            for g in range(TPB):
                count(1, g, rows[0:GT, g, :])
            then(v.tensor_scalar(row_f[0:GT, :], row_f[0:GT, :], float(SAMPLE), None, ALU.mult))
            then(v.tensor_tensor(k.start0[0:GT, :], row_f[0:GT, :], before[0:GT, 1, :], ALU.add))
            then(v.tensor_copy(k.start[0:GT, :], k.start0[0:GT, :]))
            then(v.tensor_copy(k.start_i[0:GT, :], k.start0[0:GT, :]))
            then(v.memset(ends[:], E))
            v.sem_inc(starts_ready, 1)
            v.wait_ge(starts_in, 16 * 3)
            g = slice(0, ROWS)
            then(v.memset(extreme[:], 0.0))
            then(v.tensor_copy(first[g], first_i[g]))
            then(v.tensor_tensor(size[g], first[g, 1:TPB + 1], first[g, 0:TPB], ALU.subtract))
            then(v.tensor_scalar(rest[g], size[g], -float(MAIN), 0.0, ALU.add, ALU.max))
            then(v.memset(offset[:], 0.0))
            for j in (1, 3):
                then(v.tensor_copy(offset[g, j:j + 1], rest[g, j - 1:j]))
            then(v.tensor_reduce(both[g], rest[g].rearrange("p (u j) -> p u j", j=2), AX, ALU.add))
            then(v.tensor_reduce(extreme[g, 0:1], both[g], AX, ALU.max))
            then(v.tensor_reduce(extreme[g, 1:2], size[g], AX, ALU.max))
            v.sem_inc(extreme_ready, 1)
            v.wait_ge(most_ready, 1)
            then(v.tensor_scalar(full[:], most[:, 0:1], float(LEFT), None, ALU.is_gt))
            then(v.tensor_scalar(more[:], cst[:, C_PASS + 1:C_PASS + MAXPASS], most[:, 1:2], full[:, 0:1], ALU.is_lt, ALU.mult))
            then(v.tensor_reduce(passes_f[:], more[:], AX, ALU.add))
            then(v.tensor_scalar(k.npass[:], passes_f[:], 1.0, None, ALU.add))
            then(v.tensor_scalar(full[:], full[:], float(EP), None, ALU.mult))
            then(v.tensor_tensor(base[g], first[g, 0:TPB], offset[g], ALU.subtract))
            for u in range(2):
                j = 2 * u + 1
                slots = cst[g, C_SLOT:C_SLOT + LEFT]
                then(v.tensor_tensor(step[g], base[g, j:j + 1], base[g, j - 1:j], ALU.subtract))
                then(v.tensor_scalar(behind[g], slots, offset[g, j:j + 1], step[g, 0:1], ALU.is_ge, ALU.mult))
                then(v.tensor_scalar(at[g, u], slots, base[g, j - 1:j], float(MAIN), ALU.add, ALU.add))
                then(v.tensor_tensor(at[g, u], at[g, u], behind[g], ALU.add))
                then(v.tensor_scalar(at[g, u], at[g, u], full[g, 0:1], float(EP - 1), ALU.add, ALU.min))
            v.sem_inc(at_ready, 1)
            v.wait_ge(at_turned, 1)
            then(v.tensor_copy(k.left_at[:].rearrange("p (g u) -> p u g", u=2),
                               spread[:, 0:2 * P].rearrange("p (u g) -> p u g", u=2)[:, :, 0:ROWS]))


def set_windows(k, tag, first):
    nc = k.nc
    with Stage(nc, tag) as z:
        starts_ready, starts_out, log_ready, order = (z.sem(x) for x in ("starts_ready", "starts_out", "log_ready", "order"))
        log = z.sb("log", [P, TILES])
        block = z.block()

        @block.vector
        def _(v):
            then = Chain(v, order)
            if first:
                then(v.tensor_copy(k.start[0:GT, :], k.start0[0:GT, :]))
            else:
                then(v.tensor_scalar(k.start[0:GT, :], k.start[0:GT, :], float(MAIN), float(E), ALU.add, ALU.min))
            then(v.tensor_copy(k.start_i[0:GT, :], k.start[0:GT, :]))
            v.sem_inc(starts_ready, 1)
            if not first:
                v.wait_ge(log_ready, 1)
                then(v.tensor_tensor(k.logit[:], log[:], k.low[:], ALU.subtract))

        @block.scalar
        def _(act):
            if not first:
                act.activation(log[:], k.total[:], ACT.Ln).then_inc(log_ready, 1)

        @block.sync
        def _(sp):
            sp.wait_ge(starts_ready, 1)
            with nc.allow_non_contiguous_dma(reason="a few hundred numbers, once"):
                sp.dma_start(k.starts[0:TILES].rearrange("(g p) -> p g", p=GT), k.start_i[0:GT, :]).then_inc(starts_out, 16)
            sp.wait_ge(starts_out, 16)
            sp.dma_start(k.starts_row[:], k.starts[0:TILES].rearrange("(o n) -> o n", o=1)).then_inc(starts_out, 16)
            sp.wait_ge(starts_out, 32)

    with Stage(nc, tag + "c") as z:
        copied = z.sem("copied")
        block = z.block()

        @block.sync
        def _(sp):
            places = [sp.alloc_register(f"{tag}_place{j}") for j in range(TPB)]
            with sp.Fori(0, ROWS) as q:
                copy_windows_of(k, sp, q * TPB, places, copied)
            sp.wait_ge(copied, 16 * TILES)


def copy_windows_of(k, eng, tile, places, copied):
    eng.load(places, k.starts_row[:, bass.ds(tile, len(places))])
    for j, place in enumerate(places):
        first = eng.snap(place, min_val=0, max_val=E)
        eng.dma_start(k.windows[bass.ds(tile + j, 1)].rearrange("t a w -> (t a) w"),
                      k.i["edges"][:, bass.ds(first, MAIN)]).then_inc(copied, 16)


def prepare_windows(k, tag, shared=False):
    nc, cst = k.nc, k.cst
    with Stage(nc, tag) as z:
        win = z.sb("win", [P, 2, 3, MAIN], I32)
        src = z.sb("src", [P, 2, MAIN])
        node = z.sb("node", [P, 2, MAIN])
        row = z.sb("row", [P, 2, 2, MAIN], BF16)
        turned = z.ps("turned", [P, 2, 512])
        win_in, row_out = z.sems("win_in", 2), z.sems("row_out", 2)
        src_ready, row_ready, turned_ready, idx_ready, order = (
            z.sem(x) for x in ("src_ready", "row_ready", "turned_ready", "idx_ready", "order"))
        if shared:
            left_f = z.sb("left_f", [P, 2, 2, ROWS])
            left_rel = z.sb("left_rel", [P, 2, LEFT], BF16)
            left_row = z.sb("left_row", [P, TPB, LEFT], BF16)
            left_node = z.sb("left_node", [P, TPB, LEFT])
            left_t = z.ps("left_t", [P, 2, 2, LEFT])
            left_ready, left_turned, left_row_ready, left_out = (
                z.sem(x) for x in ("left_ready", "left_turned", "left_row_ready", "left_out"))
        block = z.block()

        @block.sync
        def _(sp):
            if shared:
                sp.wait_ge(left_row_ready, 1)
                to = k.match.rearrange("(g j) a w -> g j a w", j=TPB)
                for j in range(TPB):
                    sp.dma_start(to[:, j, 0, MAIN:SLOTS], left_rel[0:ROWS, j // 2]).then_inc(left_out, 16)
                    sp.dma_start(to[:, j, 1, MAIN:SLOTS], left_row[0:ROWS, j]).then_inc(left_out, 16)
            for g in range(TPB):
                if g >= 2:
                    sp.wait_ge(row_ready, g - 1)
                    sp.wait_ge(src_ready, g - 1)
                sp.dma_start(win[0:GT, g % 2], k.windows[GT * g:GT * g + GT]).then_inc(win_in[g % 2], 16)
            for g in range(TPB):
                sp.wait_ge(row_ready, g + 1)
                sp.dma_start(k.match[GT * g:GT * g + GT, :, 0:MAIN], row[0:GT, g % 2]).then_inc(row_out[g % 2], 16)
            for half in range(2):
                sp.wait_ge(row_out[half], 16 * (TPB // 2))
            if shared:
                sp.wait_ge(left_out, 16 * 2 * TPB)

        @block.tensor
        def _(pe):
            if shared:
                pe.wait_ge(left_ready, 1)
                for a in range(2):
                    for u in range(2):
                        last = pe.transpose(left_t[0:ROWS, a, u], left_f[:, a, u], k.ident)
                last.then_inc(left_turned, 1)
            for g in range(TPB):
                pe.wait_ge(src_ready, g + 1)
                if g >= 2:
                    pe.wait_ge(idx_ready, g - 1)
                for j in range(CH):
                    last = pe.transpose(turned[:, g % 2, j * P:j * P + GT], src[0:GT, g % 2, j * P:j * P + P],
                                        k.ident[0:GT, 0:GT])
                last.then_inc(turned_ready, 1)

        @block.vector
        def _(v):
            then = Chain(v, order)
            if shared:
                g = slice(0, ROWS)
                for a in range(2):
                    then(v.tensor_copy(left_f[:, a], k.left[:, :, 1 + a].rearrange("p (g u) -> p u g", u=2)))
                v.sem_inc(left_ready, 1)
                then(v.tensor_copy(k.left_idx[:], k.left[:, :, 0]))
                v.wait_ge(left_turned, 1)
                then(v.tensor_copy(left_rel[g], left_t[g, 1]))
                for j in range(TPB):
                    then(v.tensor_scalar(left_node[g, j], left_t[g, 0, j // 2], cst[g, C_GRP + j:C_GRP + j + 1], float(TN), ALU.subtract, ALU.min))
                    then(v.tensor_scalar(left_row[g, j], left_node[g, j], -1.0, None, ALU.max))
                v.sem_inc(left_row_ready, 1)
            for g in range(TPB):
                v.wait_ge(win_in[g % 2], 16 * (g // 2 + 1))
                if g >= 2:
                    v.wait_ge(turned_ready, g - 1)
                    v.wait_ge(row_out[g % 2], 16 * (g // 2))
                v.tensor_copy(src[0:GT, g % 2], win[0:GT, g % 2, 0]).then_inc(src_ready, 1)
                first_node = cst[0:GT, C_THR + g:C_THR + g + 1]
                then(v.tensor_scalar(node[0:GT, g % 2], win[0:GT, g % 2, 1], first_node, float(TN), ALU.subtract, ALU.min))
                then(v.tensor_scalar(row[0:GT, g % 2, 1], node[0:GT, g % 2], -1.0, None, ALU.max))
                then(v.tensor_copy(row[0:GT, g % 2, 0], win[0:GT, g % 2, 2]))
                v.sem_inc(row_ready, 1)
                v.wait_ge(turned_ready, g + 1)
                v.tensor_copy(k.idx[:, g * GT:g * GT + GT, :].rearrange("p t j -> p j t"),
                              turned[:, g % 2].rearrange("p (j t) -> p j t", j=CH)[:, :, 0:GT]).then_inc(idx_ready, 1)


def project_qkv(k):
    nc, cst = k.nc, k.cst
    scale = float(HC) ** -0.5
    LN = 14
    with Stage(nc, "qkv") as z:
        wq = z.sb("wq", [P, 2, D])
        wkv = z.sb("wkv", [P, 2, 2 * D])
        bq = z.sb("bq", [P, 2])
        bkv = z.sb("bkv", [P, 2 * D])
        query = z.sb("query", [P, D])
        x = z.sb("x", [P, AHEAD, D])
        enh = z.sb("enh", [P, 2, D])
        enh_t = z.sb("enh_t", [P, 2, D])
        kv = z.sb("kv", [P, AHEAD, 2 * D])
        q_now = z.sb("q_now", [P, AHEAD, 2, P])
        p_t = z.ps("p_t", [P, 2, 512])
        p_q = z.ps("p_q", [P, 2, 512])
        p_kv = z.ps("p_kv", [P, 2, 512])
        p_rq = z.ps("p_rq", [P, 512])
        p_rel = z.ps("p_rel", [P, 512])
        rel2 = z.sb("rel2", [REL, P])
        rel = z.sb("rel", [P, 2, REL])
        rq = z.sb("rq", [REL, AHEAD, TPB, 3, HEADS, TN], BF16)
        rest = z.sb("rest", [REL, 2, TPB, HEADS, TN])
        left_now = z.sb("left_now", [P, LN], I32)
        left_got = z.sb("left_got", [P, LN, 3], I32)
        rq_out, qt_out = z.sems("rq_out", AHEAD), z.sems("qt_out", AHEAD)
        rel_turned, rel_ready, rq_done, rq_hi, rq_rest, rq_mid, rq_ready, copied, copied2, left_now_ready, left_in, left_ready, settled = (
            z.sem(n) for n in ("rel_turned", "rel_ready", "rq_done", "rq_hi", "rq_rest", "rq_mid", "rq_ready", "copied", "copied2",
                               "left_now_ready", "left_in", "left_ready", "settled"))
        weights_in, x_in, kv_out = z.sem("weights_in"), z.sems("x_in", AHEAD), z.sems("kv_out", AHEAD)
        small_ready, enh_ready, turned, enh_t_ready, q_done, kv_done, q_copied, kv_ready, zeroed = (
            z.sem(n) for n in ("small_ready", "enh_ready", "turned", "enh_t_ready", "q_done", "kv_done",
                               "q_copied", "kv_ready", "zeroed"))
        block = z.block()

        @block.sync
        def _(sp):
            for w, dst in (("Wq", wq[:]), ("Wk", wkv[:, :, 0:D]), ("Wv", wkv[:, :, D:2 * D])):
                sp.dma_start(dst, k.i["L0_gnn_" + w].rearrange("(a p) n -> p a n", p=P)).then_inc(weights_in, 16)
            row = lambda name: k.i[name].rearrange("(o n) -> o n", o=1).broadcast_to((P, D))
            sp.dma_start(bkv[:, 0:D], row("L0_gnn_bk")).then_inc(weights_in, 16)
            sp.dma_start(bkv[:, D:2 * D], row("L0_gnn_bv")).then_inc(weights_in, 16)
            sp.dma_start(query[:], row("L0_gnn_query_emb")).then_inc(weights_in, 16)
            with nc.allow_non_contiguous_dma(reason="one bias, once"):
                sp.dma_start(bq[:], k.i["L0_gnn_bq"].rearrange("(a p) -> p a", p=P)).then_inc(weights_in, 16)
            for half in range(2):
                sp.dma_start(rel2[:, half * HC:half * HC + HC], k.i["L0_gnn_rel_w"]).then_inc(weights_in, 16)

            def store(t):
                b = t.slot(AHEAD)
                sp.wait_ge(kv_ready, t.n + 1)
                sp.dma_start(k.kv[bass.ds(t.n * P, P), :], kv[:, b]).then_inc(kv_out[b], 16)
                sp.dma_start(k.agg[bass.ds(t.n * P, P), :], kv[:, b, D:2 * D]).then_inc(kv_out[b], 16)

            def load(t):
                if not t.known_below(AHEAD):
                    sp.wait_ge(enh_ready, t.n - AHEAD + 1)
                sp.dma_start(x[:, t.slot(AHEAD)], k.i["x"][bass.ds(t.n * P, P), :]).then_inc(x_in[t.slot(AHEAD)], 16)

            def copy_windows(t):
                copy_windows_of(k, sp, t.n * 2, places, copied)

            places = [sp.alloc_register(f"place{j}") for j in range(2)]
            in_turn(sp, (0, load), (4, store), (0, copy_windows))
            sp.wait_ge(copied, 16 * (TILES // 2))
            for b in range(AHEAD):
                sp.wait_ge(kv_out[b], 32 * blocks_of(b))

        @block.gpsimd
        def _(pool):
            places = [pool.alloc_register(f"pool_place{j}") for j in range(TPB)]
            with pool.Fori(TILES // 2 // TPB, TILES // TPB) as q:
                copy_windows_of(k, pool, q * TPB, places, copied2)
            pool.wait_ge(copied2, 16 * (TILES // 2))
            with pool.Fori(0, PAIRS // LN) as q:
                pool.tensor_copy(left_now[:], k.left_at[:, bass.ds(q * LN, LN)]).then_inc(left_now_ready, 1)
                pool.wait_ge(left_now_ready, q + 1)
                pool.sem_inc(settled, 1)
                for u in range(LN):
                    pool.indirect_dma_start(left_got[:, u, :], None, k.i["edge_rows"], bass.IndirectOffsetOnAxis(
                        ap=left_now[:, u:u + 1], axis=0)).then_inc(left_in, 16)
                pool.wait_ge(left_in, q * (16 * LN) + 16 * LN)
                pool.sem_inc(settled, 1)
                pool.tensor_copy(k.left[:, bass.ds(q * LN, LN), :], left_got[:]).then_inc(left_ready, 1)
                pool.wait_ge(left_ready, q + 1)
                pool.sem_inc(settled, 1)

        @block.tensor
        def _(pe):
            def turn(t):
                pe.wait_ge(enh_ready, t.n + 1)
                if not t.known_below(2):
                    pe.wait_ge(enh_t_ready, t.n - 1)
                for a in range(2):
                    last = pe.transpose(p_t[:, t.slot(2), a * P:a * P + P], enh[:, t.slot(2), a * P:a * P + P], k.ident)
                last.then_inc(turned, 1)

            def project(t):
                b = t.slot(2)
                pe.wait_ge(enh_t_ready, t.n + 1)
                if not t.known_below(2):
                    pe.wait_ge(q_copied, t.n - 1)
                    pe.wait_ge(kv_ready, t.n - 1)
                for pair in range(2):
                    for a in range(2):
                        last = pe.matmul(p_q[:, b, pair * P:pair * P + P], wq[:, a, pair * P:pair * P + P],
                                         enh_t[:, b, a * P:a * P + P], start=a == 0, stop=a == 1)
                last.then_inc(q_done, 1)
                for a in range(2):
                    last = pe.matmul(p_kv[:, b], enh_t[:, b, a * P:a * P + P], wkv[:, a], start=a == 0, stop=a == 1)
                last.then_inc(kv_done, 1)

            def relations(t):
                pe.wait_ge(q_copied, t.n + 1)
                if not t.known_below(1):
                    pe.wait_ge(rq_rest, t.n)
                for h in range(HEADS):
                    last = pe.matmul(p_rq[0:REL, h * P:h * P + P], rel[:, h % 2], q_now[:, t.slot(AHEAD), h // 2],
                                     start=True, stop=True)
                last.then_inc(rq_done, 1)

            pe.wait_ge(weights_in, 16 * 9)
            pe.transpose(p_rel[:, 0:REL], rel2[:, :], k.ident[0:REL, 0:REL]).then_inc(rel_turned, 1)
            pe.wait_ge(rel_ready, 3)
            in_turn(pe, (1, turn), (2, project), (3, relations))

        @block.vector
        def _(v):
            def enhance(t):
                b = t.slot(2)
                v.wait_ge(x_in[t.slot(AHEAD)], 16 * (t.use(AHEAD) + 1))
                if not t.known_below(2):
                    v.wait_ge(turned, t.n - 1)
                v.scalar_tensor_tensor(enh[:, b], query[:], 0.1, x[:, t.slot(AHEAD)], ALU.mult, ALU.add).then_inc(enh_ready, 1)

            def first_rest(t):
                b, o = t.slot(2), t.slot(AHEAD)
                v.wait_ge(rq_hi, t.n + 1)
                psum = p_rq[0:REL].rearrange("r (h j d) -> r j h d", h=HEADS, j=TPB)
                for j in range(TPB):
                    last = v.tensor_tensor(rest[:, b, j], psum[:, j], rq[:, o, j, 0], ALU.subtract)
                last.then_inc(rq_rest, 1)

            def second_rest(t):
                b, o = t.slot(2), t.slot(AHEAD)
                v.wait_ge(rq_mid, t.n + 1)
                for j in range(TPB):
                    last = v.tensor_tensor(rq[:, o, j, 2], rest[:, b, j], rq[:, o, j, 1], ALU.subtract)
                last.then_inc(rq_ready, 1)

            def bias(t):
                b, o = t.slot(2), t.slot(AHEAD)
                v.wait_ge(kv_done, t.n + 1)
                if not t.known_below(AHEAD):
                    v.wait_ge(kv_out[o], 32 * t.use(AHEAD))
                v.tensor_tensor(kv[:, o], p_kv[:, b], bkv[:], ALU.add).then_inc(kv_ready, 1)

            v.memset(k.logit[:], NOEDGE).then_inc(zeroed, 1)
            v.memset(rel[:], 0.0).then_inc(rel_ready, 1)
            v.wait_ge(rel_ready, 1)
            v.wait_ge(rel_turned, 1)
            for half in range(2):
                at = slice(half * HC, half * HC + HC)
                v.tensor_scalar(rel[at, half], p_rel[at, 0:REL], 0.2, None, ALU.mult).then_inc(rel_ready, 1)
            v.wait_ge(weights_in, 16 * 9)
            in_turn(v, (0, enhance), (4, first_rest), (3, bias), (4, second_rest))

        @block.scalar
        def _(act):
            def q_out(t):
                act.wait_ge(q_done, t.n + 1)
                o = t.slot(AHEAD)
                if not t.known_below(AHEAD):
                    act.wait_ge(rq_done, t.n - AHEAD + 1)
                    act.wait_ge(qt_out[o], 16 * t.use(AHEAD))
                for pair in range(2):
                    last = act.activation(q_now[:, o, pair], p_q[:, t.slot(2), pair * P:pair * P + P],
                                          ACT.Identity, bias=bq[:, pair:pair + 1], scale=scale)
                last.then_inc(q_copied, 1)

            def split(t):
                b, o = t.slot(2), t.slot(AHEAD)
                act.wait_ge(rq_done, t.n + 1)
                if not t.known_below(AHEAD):
                    act.wait_ge(rq_out[o], 16 * t.use(AHEAD))
                psum = p_rq[0:REL].rearrange("r (h j d) -> r j h d", h=HEADS, j=TPB)
                for j in range(TPB):
                    last = act.copy(rq[:, o, j, 0], psum[:, j])
                last.then_inc(rq_hi, 1)
                act.wait_ge(rq_rest, t.n + 1)
                for j in range(TPB):
                    last = act.copy(rq[:, o, j, 1], rest[:, b, j])
                last.then_inc(rq_mid, 1)

            def store_q(t):
                o = t.slot(AHEAD)
                act.wait_ge(q_copied, t.n + 1)
                act.dma_start(k.qt[bass.ds(t.n, 1)].rearrange("o p a n -> (o p) a n"), q_now[:, o]).then_inc(qt_out[o], 16)

            def store_relations(t):
                b = t.slot(AHEAD)
                act.wait_ge(rq_ready, t.n + 1)
                act.dma_start(k.relq[bass.ds(t.n, 1)].rearrange("o r j s m -> (o r) (j s m)"),
                             rq[:, b].rearrange("r j s h d -> r (j s h d)")).then_inc(rq_out[b], 16)

            def copy_turned(t):
                act.wait_ge(turned, t.n + 1)
                if not t.known_below(2):
                    act.wait_ge(kv_done, t.n - 1)
                act.copy(enh_t[:, t.slot(2)], p_t[:, t.slot(2), 0:D]).then_inc(enh_t_ready, 1)

            act.wait_ge(weights_in, 16 * 9)
            act.mul(bq[:], bq[:], scale).then_inc(small_ready, 1)
            act.wait_ge(small_ready, 1)
            in_turn(act, (1, copy_turned), (4, split), (2, q_out), (3, store_q), (5, store_relations))
            for b in range(AHEAD):
                act.wait_ge(rq_out[b], 16 * blocks_of(b))
                act.wait_ge(qt_out[b], 16 * blocks_of(b))


def attention(k, layer, tag):
    nc, cst, ident = k.nc, k.cst, k.ident
    table = k.xp if layer else k.kv
    width = V1 if layer else 2 * D
    val = 0 if layer else D
    parts = 1 if layer else 3
    krows = TN if layer else REL + TN
    cmp = C_CMP1 if layer else C_CMP
    neg = C_NEG1 if layer else C_NEG
    R = 8
    B = 2 if layer else 1
    M = 4
    KEYS = 1 if layer else 0
    LAG = 2
    with Stage(nc, tag) as z:
        rows = z.sb("rows", [P, R, CH, width])
        left = z.sb("left", [P, 4, width])
        index = z.sb("index", [P, 2, 4 * CH], I32)
        left_index = z.sb("left_index", [P, 4], I32)
        match = z.sb("match", [REL + TN, M, SLOTS], BF16)
        hit = z.sb("hit", [REL + TN, 2, SLOTS], BF16)
        lower = z.sb("lower", [REL + TN, M, parts, P], BF16)
        value = z.sb("value", [P, 8, HC])
        weight = z.sb("weight", [P, 2, SLOTS])
        weight_t = z.sb("weight_t", [P, SLOTS])
        col = z.sb("col", [P, 4, 6])
        MAXED, SUM, SELF, WHOLE, INV, RAW = range(6)
        joined = z.sb("joined", [P, HC])
        result = z.sb("result", [P, 2, HC])
        if layer:
            alpha = z.sb("alpha", [P, 2, SLOTS])
        else:
            kt = z.sb("kt", [P, 2, 2, MAIN])
            left_kt = z.sb("left_kt", [P, 2, 2, LEFT])
            q_block = z.sb("q_block", [P, 2, 2, P])
            q = z.sb("q", [P, 2, 2, P])
            p_kt = z.ps("p_kt", [P, 2, 512])
            p_left = z.ps("p_left", [P, 512])
        p_s = z.ps("p_s", [P, B, 1024])
        p_w = z.ps("p_w", [P, 1024])
        p_o = z.ps("p_o", [P, 512])
        rows_in, left_in, value_in = z.sems("rows_in", R), z.sems("left_in", 4), z.sems("value_in", 8)
        match_in, result_out = z.sems("match_in", M), z.sems("result_out", 2)
        (consts_ready, index_ready, settled, hit_ready, scores_ready, low_ready, exp_done, turned,
         weight_t_ready, agg_done, result_ready, max_ready, order, joined_ready, setup) = (z.sem(n) for n in (
            "consts_ready", "index_ready", "settled", "hit_ready", "scores_ready", "low_ready", "exp_done",
            "turned", "weight_t_ready", "agg_done", "result_ready", "max_ready", "order", "joined_ready", "setup"))
        self_done = z.sem("self_done")
        if layer:
            alpha_ready = z.sem("alpha_ready")
        else:
            q_in = z.sems("q_in", 2)
            kt_turned, left_turned, kt0_ready, kt1_ready, left_kt_ready, q_ready = (z.sem(n) for n in (
                "kt_turned", "left_turned", "kt0_ready", "kt1_ready", "left_kt_ready", "q_ready"))
        block = z.block()
        MATCHED = 16 if layer else 48

        def pair_of(t):
            return t.slot(UNROLL) // 2, t.q * (UNROLL // 2) + t.c // 2, t.q + t.c // UNROLL

        @block.gpsimd
        def _(pool):
            def gather(t):
                b, r = t.slot(4), t.slot(R)
                ls, pair, _ = pair_of(t)
                half = t.slot(UNROLL) // 4
                if not t.known_below(R):
                    pool.wait_ge(agg_done, t.n - R + (1 if R < 8 or b % 2 else 2))
                if b == 0:
                    if not t.known_below(8):
                        pool.wait_ge(scores_ready, t.n - 4)
                    pool.tensor_copy(index[:, half], k.idx[:, bass.ds(t.n, TPB), :].rearrange("p t j -> p (t j)")).then_inc(index_ready, 1)
                    pool.tensor_copy(left_index[:, 2 * half:2 * half + 2], k.left_idx[:, bass.ds(pair, 2)]).then_inc(index_ready, 1)
                    pool.wait_ge(index_ready, t.q * 4 + (t.c // 4) * 2 + 2)
                pool.sem_inc(settled, 1)
                if b % 2 == 0:
                    pool.indirect_dma_start(left[:, ls, :], None, table, bass.IndirectOffsetOnAxis(
                        ap=left_index[:, ls:ls + 1], axis=0)).then_inc(left_in[ls], 16)
                for j in range(CH):
                    at = b * CH + j
                    pool.indirect_dma_start(rows[:, r, j, :], None, table, bass.IndirectOffsetOnAxis(
                        ap=index[:, half, at:at + 1], axis=0)).then_inc(rows_in[r], 16)

            steps(pool, TILES, UNROLL, gather)

        @block.sync
        def _(sp):
            def step(t):
                b, m, w = t.slot(TPB), t.slot(M), t.slot(8)
                if not t.known_below(M):
                    sp.wait_ge(scores_ready, t.n - M + 1)
                if not layer:
                    sp.dma_start(match[0:REL, m], k.match[bass.ds(t.n, 1), 0].broadcast_to((REL, SLOTS))).then_inc(match_in[m], 16)
                    sp.dma_start(lower[0:REL, m], k.relq[bass.ds(t.q * 2 + t.c // TPB, 1), :, b].rearrange("o r s m -> (o r) s m")).then_inc(match_in[m], 16)
                sp.dma_start(match[krows - TN:krows, m], k.match[bass.ds(t.n, 1), 1].broadcast_to((TN, SLOTS))).then_inc(match_in[m], 16)
                if not layer and b == 0:
                    half = t.slot(UNROLL) // TPB
                    if not t.known_below(UNROLL):
                        sp.wait_ge(q_ready, t.n - TPB)
                    sp.dma_start(q_block[:, half], k.qt[bass.ds(t.q * 2 + t.c // TPB, 1)].rearrange("o p a n -> (o p) a n")).then_inc(q_in[half], 16)
                if not t.known_below(8):
                    sp.wait_ge(result_ready, t.n - 7)
                sp.dma_start(value[:, w], k.agg[bass.ds(t.n * TN, TN), :].rearrange("n (h c) -> h n c", h=HEADS)).then_inc(value_in[w], 16)

            steps(sp, TILES, UNROLL, step)

        @block.tensor
        def _(pe):
            def turn_keys(t):
                b = t.slot(4)
                ls, _, used = pair_of(t)
                pe.wait_ge(rows_in[t.slot(R)], t.use(R) * (16 * CH) + 16 * CH)
                if b % 2 == 0:
                    pe.wait_ge(left_in[ls], used * 16 + 16)
                if layer:
                    return
                if b % 2 == 0:
                    for pair in range(2):
                        last = pe.transpose(p_left[:, pair * P:pair * P + P], left[:, ls, pair * P:pair * P + P], ident)
                    last.then_inc(left_turned, 1)
                if not t.known_below(1):
                    pe.wait_ge(kt0_ready, t.n)
                    pe.wait_ge(kt1_ready, t.n)
                for pair in range(2):
                    for j in range(CH):
                        last = pe.transpose(p_kt[:, pair, j * P:j * P + P], rows[:, t.slot(R), j, pair * P:pair * P + P], ident)
                last.then_inc(kt_turned, 1)

            def turn_weights(t):
                pe.wait_ge(exp_done, t.n + 1)
                if not t.known_below(1):
                    pe.wait_ge(weight_t_ready, t.n)
                for j in range(CH + 1):
                    last = pe.transpose(p_w[:, j * P:j * P + P], weight[:, t.slot(2), j * P:j * P + P], ident)
                last.then_inc(turned, 1)

            def score(t):
                b, c = t.slot(4), t.slot(2)
                ls, pair_number, _ = pair_of(t)
                if B == 1 and not t.known_below(1):
                    pe.wait_ge(exp_done, t.n)
                ps = p_s[:, t.slot(B)]
                pe.wait_ge(hit_ready, t.n + 1)
                for lo, hi in ((0, MAIN), (MAIN, SLOTS)):
                    for part in range(parts):
                        pe.matmul(ps[:, lo:hi], lower[0:krows, 0 if layer else t.slot(M), part], hit[0:krows, c, lo:hi],
                                  start=part == 0, stop=False, skip_group_check=True)
                if layer:
                    for j in range(CH + 1):
                        a_src = rows[:, t.slot(R), j, D:V1] if j < CH else left[:, ls, D:V1]
                        last = pe.matmul(ps[:, j * P:j * P + P], a_src, ident, start=False, stop=j >= CH - 1, skip_group_check=True)
                else:
                    pe.wait_ge(kt0_ready, t.n + 1)
                    pe.wait_ge(kt1_ready, t.n + 1)
                    pe.wait_ge(left_kt_ready, pair_number + 1)
                    pe.wait_ge(q_ready, t.n + 1)
                    for pair in range(2):
                        pe.matmul(ps[:, 0:MAIN], q[:, c, pair], kt[:, c, pair], start=False, stop=pair == 1, skip_group_check=True)
                        last = pe.matmul(ps[:, MAIN:SLOTS], q[:, c, pair], left_kt[:, b // 2, pair], start=False, stop=pair == 1,
                                         skip_group_check=True)
                last.then_inc(scores_ready, 1)

            def aggregate(t):
                ls, _, _ = pair_of(t)
                pe.wait_ge(weight_t_ready, t.n + 1)
                if not t.known_below(1):
                    pe.wait_ge(joined_ready, t.n)
                for j in range(CH + 1):
                    v = rows[:, t.slot(R), j, val:val + D] if j < CH else left[:, ls, val:val + D]
                    for h in range(HEADS):
                        at = TN * h
                        last = pe.matmul(p_o[at:at + TN, 0:HC], weight_t[:, j * P + at:j * P + at + TN], v[:, HC * h:HC * h + HC],
                                         start=j == 0, stop=j == CH, tile_position=(0, at), skip_group_check=True)
                last.then_inc(agg_done, 1)

            pe.wait_ge(consts_ready, 1)
            in_turn(pe, (KEYS, turn_keys), (1 + LAG, turn_weights), (1, score), (1 + LAG, aggregate), count=TILES, unroll=UNROLL)

        @block.vector
        def _(v):
            then = Chain(v, order, 2)

            def sums(t):
                c = t.slot(4)
                then.begin(t)
                v.wait_ge(exp_done, t.n + 1)
                v.wait_ge(self_done, t.n + 1)
                add = lambda to: v.tensor_tensor(to, col[:, c, SUM:SUM + 1], col[:, c, SELF:SELF + 1], ALU.add)
                add(k.total[:, bass.ds(t.n, 1)])
                then(add(col[:, c, WHOLE:WHOLE + 1]))
                then(v.reciprocal(col[:, c, INV:INV + 1], col[:, c, WHOLE:WHOLE + 1]))

            def copy_weights(t):
                v.wait_ge(turned, t.n + 1)
                if not t.known_below(1):
                    v.wait_ge(agg_done, t.n)
                v.tensor_copy(weight_t[:], p_w[:, 0:SLOTS]).then_inc(weight_t_ready, 1)

            def put_result(t):
                w, c, o = t.slot(8), t.slot(4), t.slot(2)
                v.wait_ge(agg_done, t.n + 1)
                v.wait_ge(value_in[w], t.use(8) * 16 + 16)
                v.scalar_tensor_tensor(joined[:], value[:, w], col[:, c, SELF:SELF + 1], p_o[:, 0:HC], ALU.mult, ALU.add).then_inc(joined_ready, 1)
                if not t.known_below(2):
                    v.wait_ge(result_out[o], t.use(2) * 16)
                v.wait_ge(joined_ready, t.n + 1)
                v.tensor_scalar(result[:, o], joined[:], col[:, c, INV:INV + 1], None, ALU.mult).then_inc(result_ready, 1)

            def prepare(t):
                b, c, m = t.slot(TPB), t.slot(2), t.slot(M)
                v.wait_ge(match_in[m], t.use(M) * MATCHED + MATCHED)
                if not t.known_below(2):
                    v.wait_ge(scores_ready, t.n - 1)
                v.tensor_scalar(hit[0:krows, c], match[0:krows, m], cst[0:krows, cmp:cmp + 1],
                                cst[0:krows, cmp + 1:cmp + 2], ALU.is_equal, ALU.not_equal).then_inc(hit_ready, 1)
                if not layer:
                    half = t.slot(UNROLL) // TPB
                    v.wait_ge(q_in[half], t.q * 16 + (t.c // UNROLL) * 16 + 16)
                    for h in range(HEADS):
                        lo = (h % 2) * HC
                        last = v.tensor_copy(q[lo:lo + HC, c, h // 2, h * TN:h * TN + TN], q_block[lo:lo + HC, half, h // 2, b * TN:b * TN + TN])
                    last.then_inc(q_ready, 1)

            def copy_keys(t):
                if not layer:
                    b = t.slot(4)
                    _, pair, _ = pair_of(t)
                    if b % 2 == 0:
                        v.wait_ge(left_turned, pair + 1)
                        v.tensor_copy(left_kt[:, b // 2], p_left[:, 0:2 * LEFT].rearrange("p (a w) -> p a w", a=2)).then_inc(left_kt_ready, 1)
                    v.wait_ge(kt_turned, t.n + 1)
                    v.tensor_copy(kt[:, t.slot(2), 1], p_kt[:, 1]).then_inc(kt1_ready, 1)

            def lower_bound(t):
                c = t.slot(2)
                v.wait_ge(scores_ready, t.n + 1)
                m = t.slot(4)
                ps = p_s[:, t.slot(B), 0:SLOTS]
                if layer:
                    raw = col[:, m, RAW:RAW + 1]
                    v.tensor_scalar(alpha[:, c], ps, k.adst[:, bass.ds(t.n, 1)], -3.0e38, ALU.add, ALU.max,
                                    accum_out=raw).then_inc(alpha_ready, 1)
                    v.wait_ge(alpha_ready, 2 * t.n + 1)
                    v.scalar_tensor_tensor(col[:, m, MAXED:MAXED + 1], raw, 0.2, raw, ALU.mult, ALU.max).then_inc(max_ready, 1)
                    v.scalar_tensor_tensor(alpha[:, c], alpha[:, c], 0.2, alpha[:, c], ALU.mult, ALU.max).then_inc(alpha_ready, 1)
                else:
                    v.tensor_reduce(col[:, m, MAXED:MAXED + 1], ps, AX, ALU.max).then_inc(max_ready, 1)
                v.wait_ge(max_ready, t.n + 1)
                v.tensor_scalar(k.low[:, bass.ds(t.n, 1)], col[:, m, MAXED:MAXED + 1], k.logit[:, bass.ds(t.n, 1)], -1.0,
                                ALU.max, ALU.mult).then_inc(low_ready, 1)

            if layer:
                v.tensor_copy(lower[0:TN, 0, 0], cst[0:TN, neg:neg + P]).then_inc(setup, 1)
                v.wait_ge(setup, 1)
            else:
                v.memset(q[:], 0.0).then_inc(setup, 1)
                v.memset(lower[REL:REL + TN], 0.0).then_inc(setup, 1)
                v.wait_ge(setup, 2)
                for c in range(M):
                    v.tensor_copy(lower[REL:REL + TN, c, 0], cst[REL:REL + TN, neg:neg + P]).then_inc(setup, 1)
                v.wait_ge(setup, 2 + M)
            v.sem_inc(consts_ready, 1)
            in_turn(v, (KEYS, copy_keys), (1 + LAG, copy_weights), (1 + LAG, sums), (0, prepare), (1, lower_bound), (1 + LAG, put_result),
                    count=TILES, unroll=UNROLL)

        @block.scalar
        def _(act):
            def copy_keys(t):
                if not layer:
                    act.wait_ge(kt_turned, t.n + 1)
                    act.copy(kt[:, t.slot(2), 0], p_kt[:, 0]).then_inc(kt0_ready, 1)

            def weigh(t):
                c, m = t.slot(2), t.slot(4)
                if not t.known_below(2):
                    act.wait_ge(turned, t.n - 1)
                act.wait_ge(low_ready, t.n + 1)
                if layer:
                    act.wait_ge(alpha_ready, 2 * t.n + 2)
                low = k.low[:, bass.ds(t.n, 1)]
                act.activation(weight[:, c], alpha[:, c] if layer else p_s[:, 0, 0:SLOTS], ACT.Exp, bias=low,
                               accum_out=col[:, m, SUM:SUM + 1]).then_inc(exp_done, 1)
                act.activation(col[:, m, SELF:SELF + 1], k.logit[:, bass.ds(t.n, 1)], ACT.Exp, bias=low).then_inc(self_done, 1)

            def put(t):
                c = t.slot(2)
                act.wait_ge(result_ready, t.n + 1)
                act.dma_start(k.agg[bass.ds(t.n * TN, TN), :].rearrange("n (h c) -> h n c", h=HEADS), result[:, c]).then_inc(result_out[c], 16)

            in_turn(act, (KEYS, copy_keys), (1, weigh), (1 + LAG, put), count=TILES, unroll=UNROLL)
            for c in range(2):
                act.wait_ge(result_out[c], 16 * (TILES // 2))


def row(k, name, lo=0, count=D):
    return k.i[name].rearrange("(o n) -> o n", o=1).broadcast_to((P, count))


def between_layers(k):
    nc, cst, ident = k.nc, k.cst, k.ident
    with Stage(nc, "mid") as z:
        wo = z.sb("wo", [P, 2, D])
        w1 = z.sb("w1", [P, 2, C1])
        att = z.sb("att", [P, 2, D])
        prod = z.sb("prod", [P, 2, 2, D])
        bo, gamma, beta = (z.sb(n, [P, D]) for n in ("bo", "gamma", "beta"))
        eps = z.sb("eps", [P, 1])
        x = z.sb("x", [P, AHEAD, D])
        agg = z.sb("agg", [P, AHEAD, D])
        agg_t = z.sb("agg_t", [P, 2, D])
        y = z.sb("y", [P, AHEAD, D])
        x_bo = z.sb("x_bo", [P, 2, D])
        x_beta = z.sb("x_beta", [P, AHEAD, D])
        stats = z.sb("stats", [P, 2, 6])
        moments = z.sb("moments", [P, AHEAD, 2, 2])
        std = z.sb("std", [P, AHEAD, 2])
        rstd = z.sb("rstd", [P, AHEAD, 2])
        x1 = z.sb("x1", [P, AHEAD, D])
        x1_t = z.sb("x1_t", [P, 2, D])
        row1 = z.sb("row1", [P, AHEAD, V1])
        both_a = z.sb("both_a", [P, 2, 2 * HEADS])
        spread = z.sb("spread", [P, 2, 2 * HEADS, TN])
        sum_a = z.sb("sum_a", [P, TILES])
        leak = z.sb("leak", [P, TILES])
        p_t = z.ps("p_t", [P, 2, 512])
        p_o = z.ps("p_o", [P, 512])
        p_t1 = z.ps("p_t1", [P, 512])
        p_1 = z.ps("p_1", [P, 512])
        p_a = z.ps("p_a", [P, 2, 512])
        weights_in, consts_ready = z.sem("weights_in"), z.sem("consts_ready")
        x_in, agg_in = z.sems("x_in", AHEAD), z.sems("agg_in", AHEAD)
        x1_out, row1_out = z.sems("x1_out", AHEAD), z.sems("row1_out", AHEAD)
        (residual_ready, moments1, moments2, std1, std2, normed, stats1, stats2, inverse1, inverse2, centered) = (z.sem(n) for n in (
            "residual_ready", "moments1", "moments2", "std1", "std2", "normed", "stats1", "stats2", "inverse1", "inverse2", "centered"))
        (agg_turned, agg_t_ready, out_done, summed, x1_ready, x1_turned, x1_t_ready,
         projected, row1_ready, spread_ready, a_done, a_copied, setup, settled) = (z.sem(n) for n in (
            "agg_turned", "agg_t_ready", "out_done", "summed", "x1_ready", "x1_turned",
            "x1_t_ready", "projected", "row1_ready", "spread_ready", "a_done", "a_copied", "setup", "settled"))
        block = z.block()
        WEIGHTS = 7

        @block.sync
        def _(sp):
            sp.dma_start(wo[:], k.i["L0_gnn_Wo"].rearrange("(a p) n -> p a n", p=P)).then_inc(weights_in, 16)
            sp.dma_start(w1[:, :, 0:D], k.i["L1_gnn_W"].rearrange("(a p) n -> p a n", p=P)).then_inc(weights_in, 16)
            for to, name in ((bo, "L0_gnn_bo"), (gamma, "L0_gnn_gamma"), (beta, "L0_gnn_beta")):
                sp.dma_start(to[:], row(k, name)).then_inc(weights_in, 16)
            for a, name in enumerate(("L1_gnn_att_src", "L1_gnn_att_dst")):
                sp.dma_start(att[:, a], k.i[name].rearrange("(o h) c -> o (h c)", o=1).broadcast_to((P, D))).then_inc(weights_in, 16)

            def store(t):
                b = t.slot(AHEAD)
                sp.wait_ge(x1_ready, t.n + 1)
                sp.dma_start(k.x1[bass.ds(t.n * P, P), :], x1[:, b]).then_inc(x1_out[b], 16)
                sp.wait_ge(row1_ready, t.n + 1)
                sp.dma_start(k.xp[bass.ds(t.n * P, P), :], row1[:, b]).then_inc(row1_out[b], 16)
                sp.dma_start(k.agg[bass.ds(t.n * P, P), :], row1[:, b, 0:D]).then_inc(row1_out[b], 16)

            def load(t):
                b = t.slot(AHEAD)
                if not t.known_below(AHEAD):
                    sp.wait_ge(residual_ready, t.n - AHEAD + 1)
                    sp.wait_ge(agg_turned, t.n - AHEAD + 1)
                sp.dma_start(x[:, b], k.i["x"][bass.ds(t.n * P, P), :]).then_inc(x_in[b], 16)
                sp.dma_start(agg[:, b], k.agg[bass.ds(t.n * P, P), :]).then_inc(agg_in[b], 16)

            in_turn(sp, (0, load), (6, store))
            for b in range(AHEAD):
                sp.wait_ge(x1_out[b], 16 * blocks_of(b))
                sp.wait_ge(row1_out[b], 32 * blocks_of(b))

        @block.tensor
        def _(pe):
            def turn_agg(t):
                b = t.slot(2)
                pe.wait_ge(agg_in[t.slot(AHEAD)], 16 * (t.use(AHEAD) + 1))
                if not t.known_below(2):
                    pe.wait_ge(agg_t_ready, t.n - 1)
                for a in range(2):
                    last = pe.transpose(p_t[:, b, a * P:a * P + P], agg[:, t.slot(AHEAD), a * P:a * P + P], ident)
                last.then_inc(agg_turned, 1)

            def output(t):
                pe.wait_ge(agg_t_ready, t.n + 1)
                if not t.known_below(1):
                    pe.wait_ge(summed, t.n)
                for a in range(2):
                    last = pe.matmul(p_o[:, 0:D], agg_t[:, t.slot(2), a * P:a * P + P], wo[:, a], start=a == 0, stop=a == 1)
                last.then_inc(out_done, 1)

            def turn_x1(t):
                pe.wait_ge(x1_ready, t.n + 1)
                if not t.known_below(1):
                    pe.wait_ge(x1_t_ready, t.n)
                for a in range(2):
                    last = pe.transpose(p_t1[:, a * P:a * P + P], x1[:, t.slot(AHEAD), a * P:a * P + P], ident)
                last.then_inc(x1_turned, 1)

            def project(t):
                pe.wait_ge(x1_t_ready, t.n + 1)
                if not t.known_below(1):
                    pe.wait_ge(row1_ready, t.n)
                for a in range(2):
                    last = pe.matmul(p_1[:, 0:C1], x1_t[:, t.slot(2), a * P:a * P + P], w1[:, a], start=a == 0, stop=a == 1)
                last.then_inc(projected, 1)

            def turn_a(t):
                b = t.slot(2)
                pe.wait_ge(spread_ready, t.n + 1)
                if not t.known_below(2):
                    pe.wait_ge(a_copied, t.n - 1)
                for a in range(2):
                    last = pe.matmul(p_a[:, b, a * TPB:a * TPB + TPB], spread[:, b, a * HEADS:a * HEADS + HEADS].rearrange("p h d -> p (h d)"),
                                     cst[:, C_TAU:C_TAU + TPB], start=True, stop=True)
                last.then_inc(a_done, 1)

            pe.wait_ge(weights_in, 16 * WEIGHTS)
            pe.wait_ge(consts_ready, 1)
            in_turn(pe, (0, turn_agg), (5, project), (0, output), (4, turn_x1), (7, turn_a))

        @block.gpsimd
        def _(pool):
            def residual(t):
                b, o = t.slot(2), t.slot(AHEAD)
                pool.wait_ge(x_in[t.slot(AHEAD)], 16 * (t.use(AHEAD) + 1))
                if not t.known_below(2):
                    pool.wait_ge(summed, t.n - 1)
                if not t.known_below(AHEAD):
                    pool.wait_ge(normed, t.n - AHEAD + 1)
                pool.tensor_tensor(x_bo[:, b], x[:, t.slot(AHEAD)], bo[:], ALU.add)
                pool.tensor_tensor(x_beta[:, o], x[:, t.slot(AHEAD)], beta[:], ALU.add).then_inc(residual_ready, 1)

            def spread_a(t):
                b = t.slot(2)
                pool.wait_ge(row1_ready, t.n + 1)
                if not t.known_below(2):
                    pool.wait_ge(a_done, t.n - 1)
                pool.tensor_tensor(spread[:, b], both_a[:, b].unsqueeze(2).broadcast_to((P, 2 * HEADS, TN)),
                                   cst[:, C_DIAG:C_DIAG + TN].unsqueeze(1).broadcast_to((P, 2 * HEADS, TN)),
                                   ALU.mult).then_inc(spread_ready, 1)

            pool.wait_ge(weights_in, 16 * WEIGHTS)
            in_turn(pool, (0, residual), (6, spread_a))

        @block.vector
        def _(v):
            def sum_up(t):
                b, o = t.slot(2), t.slot(AHEAD)
                if not t.known_below(AHEAD):
                    v.wait_ge(x1_ready, t.n - AHEAD + 1)
                v.wait_ge(residual_ready, t.n + 1)
                v.wait_ge(out_done, t.n + 1)
                v.tensor_tensor(y[:, o], p_o[:, 0:D], x_bo[:, b], ALU.add).then_inc(summed, 1)

            def statistics(t, norm, y_ready, moments_ready, stats_ready):
                v.wait_ge(y_ready, t.n + 1)
                if not t.known_below(1):
                    v.wait_ge(moments_ready, t.n)
                v.bn_stats(stats[:, norm], y[:, t.slot(AHEAD)]).then_inc(stats_ready, 1)

            def moment(t, norm, stats_ready, moments_ready):
                v.wait_ge(stats_ready, t.n + 1)
                v.sem_inc(settled, 1)
                v.bn_aggr(moments[:, t.slot(AHEAD), norm], stats[:, norm]).then_inc(moments_ready, 1)

            def invert(t, norm, std_ready, inverse_ready):
                o = t.slot(AHEAD)
                v.wait_ge(std_ready, t.n + 1)
                v.reciprocal(rstd[:, o, norm:norm + 1], std[:, o, norm:norm + 1]).then_inc(inverse_ready, 1)

            def statistics1(t):
                statistics(t, 0, summed, moments1, stats1)

            def moment1(t):
                moment(t, 0, stats1, moments1)

            def invert1(t):
                invert(t, 0, std1, inverse1)

            def center(t):
                o = t.slot(AHEAD)
                v.wait_ge(std1, t.n + 1)
                v.scalar_tensor_tensor(y[:, o], y[:, o], moments[:, o, 0, 0:1], gamma[:], ALU.subtract, ALU.mult).then_inc(centered, 1)

            def normalize(t):
                o = t.slot(AHEAD)
                v.wait_ge(inverse1, t.n + 1)
                v.wait_ge(centered, t.n + 1)
                v.scalar_tensor_tensor(y[:, o], y[:, o], rstd[:, o, 0:1], x_beta[:, o], ALU.mult, ALU.add).then_inc(normed, 1)

            def statistics2(t):
                statistics(t, 1, normed, moments2, stats2)

            def moment2(t):
                moment(t, 1, stats2, moments2)

            def invert2(t):
                invert(t, 1, std2, inverse2)

            def end_norm(t):
                o = t.slot(AHEAD)
                v.wait_ge(inverse2, t.n + 1)
                if not t.known_below(AHEAD):
                    v.wait_ge(x1_turned, t.n - AHEAD + 1)
                    v.wait_ge(x1_out[o], 16 * t.use(AHEAD))
                v.tensor_scalar(x1[:, o], y[:, o], moments[:, o, 1, 0:1], rstd[:, o, 1:2], ALU.subtract, ALU.mult).then_inc(x1_ready, 1)

            def copy_a(t):
                v.wait_ge(a_done, t.n + 1)
                v.tensor_copy(k.logit[:, bass.ds(t.n * TPB, TPB)], p_a[:, t.slot(2), 0:TPB])
                v.tensor_copy(k.adst[:, bass.ds(t.n * TPB, TPB)], p_a[:, t.slot(2), TPB:2 * TPB]).then_inc(a_copied, 1)

            v.memset(eps[:], 1e-5).then_inc(setup, 1)
            v.wait_ge(weights_in, 16 * WEIGHTS)
            for side in range(2):
                for a in range(2):
                    v.tensor_tensor(prod[:, side, a], w1[:, a, 0:D], att[:, side], ALU.mult).then_inc(setup, 1)
            v.wait_ge(setup, 5)
            for side in range(2):
                at = D + side * HEADS
                v.tensor_reduce(w1[:, :, at:at + HEADS], prod[:, side].rearrange("p a (h c) -> p a h c", h=HEADS), AX, ALU.add).then_inc(setup, 1)
            v.wait_ge(setup, 7)
            v.sem_inc(consts_ready, 1)
            in_turn(v, (1, sum_up), (2, invert1), (2, center), (1, statistics1), (3, invert2), (2, normalize), (1, moment1),
                    (3, end_norm), (2, statistics2), (8, copy_a), (2, moment2))
            v.wait_ge(a_copied, ROWS)
            v.tensor_tensor(sum_a[:], k.logit[:], k.adst[:], ALU.add).then_inc(setup, 1)
            v.wait_ge(setup, 8)
            v.tensor_scalar(leak[:], sum_a[:], 0.2, None, ALU.mult).then_inc(setup, 1)
            v.wait_ge(setup, 9)
            v.tensor_tensor(k.logit[:], leak[:], sum_a[:], ALU.max).then_inc(setup, 1)

        @block.scalar
        def _(act):
            def copy_agg(t):
                b = t.slot(2)
                act.wait_ge(agg_turned, t.n + 1)
                if not t.known_below(2):
                    act.wait_ge(out_done, t.n - 1)
                act.copy(agg_t[:, b], p_t[:, b, 0:D]).then_inc(agg_t_ready, 1)

            def copy_x1(t):
                act.wait_ge(x1_turned, t.n + 1)
                if not t.known_below(2):
                    act.wait_ge(projected, t.n - 1)
                act.copy(x1_t[:, t.slot(2)], p_t1[:, 0:D]).then_inc(x1_t_ready, 1)

            def copy_row(t):
                b, o = t.slot(2), t.slot(AHEAD)
                act.wait_ge(projected, t.n + 1)
                if not t.known_below(2):
                    act.wait_ge(spread_ready, t.n - 1)
                if not t.known_below(AHEAD):
                    act.wait_ge(row1_out[o], 32 * t.use(AHEAD))
                act.copy(both_a[:, b], p_1[:, D:C1])
                act.copy(row1[:, o, D:V1].rearrange("p (h d) -> p h d", h=HEADS),
                         p_1[:, D:D + HEADS].unsqueeze(2).broadcast_to((P, HEADS, TN)))
                act.copy(row1[:, o, 0:D], p_1[:, 0:D]).then_inc(row1_ready, 1)

            def root(t, norm, moments_ready, std_ready):
                o = t.slot(AHEAD)
                act.wait_ge(moments_ready, t.n + 1)
                act.activation(std[:, o, norm:norm + 1], moments[:, o, norm, 1:2], ACT.Sqrt, bias=eps[:, 0:1]).then_inc(std_ready, 1)

            def root1(t):
                root(t, 0, moments1, std1)

            def root2(t):
                root(t, 1, moments2, std2)

            act.wait_ge(consts_ready, 1)
            in_turn(act, (0, copy_agg), (5, copy_row), (1, root1), (2, root2), (4, copy_x1))


def finish(k):
    nc = k.nc
    with Stage(nc, "fin") as z:
        bias = z.sb("bias", [P, D])
        one = z.sb("one", [P, 1])
        eps = z.sb("eps", [P, 1])
        power = z.sb("power", [P, 1])
        var = z.sb("var", [P, 2])
        agg = z.sb("agg", [P, AHEAD, D])
        x1 = z.sb("x1", [P, AHEAD, D])
        h = z.sb("h", [P, 2, D])
        grown = z.sb("grown", [P, 2, D])
        kept = z.sb("kept", [P, 2, D])
        y = z.sb("y", [P, 2, D])
        stats = z.sb("stats", [P, 2, 6])
        moments = z.sb("moments", [P, 2, 2])
        rstd = z.sb("rstd", [P, 2])
        res = z.sb("res", [P, AHEAD, D])
        bias_in, setup = z.sem("bias_in"), z.sem("setup")
        in_, out_ = z.sems("in", AHEAD), z.sems("out", AHEAD)
        h_ready, grown_ready, kept_ready, y_ready, stats_ready, moments_ready, rstd_ready, res_ready, settled, settled2, var_ready = (
            z.sem(n) for n in ("h_ready", "grown_ready", "kept_ready", "y_ready", "stats_ready", "moments_ready",
                               "rstd_ready", "res_ready", "settled", "settled2", "var_ready"))
        block = z.block()

        @block.sync
        def _(sp):
            sp.dma_start(bias[:], row(k, "L1_gnn_bias")).then_inc(bias_in, 16)

            def store(t):
                b = t.slot(AHEAD)
                sp.wait_ge(res_ready, t.n + 1)
                sp.dma_start(k.out[bass.ds(t.n * P, P), :], res[:, b]).then_inc(out_[b], 16)

            def step(t):
                b = t.slot(AHEAD)
                if not t.known_below(AHEAD):
                    sp.wait_ge(kept_ready, t.n - AHEAD + 1)
                sp.dma_start(x1[:, b], k.x1[bass.ds(t.n * P, P), :]).then_inc(in_[b], 16)
                sp.dma_start(agg[:, b], k.agg[bass.ds(t.n * P, P), :]).then_inc(in_[b], 16)
                if not t.known_below(AHEAD):
                    store(t.back(AHEAD))

            end = steps(sp, ROWS, BLOCKS, step)
            for back in range(AHEAD, 0, -1):
                store(end.back(back))
            for b in range(AHEAD):
                sp.wait_ge(out_[b], 16 * blocks_of(b))

        @block.vector
        def _(v):
            def biased(t):
                b = t.slot(2)
                v.wait_ge(in_[t.slot(AHEAD)], 32 * (t.use(AHEAD) + 1))
                if not t.known_below(2):
                    v.wait_ge(grown_ready, t.n - 1)
                    v.wait_ge(kept_ready, t.n - 1)
                v.tensor_tensor(h[:, b], agg[:, t.slot(AHEAD)], bias[:], ALU.add).then_inc(h_ready, 1)

            def keep(t):
                b = t.slot(2)
                v.wait_ge(h_ready, t.n + 1)
                if not t.known_below(2):
                    v.wait_ge(y_ready, t.n - 1)
                v.scalar_tensor_tensor(kept[:, b], h[:, b], -1.0, x1[:, t.slot(AHEAD)], ALU.max, ALU.add).then_inc(kept_ready, 1)

            def join(t):
                b = t.slot(2)
                v.wait_ge(kept_ready, t.n + 1)
                v.wait_ge(grown_ready, t.n + 1)
                if not t.known_below(2):
                    v.wait_ge(res_ready, t.n - 1)
                v.scalar_tensor_tensor(y[:, b], grown[:, b], 1.0, kept[:, b], ALU.min, ALU.add).then_inc(y_ready, 1)

            def measure(t):
                b = t.slot(2)
                v.wait_ge(y_ready, t.n + 1)
                if not t.known_below(2):
                    v.wait_ge(moments_ready, t.n - 1)
                v.bn_stats(stats[:, b], y[:, b]).then_inc(stats_ready, 1)

            def moment(t):
                b = t.slot(2)
                v.wait_ge(stats_ready, t.n + 1)
                if not t.known_below(2):
                    v.wait_ge(res_ready, t.n - 1)
                v.sem_inc(settled, 1)
                v.bn_aggr(moments[:, b], stats[:, b]).then_inc(moments_ready, 1)

            def end_norm(t):
                b, o = t.slot(2), t.slot(AHEAD)
                v.wait_ge(rstd_ready, t.n + 1)
                if not t.known_below(AHEAD):
                    v.wait_ge(out_[o], 16 * t.use(AHEAD))
                v.tensor_scalar(res[:, o], y[:, b], moments[:, b, 0:1], rstd[:, b:b + 1], ALU.subtract, ALU.mult).then_inc(res_ready, 1)

            def step(t):
                biased(t)
                if not t.known_below(1):
                    join(t.back())
                keep(t)
                if not t.known_below(1):
                    measure(t.back())
                if not t.known_below(2):
                    end_norm(t.back(2))
                if not t.known_below(1):
                    moment(t.back())

            for to, value in ((one, 1.0), (eps, 1e-5), (power, -0.5)):
                v.memset(to[:], value).then_inc(setup, 1)
            v.wait_ge(bias_in, 16)
            v.tensor_scalar(bias[:], bias[:], -1.0, None, ALU.add).then_inc(setup, 1)
            v.wait_ge(setup, 4)
            end = steps(v, ROWS, BLOCKS, step)
            join(end.back())
            measure(end.back())
            end_norm(end.back(2))
            moment(end.back())
            end_norm(end.back())

        @block.gpsimd
        def _(pool):
            def root(t):
                b = t.slot(2)
                pool.wait_ge(moments_ready, t.n + 1)
                if not t.known_below(2):
                    pool.wait_ge(res_ready, t.n - 1)
                pool.sem_inc(settled2, 1)
                pool.tensor_tensor(var[:, b:b + 1], moments[:, b, 1:2], eps[:, 0:1], ALU.add).then_inc(var_ready, 1)
                pool.wait_ge(var_ready, t.n + 1)
                pool.sem_inc(settled2, 1)
                pool.tensor_tensor(rstd[:, b:b + 1], var[:, b:b + 1], power[:, 0:1], ALU.pow).then_inc(rstd_ready, 1)

            pool.wait_ge(setup, 4)
            steps(pool, ROWS, BLOCKS, root)

        @block.scalar
        def _(act):
            def step(t):
                b = t.slot(2)
                act.wait_ge(h_ready, t.n + 1)
                if not t.known_below(2):
                    act.wait_ge(y_ready, t.n - 1)
                act.activation(grown[:, b], h[:, b], ACT.Exp, bias=one[:, 0:1]).then_inc(grown_ready, 1)

            act.wait_ge(setup, 4)
            steps(act, ROWS, BLOCKS, step)


def kernel(**inputs):
    import numpy as _np
    import concourse.bacc as _bacc
    from concourse import mybir as _mybir
    from concourse.bass_utils import run_bass_kernel_spmd as _run

    nc = _bacc.Bacc("TRN2", target_bir_lowering=False, num_devices=1)
    given = {name: _np.ascontiguousarray(a) for name, a in inputs.items()}
    x = given.pop("x")
    src, dst, rel = (given.pop(name) for name in ("src", "dst", "edge_type_64"))
    given["x"] = _np.concatenate([x, _np.zeros((NP - N, D), x.dtype)])
    pad = lambda a, value: _np.concatenate([a, _np.full((EP - E,), value, a.dtype)])
    given["edges"] = _np.stack([pad(src, 0), pad(dst, PAD_DST), pad(rel, 0)])
    given["edge_rows"] = _np.ascontiguousarray(given["edges"].T)
    given["consts"] = constants()
    aps = {name: nc.dram_tensor(f"in_{name}", a.shape, _mybir.dt.from_np(a.dtype), kind="ExternalInput").ap()
           for name, a in given.items()}
    out = nc.dram_tensor("out_dram", (NP, D), _mybir.dt.float32, kind="ExternalOutput").ap()
    gat_kernel(nc, aps, out)
    r = _run(nc, [{f"in_{name}": a for name, a in given.items()}], core_ids=[0])
    return r.results[0]["out_dram"][0:N]
```
